# Optimizing a Trainium2 kernel written in Bass

```python
import numpy as np
import jax
import jax.numpy as jnp

def _softmax(x, axis=-1):
    return jax.nn.softmax(x, axis=axis)

def _gelu(x):
    return jax.nn.gelu(x, approximate=True)

def _silu(x):
    return jax.nn.silu(x)

def _sigmoid(x):
    return jax.nn.sigmoid(x)

def _layernorm(x, axis=-1, eps=1e-05):
    m = jnp.mean(x, axis=axis, keepdims=True)
    v = jnp.var(x, axis=axis, keepdims=True)
    return (x - m) / jnp.sqrt(v + eps)

def _scatter_add(tgt, idx, src, axis=0):
    return tgt.at[idx].add(src)

def _segment_sum(src, seg, n):
    return jax.ops.segment_sum(src, seg, n)
kernel_name = 'mk_flamingo_gated_d2_seqx_r4_7f6869'

def setup_inputs(seed: int=0):
    np.random.seed(seed)
    _w = jnp.asarray

    def _rec_inputs():
        import jax
        import jax.numpy as jnp
        _rk = jax.random.key(seed)
        x = 4.136e-05 + 0.9999 * jax.random.normal(jax.random.fold_in(_rk, 1), (4, 512, 512), jnp.float32)
        _lenS = 512 - jax.random.randint(jax.random.fold_in(_rk, 7), (4,), 0, max(1, 512 // 4) + 1, jnp.int32)
        _lenS2 = 512 - jax.random.randint(jax.random.fold_in(_rk, 8), (4,), 0, max(1, 512 // 4) + 1, jnp.int32)
        _ctx_1024P = jax.random.normal(jax.random.fold_in(_rk, 11), (4, 16, 256), jnp.float32)
        _ctx_1024c = jax.random.dirichlet(jax.random.fold_in(_rk, 511), 0.3 * jnp.ones((16,), jnp.float32), (4, 512))
        _ctx_1024t = jnp.einsum('bsk,bkd->bsd', _ctx_1024c, _ctx_1024P)
        _ctx_1024t = _ctx_1024t * jax.lax.rsqrt(jnp.mean(jnp.square(_ctx_1024t)) + 1e-12) * 0.953939
        ctx_1024 = -0.000292821 + 1.00034 * (_ctx_1024t + 0.3 * jax.random.normal(jax.random.fold_in(_rk, 611), (4, 512, 256), jnp.float32))
        _g = jax.random.normal(jax.random.fold_in(_rk, 9001), (2, 2), jnp.float32)
        _g = jnp.sign(_g) * jnp.maximum(jnp.abs(_g), 1.0) + (_g == 0) * 1.0
        g_xattn = _g[0]
        g_ffn = _g[1]
        return (x, ctx_1024, g_xattn, g_ffn)
    x, ctx_1024, g_xattn, g_ffn = _rec_inputs()

    def _L0_xattn_setup():
        import jax, jax.numpy as jnp
        import numpy as np
        import math
        B, L, DM = (2, 512, 256)
        DS, DC, EXP = (16, 4, 2)
        DI = EXP * DM
        DR = math.ceil(DM / 16)
        DT_MIN, DT_MAX, DT_FLOOR = (0.001, 0.1, 0.0001)

        def _ssm_forward(hidden_states, z, in_proj_w, conv_w, conv_b, x_proj_w, dt_proj_w, dt_proj_b, A_log, D):
            b = hidden_states.shape[0]
            x = jnp.einsum('ed,bld->bel', in_proj_w, hidden_states)
            xp = jnp.pad(x, ((0, 0), (0, 0), (DC - 1, 0)))
            xc = jax.lax.conv_general_dilated(xp, conv_w[:, None, :], window_strides=(1,), padding='VALID', dimension_numbers=('NCH', 'OIH', 'NCH'), feature_group_count=DI)
            u = jax.nn.silu(xc + conv_b[None, :, None])
            x_dbl = jnp.einsum('ke,bel->bkl', x_proj_w, u)
            dt_lo = x_dbl[:, :DR]
            Bm = x_dbl[:, DR:DR + DS]
            Cm = x_dbl[:, DR + DS:]
            delta = jax.nn.softplus(jnp.einsum('er,brl->bel', dt_proj_w, dt_lo) + dt_proj_b[None, :, None])
            A = -jnp.exp(A_log)

            def step(state, xs):
                d_t, B_t, C_t, u_t = xs
                dA = jnp.exp(d_t[..., None] * A)
                state = state * dA + (d_t * u_t)[..., None] * B_t[:, None, :]
                y_t = jnp.einsum('ben,bn->be', state, C_t)
                return (state, y_t)
            xs = (jnp.moveaxis(delta, -1, 0), jnp.moveaxis(Bm, -1, 0), jnp.moveaxis(Cm, -1, 0), jnp.moveaxis(u, -1, 0))
            state0 = jnp.zeros((b, DI, DS), delta.dtype)
            _, ys = jax.lax.scan(step, state0, xs)
            y = jnp.moveaxis(ys, 0, -1)
            y = y + D[None, :, None] * u
            y = y * jax.nn.silu(z)
            return jnp.swapaxes(y, 1, 2)
        key = jax.random.key(seed)
        ks = jax.random.split(key, 8)
        hidden_states = jax.random.normal(ks[0], (B, L, DM), jnp.float32)
        z = jax.random.normal(ks[1], (B, DI, L), jnp.float32)
        in_proj_w = jax.random.normal(ks[2], (DI, DM), jnp.float32) * DM ** (-0.5)
        conv_w = jax.random.normal(ks[3], (DI, DC), jnp.float32) * DC ** (-0.5)
        conv_b = jnp.zeros((DI,), jnp.float32)
        x_proj_w = jax.random.normal(ks[4], (DR + 2 * DS, DI), jnp.float32) * DI ** (-0.5)
        dt_std = DR ** (-0.5)
        dt_proj_w = jax.random.uniform(ks[5], (DI, DR), jnp.float32, -dt_std, dt_std)
        dt = jnp.exp(jax.random.uniform(ks[6], (DI,), jnp.float32) * (math.log(DT_MAX) - math.log(DT_MIN)) + math.log(DT_MIN))
        dt = jnp.clip(dt, DT_FLOOR)
        dt_proj_b = dt + jnp.log(-jnp.expm1(-dt))
        A_log = jnp.log(jnp.broadcast_to(jnp.arange(1, DS + 1, dtype=jnp.float32), (DI, DS)))
        D = jnp.ones((DI,), jnp.float32)
        return dict(hidden_states=hidden_states, z=z, in_proj_w=in_proj_w, conv_w=conv_w, conv_b=conv_b, x_proj_w=x_proj_w, dt_proj_w=dt_proj_w, dt_proj_b=dt_proj_b, A_log=A_log, D=D)
    _L0_xattn_all = _L0_xattn_setup()
    _L0_xattn_in = {k: v for k, v in _L0_xattn_all.items() if k in ('in_proj_w', 'conv_w', 'conv_b', 'x_proj_w', 'dt_proj_w', 'dt_proj_b', 'A_log', 'D')}
    del _L0_xattn_all

    def _L0_ffn_setup():
        import jax, jax.numpy as jnp
        import numpy as np

        def ternary_quantize(t, threshold, scale):
            return jnp.where(t > threshold, scale, jnp.where(t < -threshold, -scale, 0.0)).astype(t.dtype)
        key = jax.random.key(seed)
        k1, k2, k3 = jax.random.split(key, 3)
        B, S, D = (4, 1024, 512)
        x = jax.random.normal(k1, (B, S, D), dtype=jnp.float32)
        weight = jax.random.normal(k2, (D, D), dtype=jnp.float32) * 0.02
        rram_variation = jax.random.normal(k3, (D, D), dtype=jnp.float32) * 0.05
        return {'x': x, 'weight': weight, 'rram_variation': rram_variation}
    _L0_ffn_all = _L0_ffn_setup()
    _L0_ffn_in = {k: v for k, v in _L0_ffn_all.items() if k in ('weight', 'rram_variation')}
    del _L0_ffn_all

    def _L1_xattn_setup():
        import jax, jax.numpy as jnp
        import numpy as np
        B, S1, S2, DCA = (2, 512, 256, 16)
        QDIM, KDIM, H = (512, 256, 16)
        HD = QDIM // H
        SCALE = HD ** (-0.5)
        EPS = 1e-06
        DCA_WEIGHT = 1.0

        def _ln(t, w, b):
            m = jnp.mean(t, axis=-1, keepdims=True)
            v = jnp.var(t, axis=-1, keepdims=True)
            return (t - m) * jax.lax.rsqrt(v + EPS) * w + b

        def _attn(q, k, v):
            s = jnp.einsum('bhqd,bhkd->bhqk', q, k) * SCALE
            p = jax.nn.softmax(s, axis=-1)
            return jnp.einsum('bhqk,bhkd->bhqd', p, v)
        key = jax.random.key(seed)
        ks = jax.random.split(key, 8)
        w = lambda k, shape: jax.random.normal(k, shape, jnp.float32) * 0.02
        return {'x': jax.random.normal(ks[0], (B, S1, QDIM), jnp.float32), 'y': jax.random.normal(ks[1], (B, S2 + DCA, KDIM), jnp.float32), 'Wq': w(ks[2], (QDIM, QDIM)), 'bq': jnp.zeros((QDIM,), jnp.float32), 'Wk': w(ks[3], (KDIM, QDIM)), 'bk': jnp.zeros((QDIM,), jnp.float32), 'Wv': w(ks[4], (KDIM, QDIM)), 'bv': jnp.zeros((QDIM,), jnp.float32), 'Wkv_dca': w(ks[5], (KDIM, 2 * QDIM)), 'bkv_dca': jnp.zeros((2 * QDIM,), jnp.float32), 'qn_w': jnp.ones((HD,), jnp.float32), 'qn_b': jnp.zeros((HD,), jnp.float32), 'kn_w': jnp.ones((HD,), jnp.float32), 'kn_b': jnp.zeros((HD,), jnp.float32), 'kn_dca_w': jnp.ones((HD,), jnp.float32), 'kn_dca_b': jnp.zeros((HD,), jnp.float32), 'Wo': w(ks[6], (QDIM, QDIM)), 'bo': jnp.zeros((QDIM,), jnp.float32)}
    _L1_xattn_all = _L1_xattn_setup()
    _L1_xattn_in = {k: v for k, v in _L1_xattn_all.items() if k in ('Wq', 'bq', 'Wk', 'bk', 'Wv', 'bv', 'Wkv_dca', 'bkv_dca', 'qn_w', 'qn_b', 'kn_w', 'kn_b', 'kn_dca_w', 'kn_dca_b', 'Wo', 'bo')}
    del _L1_xattn_all

    def _L1_ffn_setup():
        import jax, jax.numpy as jnp
        import numpy as np
        HID = 512
        N_EXP = 32
        F_EXP = 192
        TOP_K = 6
        F_SH = 384
        B, S = (1, 256)
        key = jax.random.key(seed)
        ks = jax.random.split(key, 8)
        s = 0.02
        return {'hidden_states': jax.random.normal(ks[0], (B, S, HID), dtype=jnp.float32), 'gate_w': jax.random.normal(ks[1], (HID, N_EXP), dtype=jnp.float32) * s, 'wg': jax.random.normal(ks[2], (N_EXP, HID, F_EXP), dtype=jnp.float32) * s, 'wu': jax.random.normal(ks[3], (N_EXP, HID, F_EXP), dtype=jnp.float32) * s, 'wd': jax.random.normal(ks[4], (N_EXP, F_EXP, HID), dtype=jnp.float32) * s, 'sg': jax.random.normal(ks[5], (HID, F_SH), dtype=jnp.float32) * s, 'su': jax.random.normal(ks[6], (HID, F_SH), dtype=jnp.float32) * s, 'sd': jax.random.normal(ks[7], (F_SH, HID), dtype=jnp.float32) * s}
    _L1_ffn_all = _L1_ffn_setup()
    _L1_ffn_in = {k: v for k, v in _L1_ffn_all.items() if k in ('gate_w', 'wg', 'wu', 'wd', 'sg', 'su', 'sd')}
    del _L1_ffn_all
    return {'x': x, 'ctx_1024': ctx_1024, 'g_xattn': g_xattn, 'g_ffn': g_ffn, 'L0_xattn_in_proj_w': _L0_xattn_in['in_proj_w'], 'L0_xattn_conv_w': _L0_xattn_in['conv_w'], 'L0_xattn_conv_b': _L0_xattn_in['conv_b'], 'L0_xattn_x_proj_w': _L0_xattn_in['x_proj_w'], 'L0_xattn_dt_proj_w': _L0_xattn_in['dt_proj_w'], 'L0_xattn_dt_proj_b': _L0_xattn_in['dt_proj_b'], 'L0_xattn_A_log': _L0_xattn_in['A_log'], 'L0_xattn_D': _L0_xattn_in['D'], 'L0_ffn_weight': _L0_ffn_in['weight'], 'L0_ffn_rram_variation': _L0_ffn_in['rram_variation'], 'L1_xattn_Wq': _L1_xattn_in['Wq'], 'L1_xattn_bq': _L1_xattn_in['bq'], 'L1_xattn_Wk': _L1_xattn_in['Wk'], 'L1_xattn_bk': _L1_xattn_in['bk'], 'L1_xattn_Wv': _L1_xattn_in['Wv'], 'L1_xattn_bv': _L1_xattn_in['bv'], 'L1_xattn_Wkv_dca': _L1_xattn_in['Wkv_dca'], 'L1_xattn_bkv_dca': _L1_xattn_in['bkv_dca'], 'L1_xattn_qn_w': _L1_xattn_in['qn_w'], 'L1_xattn_qn_b': _L1_xattn_in['qn_b'], 'L1_xattn_kn_w': _L1_xattn_in['kn_w'], 'L1_xattn_kn_b': _L1_xattn_in['kn_b'], 'L1_xattn_kn_dca_w': _L1_xattn_in['kn_dca_w'], 'L1_xattn_kn_dca_b': _L1_xattn_in['kn_dca_b'], 'L1_xattn_Wo': _L1_xattn_in['Wo'], 'L1_xattn_bo': _L1_xattn_in['bo'], 'L1_ffn_gate_w': _L1_ffn_in['gate_w'], 'L1_ffn_wg': _L1_ffn_in['wg'], 'L1_ffn_wu': _L1_ffn_in['wu'], 'L1_ffn_wd': _L1_ffn_in['wd'], 'L1_ffn_sg': _L1_ffn_in['sg'], 'L1_ffn_su': _L1_ffn_in['su'], 'L1_ffn_sd': _L1_ffn_in['sd']}

def reference(x, ctx_1024, g_xattn, g_ffn, L0_xattn_in_proj_w, L0_xattn_conv_w, L0_xattn_conv_b, L0_xattn_x_proj_w, L0_xattn_dt_proj_w, L0_xattn_dt_proj_b, L0_xattn_A_log, L0_xattn_D, L0_ffn_weight, L0_ffn_rram_variation, L1_xattn_Wq, L1_xattn_bq, L1_xattn_Wk, L1_xattn_bk, L1_xattn_Wv, L1_xattn_bv, L1_xattn_Wkv_dca, L1_xattn_bkv_dca, L1_xattn_qn_w, L1_xattn_qn_b, L1_xattn_kn_w, L1_xattn_kn_b, L1_xattn_kn_dca_w, L1_xattn_kn_dca_b, L1_xattn_Wo, L1_xattn_bo, L1_ffn_gate_w, L1_ffn_wg, L1_ffn_wu, L1_ffn_wd, L1_ffn_sg, L1_ffn_su, L1_ffn_sd):
    import jax
    import jax.numpy as jnp

    def _L0_xattn_ref(hidden_states, z, in_proj_w, conv_w, conv_b, x_proj_w, dt_proj_w, dt_proj_b, A_log, D):
        import jax, jax.numpy as jnp
        import numpy as np
        import math
        B, L, DM = (2, 512, 256)
        DS, DC, EXP = (16, 4, 2)
        DI = EXP * DM
        DR = math.ceil(DM / 16)
        DT_MIN, DT_MAX, DT_FLOOR = (0.001, 0.1, 0.0001)

        def _ssm_forward(hidden_states, z, in_proj_w, conv_w, conv_b, x_proj_w, dt_proj_w, dt_proj_b, A_log, D):
            b = hidden_states.shape[0]
            x = jnp.einsum('ed,bld->bel', in_proj_w, hidden_states)
            xp = jnp.pad(x, ((0, 0), (0, 0), (DC - 1, 0)))
            xc = jax.lax.conv_general_dilated(xp, conv_w[:, None, :], window_strides=(1,), padding='VALID', dimension_numbers=('NCH', 'OIH', 'NCH'), feature_group_count=DI)
            u = jax.nn.silu(xc + conv_b[None, :, None])
            x_dbl = jnp.einsum('ke,bel->bkl', x_proj_w, u)
            dt_lo = x_dbl[:, :DR]
            Bm = x_dbl[:, DR:DR + DS]
            Cm = x_dbl[:, DR + DS:]
            delta = jax.nn.softplus(jnp.einsum('er,brl->bel', dt_proj_w, dt_lo) + dt_proj_b[None, :, None])
            A = -jnp.exp(A_log)

            def step(state, xs):
                d_t, B_t, C_t, u_t = xs
                dA = jnp.exp(d_t[..., None] * A)
                state = state * dA + (d_t * u_t)[..., None] * B_t[:, None, :]
                y_t = jnp.einsum('ben,bn->be', state, C_t)
                return (state, y_t)
            xs = (jnp.moveaxis(delta, -1, 0), jnp.moveaxis(Bm, -1, 0), jnp.moveaxis(Cm, -1, 0), jnp.moveaxis(u, -1, 0))
            state0 = jnp.zeros((b, DI, DS), delta.dtype)
            _, ys = jax.lax.scan(step, state0, xs)
            y = jnp.moveaxis(ys, 0, -1)
            y = y + D[None, :, None] * u
            y = y * jax.nn.silu(z)
            return jnp.swapaxes(y, 1, 2)
        return _ssm_forward(hidden_states, z, in_proj_w, conv_w, conv_b, x_proj_w, dt_proj_w, dt_proj_b, A_log, D)

    def _L0_ffn_ref(x, weight, rram_variation):
        import jax, jax.numpy as jnp
        import numpy as np

        def ternary_quantize(t, threshold, scale):
            return jnp.where(t > threshold, scale, jnp.where(t < -threshold, -scale, 0.0)).astype(t.dtype)
        TH_X, SC_X = (0.33, 0.5)
        TH_W, SC_W = (0.2, 0.6)
        x_q = ternary_quantize(x, TH_X, SC_X)
        w_q = ternary_quantize(weight, TH_W, SC_W)
        w_rram = w_q + rram_variation
        return jnp.einsum('bsd,od->bso', x_q, w_rram)

    def _L1_xattn_ref(x, y, Wq, bq, Wk, bk, Wv, bv, Wkv_dca, bkv_dca, qn_w, qn_b, kn_w, kn_b, kn_dca_w, kn_dca_b, Wo, bo):
        import jax, jax.numpy as jnp
        import numpy as np
        B, S1, S2, DCA = (2, 512, 256, 16)
        QDIM, KDIM, H = (512, 256, 16)
        HD = QDIM // H
        SCALE = HD ** (-0.5)
        EPS = 1e-06
        DCA_WEIGHT = 1.0

        def _ln(t, w, b):
            m = jnp.mean(t, axis=-1, keepdims=True)
            v = jnp.var(t, axis=-1, keepdims=True)
            return (t - m) * jax.lax.rsqrt(v + EPS) * w + b

        def _attn(q, k, v):
            s = jnp.einsum('bhqd,bhkd->bhqk', q, k) * SCALE
            p = jax.nn.softmax(s, axis=-1)
            return jnp.einsum('bhqk,bhkd->bhqd', p, v)
        b, s1, _ = x.shape
        y_dca = y[:, -DCA:, :]
        y_main = y[:, :-DCA, :]
        kv_dca = (y_dca @ Wkv_dca + bkv_dca).reshape(b, DCA, 2, H, HD)
        k_dca = _ln(kv_dca[:, :, 0], kn_dca_w, kn_dca_b)
        v_dca = kv_dca[:, :, 1]
        s2 = y_main.shape[1]
        q = _ln((x @ Wq + bq).reshape(b, s1, H, HD), qn_w, qn_b)
        kv = jnp.concatenate([y_main @ Wk + bk, y_main @ Wv + bv], axis=-1)
        kv = kv.reshape(b, s2, H, 2 * HD)
        k = _ln(kv[..., :HD], kn_w, kn_b)
        v = kv[..., HD:]
        qT = q.transpose(0, 2, 1, 3)
        ctx = _attn(qT, k.transpose(0, 2, 1, 3), v.transpose(0, 2, 1, 3))
        ctx = ctx.transpose(0, 2, 1, 3).reshape(b, s1, QDIM)
        ctx_dca = _attn(qT, k_dca.transpose(0, 2, 1, 3), v_dca.transpose(0, 2, 1, 3))
        ctx_dca = ctx_dca.transpose(0, 2, 1, 3).reshape(b, s1, QDIM)
        ctx = ctx + DCA_WEIGHT * ctx_dca
        return ctx @ Wo + bo

    def _L1_ffn_ref(hidden_states, gate_w, wg, wu, wd, sg, su, sd):
        import jax, jax.numpy as jnp
        import numpy as np
        HID = 512
        N_EXP = 32
        F_EXP = 192
        TOP_K = 6
        F_SH = 384
        B, S = (1, 256)
        orig_shape = hidden_states.shape
        x = hidden_states.reshape(-1, HID)
        scores = jax.nn.sigmoid(x @ gate_w)
        topk_w, topk_i = jax.lax.top_k(scores, TOP_K)
        topk_w = topk_w / (jnp.sum(topk_w, axis=-1, keepdims=True) + 1e-20)
        combine = jnp.sum(jax.nn.one_hot(topk_i, N_EXP, dtype=topk_w.dtype) * topk_w[..., None], axis=1)
        g = jnp.einsum('td,edf->tef', x, wg)
        u = jnp.einsum('td,edf->tef', x, wu)
        act = jax.nn.silu(g) * u
        routed = jnp.einsum('tef,efd,te->td', act, wd, combine)
        routed = routed.reshape(orig_shape)
        shared = jax.nn.silu(hidden_states @ sg) * (hidden_states @ su) @ sd
        return routed + shared
    x = x + jnp.tanh(g_xattn[0]) * _L0_xattn_ref(ctx_1024, _layernorm(x, axis=-1), L0_xattn_in_proj_w, L0_xattn_conv_w, L0_xattn_conv_b, L0_xattn_x_proj_w, L0_xattn_dt_proj_w, L0_xattn_dt_proj_b, L0_xattn_A_log, L0_xattn_D)
    x = x + jnp.tanh(g_ffn[0]) * _L0_ffn_ref(_layernorm(x, axis=-1), L0_ffn_weight, L0_ffn_rram_variation)
    x = x + jnp.tanh(g_xattn[1]) * _L1_xattn_ref(_layernorm(x, axis=-1), ctx_1024, L1_xattn_Wq, L1_xattn_bq, L1_xattn_Wk, L1_xattn_bk, L1_xattn_Wv, L1_xattn_bv, L1_xattn_Wkv_dca, L1_xattn_bkv_dca, L1_xattn_qn_w, L1_xattn_qn_b, L1_xattn_kn_w, L1_xattn_kn_b, L1_xattn_kn_dca_w, L1_xattn_kn_dca_b, L1_xattn_Wo, L1_xattn_bo)
    x = x + jnp.tanh(g_ffn[1]) * _L1_ffn_ref(_layernorm(x, axis=-1), L1_ffn_gate_w, L1_ffn_wg, L1_ffn_wu, L1_ffn_wd, L1_ffn_sg, L1_ffn_su, L1_ffn_sd)
    return x

_drawn_inputs = setup_inputs


def setup_inputs(seed=0):
    import zlib

    import numpy as np

    out = dict(_drawn_inputs(seed))
    spreads = {'g_ffn': (-1.0, 0.6),
     'L0_xattn_conv_b': (0.0, 0.1),
     'L0_xattn_D': (1.0, 0.2),
     'L1_xattn_bq': (0.0, 0.8),
     'L1_xattn_bk': (0.0, 0.312),
     'L1_xattn_bv': (0.0, 0.294),
     'L1_xattn_bkv_dca': (0.0, 0.1),
     'L1_xattn_qn_w': (1.0, 0.6),
     'L1_xattn_qn_b': (0.0, 0.8),
     'L1_xattn_kn_w': (1.0, 0.6),
     'L1_xattn_kn_b': (0.0, 2.0),
     'L1_xattn_kn_dca_w': (1.0, 0.6),
     'L1_xattn_kn_dca_b': (0.0, 2.0),
     'L1_xattn_bo': (0.0, 0.1)}
    factors = {'L0_xattn_dt_proj_w': 3.492,
     'L1_ffn_gate_w': 6.849,
     'L1_ffn_wg': 6.314,
     'L1_ffn_wu': 6.178,
     'L1_ffn_wd': 6.186,
     'L1_ffn_sg': 5.431,
     'L1_ffn_su': 5.345,
     'L1_ffn_sd': 5.342}
    for name, (base, spread) in spreads.items():
        noise = np.random.default_rng([zlib.crc32(name.encode()), seed]).standard_normal(out[name].shape)
        drawn = base * np.exp(spread * noise) if base else spread * noise
        out[name] = jnp.asarray(drawn.astype(out[name].dtype))
    for name, factor in factors.items():
        out[name] = (out[name] * factor).astype(out[name].dtype)
    return out
```

```python
import numpy as np
import concourse.bass as bass
from concourse import mybir

F32 = mybir.dt.float32
BF16 = mybir.dt.bfloat16
I32 = mybir.dt.int32
U32 = mybir.dt.uint32
ALU = mybir.AluOpType
ACT = mybir.ActivationFunctionType
AX = mybir.AxisListType

P = 128
B, L, DM = 4, 512, 512
DC = 256
KC = DC // P
KT = DM // P
LT = L // P
DS, DR, TAPS = 16, 16, 4
H, HD = 16, 32
HPT = P // HD
DCA = 16
MAIN = L - DCA
LN_EPS, QK_EPS = 1e-5, 1e-6
QK_SCALE = HD ** -0.5
TH_X, TH_W, SC_X, SC_W = 0.33, 0.2, 0.5, 0.6

NE, TOPK, FE, FS = 32, 6, 192, 384
FH = FE // 2
NT = B * LT
BLK = 256
NBLK = 80
assert (NT * P * TOPK + NE * (BLK - 1)) // BLK <= NBLK and NBLK % 2 == 0
NSLOT = NBLK * BLK

VEC = {}
_at = 0
for _name, _n in (("conv_w", KT * TAPS), ("conv_b", KT), ("dt_b", KT), ("A_log", KT * DS), ("D", KT),
                  ("bq", KT), ("bk", KT), ("bkd", KT), ("bv", KT), ("bvd", KT),
                  ("qw", 1), ("qb", 1), ("kw", 1), ("kb", 1), ("kdw", 1), ("kdb", 1), ("gates", 4)):
    VEC[_name] = (_at, _at + _n)
    _at += _n
NVEC = _at


class Signal:

    def __init__(self, sem, per, first=0):
        self.sem, self.per, self.first = sem, per, first

    def at(self, b, n):
        return b * self.per + (self.first + n)


class Order:

    def __init__(self, eng, sem, per):
        self.eng, self.sem, self.per = eng, sem, per
        self.first = self.n = 0
        self.b = None

    def enter(self, b):
        self.first, self.n, self.b = self.n, 0, b

    def leave(self):
        assert self.n == self.per, (self.sem, self.n, self.per)
        self.first, self.n, self.b = self.first + self.per * B, 0, None

    def mark(self, ins):
        ins.then_inc(self.sem, 1)
        self.n += 1
        return self.n

    def wait(self, n=None):
        n = self.n if n is None else n
        value = self.first + n if self.b is None else self.b * self.per + (self.first + n)
        self.eng.wait_ge(self.sem, value)

DVE_STEPS = 71
ACT_STEPS = 6


def program(nc, x, ctxT, vecs, w_in, w_xp, w_dt, ffn_w, ffn_r, w_q, w_k, w_v, w_kd, w_vd, w_o, b_o, w_g, w_sh, w_sd,
            w_gu, w_dn, out):
    def sb(name, shape, dt=F32):
        return nc.alloc_sbuf_tensor(name, shape, dt)

    def sem(name):
        return nc.alloc_semaphore(name)

    X = sb("X", [P, B * LT, DM])
    ps = nc.alloc_psum_tensor("ps", [P, 8, 512], F32)
    ctx = sb("ctx", [P, KC, L])
    V_ = sb("vecs_sb", [P, NVEC])
    region = sb("region", [P, 12288])

    def carve(at, *shape):
        n = int(np.prod(shape))
        v = region[:, at:at + n]
        if len(shape) == 2:
            v = v.rearrange("p (a c) -> p a c", c=shape[1])
        elif len(shape) == 3:
            v = v.rearrange("p (a t c) -> p a t c", t=shape[1], c=shape[2])
        return v

    Win, Wk, Wv, Wkd, Wvd = (carve(1024 * i, KC, DM) for i in range(5))
    Wq, Wo = carve(5120, KT, DM), carve(7168, KT, DM)
    W3 = region[:, 9216:12288].bitcast(BF16).rearrange("p (a t c) -> p a t c", a=3, t=KT)
    wgu = carve(0, 2, KT, 2 * FE)
    wdn = carve(3072, 2, 2, DM)
    G = carve(5120, 2, 2, DM)
    GT = carve(7168, 2, KT, BLK)
    Yb = carve(9216, 2, 2, DM)
    Wxp = sb("Wxp", [P, KT, DR + 2 * DS])
    Wdt = sb("Wdt", [DR, DM])
    bo = sb("bo", [1, DM])
    Wg = sb("Wg", [P, KT, NE])
    ident = sb("ident", [P, P])
    identb = sb("identb", [P, P], BF16)
    ones1 = sb("ones1", [1, P])
    ctx_credit = sb("ctx_credit", [1, 1])
    negA = sb("negA", [P, KT * DS])
    tg = sb("tg", [P, 4])
    eps = sb("eps", [P, 2])
    headmean = sb("headmean", [P, P])
    headvar = sb("headvar", [P, 8, 32])
    headrow = sb("headrow", [32, 8, P])
    bvsum = sb("bvsum", [P, KT])
    qkbias = sb("qkbias", [P, 3 * KT])
    aff = sb("aff", [P, 6])
    wsum = sb("wsum", [P, KT * H])
    st6 = sb("st6", [P, LT, 6])
    mv = sb("mv", [P, LT, 2])
    std = sb("std", [P, LT])
    rstd = sb("rstd", [P, LT])
    nmr = sb("nmr", [P, LT])
    XD = sb("XD", [DR + 2 * DS, L])
    sdr = sb("sdr", [32, L])
    rrow = sb("rrow", [32, L])
    nm = sb("nm", [P, 2, 4])
    esum = sb("prob_sums", [P, 2, 4])
    escale = sb("prob_scale", [P, 2, 4])
    arena = sb("arena", [P, 11, KT, L])
    siluz, U, delta, du = (arena[:, i] for i in range(4))
    conv = du
    xpad = arena[:, 4:6].rearrange("p a t l -> p (a t l)")[:, 0:KT * 516].rearrange("p (e l) -> p e l", l=516)
    dA = [arena[:, 4], arena[:, 5]]
    dBu = [arena[:, 6], arena[:, 7]]
    hs = [arena[:, 8], arena[:, 9], arena[:, 10]]
    sp_abs, sp_exp, sp_relu, sp_ln = dBu[0], dBu[1], hs[0], hs[1]
    yt, yz = dBu[0], dBu[1]
    xn, gt = arena[:, 0], arena[:, 1]
    tern = arena[:, 2].bitcast(BF16)[:, 0:2].rearrange("p a (t l) -> p (a t) l", l=L)
    ternT = arena[:, 3].bitcast(BF16)[:, 0:2].rearrange("p a (t l) -> p (a t) l", l=L)
    xnT = arena[:, 1]
    qk = arena[:, 2:4].rearrange("p a t l -> p (a t) l")
    sq = arena[:, 4:6].rearrange("p a t l -> p (a t) l")
    Vn = arena[:, 6]
    Pr = arena[:, 7].rearrange("p (s q) l -> p s q l", s=2)
    PT = arena[:, 8].rearrange("p (s q) l -> p s q l", s=2)
    ctxnT = arena[:, 10]
    wtmp = [arena[:, i] for i in range(4)]

    HT = arena[:, 0:4].rearrange("p k t l -> p k (t l)")
    hn = arena[:, 4]
    Wsh = arena[:, 5:7].rearrange("p a t l -> p (a t l)")[:, 0:KT * 2 * FS].rearrange("p (k f) -> p k f", k=KT)
    Wsd = arena[:, 7, 0:3]
    sil, aS = arena[:, 8, 0:3], arena[:, 9, 0:3]
    pick = region[:, 0:TOPK * NT * NE].rearrange("p (j t e) -> p j t e", t=NT, e=NE)
    SC = arena[:, 10, 0].rearrange("p (t e) -> p t e", e=NE)
    msum = arena[:, 10, 1].rearrange("p (t e) -> p t e", e=NE)
    slot = arena[:, 10, 2].rearrange("p (t e) -> p t e", e=NE)
    tmp = arena[:, 10, 3].rearrange("p (t e) -> p t e", e=NE)
    tot = arena[:, 9, 3].rearrange("p (e t) -> p e t", t=NT)
    cum = arena[:, 8, 3].rearrange("p (e t) -> p e t", t=NT)
    top = sb("top", [P, NT, 8])
    topi = sb("topi", [P, NT, 8], U32)
    topf = sb("topf", [P, NT, 8])
    den = sb("den", [P, NT])
    keep = sb("keep", [P, NE, NT])
    iota_i = sb("iota_i", [P, NE], I32)
    iota_f = sb("iota_f", [P, NE])
    blk_i = sb("blk_i", [1, NBLK], I32)
    blk_f = sb("blk_f", [1, NBLK])
    tri_f = sb("tri_f", [P, P])
    tri = sb("tri", [P, P], BF16)
    onesb = sb("onesb", [P, P], BF16)
    Mb = sb("Mb", [P, NT * NE], BF16)
    nb_f = sb("nb_f", [P, NE])
    nb_i = sb("nb_i", [P, NE], I32)
    end_b = sb("end_b", [P, NE])
    start_b = sb("start_b", [P, NE])
    ones_e = sb("ones_e", [P, NE])
    slots_f = sb("slots_f", [P, TOPK, NT])
    slots = sb("slots", [P, TOPK, NT], U32)
    pairs = sb("pairs", [P, NT, TOPK, 2], I32)
    tok_i = sb("tok_i", [P, NT], I32)
    le = region[0:1, 0:NBLK * NE].rearrange("p (n e) -> p n e", e=NE)
    expert_f = sb("expert_f", [1, NBLK])
    expert_i = sb("expert_i", [1, NBLK], I32)
    meta = sb("meta", [P, NSLOT // P, 2], I32)
    gidx = sb("gidx", [P, 2, 2, 2], I32)
    aidx = sb("aidx", [P, 2, 2], I32)
    act_s = sb("act_s", [P, 2, FE])
    act_m = sb("act_m", [P, 2, FE])
    aT = sb("aT", [FH, 2, BLK])
    Hd = nc.dram_tensor("Hd", [NT * P + BLK, DM], F32, kind="Internal").ap()
    listd = nc.dram_tensor("listd", [NSLOT, 2], I32, kind="Internal").ap()

    ln4_mv, ln4_std, ln4_coef = (Signal(sem(n), 1) for n in ("ln4_mv", "ln4_std", "ln4_coef"))
    hn_ready, hT_ready = (Signal(sem(n), LT) for n in ("hn_ready", "hT_ready"))
    hT_sb = Signal(sem("hT_sb"), LT, 1)
    h_stored = Signal(sem("h_stored"), 16 * LT, 16)
    setup_iota, zero_ready, fill_ready, list_filled = (sem(n) for n in ("setup_iota", "zero_ready", "fill_ready", "list_filled"))
    logits_ready, sc_ready, mask_ready, prefix_ready, slots_ready, scattered, meta_loaded, expert_ready = (
        sem(n) for n in ("logits_ready", "sc_ready", "mask_ready", "prefix_ready", "slots_ready", "scattered",
                         "meta_loaded", "expert_ready"))
    sh_loaded = sem("sh_loaded")
    shg_ready, sil_ready, aS_ready = (Signal(sem(n), 3) for n in ("shg_ready", "sil_ready", "aS_ready"))
    shy_ready, shx_done = (Signal(sem(n), LT) for n in ("shy_ready", "shx_done"))
    out_stored = sem("out_stored")
    wgu_loaded = [sem(f"wgu_loaded{u}") for u in range(2)]
    wdn_loaded = [sem(f"wdn_loaded{u}") for u in range(2)]
    gathered = [sem(f"gathered{u}") for u in range(2)]
    gt_ready, gt_a, gt_d, gu_ready, silu_done, act_done, at_ready, at_sb, y_ready, y_a, y_d, gidx_ready = (
        sem(n) for n in ("gt_ready", "gt_a", "gt_d", "gu_ready", "silu_done", "act_done", "at_ready", "at_sb", "y_ready",
                         "y_a", "y_d", "gidx_ready"))
    added = sem("added")
    prep_order = sem("prep_order")
    aidx_ready = sem("aidx_ready")
    zero_rows = Yb[:, 1]

    def ds2(s):
        return bass.ds(2 * s, 2)

    def ds1(s):
        return bass.ds(s, 1)

    def ge(eng, s, value):
        if not (isinstance(value, int) and value <= 0):
            eng.wait_ge(s, value)

    def steps(eng, step, first, last):
        lo, hi = first + first % 2, last + 1 - (last + 1) % 2
        lo += 4
        hi -= 2
        for s in range(first, lo):
            step(s, s // 2, s % 2)
        with eng.Fori(lo // 2, hi // 2) as r:
            for u in range(2):
                step(2 * r + u, r, u)
        for s in range(hi, last + 1):
            step(s, s // 2, s % 2)

    loaded = sem("loaded")
    setup_pool = sem("setup_pool")
    setup_act = sem("setup_act")
    setup_pe = sem("setup_pe")
    setup_dve = sem("setup_dve")
    batch_done = Signal(sem("batch_done"), 1, 1)
    ctx_loaded = Signal(sem("ctx_loaded"), 16)
    ctx_free = Signal(sem("ctx_free"), 1, 1)
    ln_mv, ln_std, ln_coef = (Signal(sem(n), 3) for n in ("ln_mv", "ln_std", "ln_coef"))
    xi_ready, xpad_ready, conv_ready, u_ready = (Signal(sem(n), KT) for n in ("xi_ready", "xpad_ready", "conv_ready", "u_ready"))
    siluz_ready = Signal(sem("siluz_ready"), LT)
    xd_ready, xd_sb, dt_ready, sp_ready, delta_ready = (Signal(sem(n), 1) for n in ("xd_ready", "xd_sb", "dt_ready", "sp_ready", "delta_ready"))
    dA_ready, b_ready, c_ready, b_used, scan_done, hc_ready, hc_used = (
        Signal(sem(n), DS) for n in ("dA_ready", "b_ready", "c_ready", "b_used", "scan_done", "hc_ready", "hc_used"))
    yz_ready = Signal(sem("yz_ready"), KT)
    yt_ready = Signal(sem("yt_ready"), 1)
    tern_ready = Signal(sem("tern_ready"), 1)
    ternT_ready, ternT_sb, ffn_ready = (Signal(sem(n), LT) for n in ("ternT_ready", "ternT_sb", "ffn_ready"))
    xn_ready, xT_ready, xT_sb = (Signal(sem(n), LT) for n in ("xn_ready", "xT_ready", "xT_sb"))
    proj_ready, qc_ready, sq_ready, rb_ready, rb_used, qk_final = (
        Signal(sem(n), 8) for n in ("proj_ready", "qc_ready", "sq_ready", "rb_ready", "rb_used", "qk_final"))
    var_ready, std_ready, rrow_ready, v_ready, v_sb = (Signal(sem(n), 1) for n in ("var_ready", "std_ready", "rrow_ready", "v_ready", "v_sb"))
    NIT = 2 * H
    s_ready, nm_ready, p_raw, p_final, t_ready, pt_d, pt_a, pv_done = (
        Signal(sem(n), NIT) for n in ("s_ready", "nm_ready", "p_raw", "p_final", "t_ready", "pt_d", "pt_a", "pv_done"))
    cT_sb, o_ready = (Signal(sem(n), LT) for n in ("cT_sb", "o_ready"))
    dve_order, act_order = sem("dve_order"), sem("act_order")
    act_passed, dve_passed, pool_passed = sem("act_passed"), sem("dve_passed"), sem("pool_passed")

    def vec(name, i=0, n=1):
        return V_[:, VEC[name][0] + i:VEC[name][0] + i + n]

    loads = [
        (V_[:, :], vecs), (Win[:, :, :], w_in), (Wxp[:, :, :], w_xp), (Wdt[:, :], w_dt),
        (X[:, :, :], x.rearrange("(t p) d -> p t d", p=P)),
        (wtmp[0], ffn_w), (wtmp[1], ffn_r), (Wq[:, :, :], w_q), (Wk[:, :, :], w_k), (Wkd[:, :, :], w_kd),
        (Wv[:, :, :], w_v), (Wvd[:, :, :], w_vd), (Wo[:, :, :], w_o), (bo[:, :], b_o), (Wg[:, :, :], w_g),
    ]

    with nc.Block() as block:
        @block.sync
        def _(sp):
            for dst, src in loads:
                sp.dma_start(dst, src).then_inc(loaded, 16)
            with sp.Fori(0, B) as b:
                sp.wait_ge(ctx_free.sem, ctx_free.at(b, 0))
                sp.dma_start(ctx[:, :, :], ctxT[b]).then_inc(ctx_loaded.sem, 16)
            sp.wait_ge(fill_ready, 1)
            sp.dma_start(listd.rearrange("(p n) c -> p n c", p=P), meta[:, :, :]).then_inc(list_filled, 16)
            sp.wait_ge(batch_done.sem, B + 1)
            sp.dma_start(Wsh, w_sh).then_inc(sh_loaded, 16)
            sp.dma_start(Wsd, w_sd).then_inc(sh_loaded, 16)
            sp.wait_ge(zero_ready, 1)
            sp.dma_start(Hd[NT * P:NT * P + BLK, :].rearrange("(a p) d -> p a d", p=P), zero_rows).then_inc(h_stored.sem, 16)
            sp.dma_start(out[NT * P:NT * P + BLK, :].rearrange("(a p) d -> p a d", p=P), zero_rows).then_inc(out_stored, 16)
            with sp.Fori(0, B) as b:
                for t in range(LT):
                    sp.wait_ge(hn_ready.sem, hn_ready.at(b, t + 1))
                    sp.dma_start(Hd.rearrange("(t p) d -> t p d", p=P)[b * LT + t], hn[:, t]).then_inc(h_stored.sem, 16)
            sp.wait_ge(scattered, 16 * NT * TOPK)
            sp.dma_start(meta[:, :, :], listd.rearrange("(n p) c -> p n c", p=P), allow_slow_non_contiguous=True)\
                .then_inc(meta_loaded, 16)
            with sp.Fori(0, B) as b:
                for t in range(LT):
                    sp.wait_ge(shx_done.sem, shx_done.at(b, t + 1))
                    sp.dma_start(out[0:NT * P, :].rearrange("(t p) d -> t p d", p=P)[b * LT + t], X[:, b * LT + t, :])\
                        .then_inc(out_stored, 16)
            sp.wait_ge(expert_ready, 1)

            def load_weights(s, r, u):
                e = sp.value_load(expert_i[0:1, ds1(s)], min_val=0, max_val=NE - 1)
                ge(sp, gu_ready, 2 * (s - 1))
                sp.dma_start(wgu[:, u], w_gu[e]).then_inc(wgu_loaded[u], 16)
                ge(sp, y_ready, 2 * (s - 1))
                sp.dma_start(wdn[0:FH, u], w_dn[e]).then_inc(wdn_loaded[u], 16)

            steps(sp, load_weights, 0, NBLK - 1)
            sp.wait_ge(added, 16 * 2 * NBLK)

        @block.gpsimd
        def _(pool):
            pool.memset(ident[:, :], 0.0).then_inc(setup_pool, 1)
            pool.memset(ones1[:, :], 1.0)
            pool.memset(eps[:, 0:1], LN_EPS)
            pool.memset(eps[:, 1:2], QK_EPS)
            pool.memset(headrow[:, :, :], 0.0).then_inc(setup_pool, 1)
            pool.wait_ge(setup_pool, 2)
            pool.affine_select(out=ident[:, :], in_=ident[:, :], compare_op=ALU.not_equal, fill=1.0, base=0,
                               pattern=[[-1, P]], channel_multiplier=1)
            hr = headrow[:, :, :].rearrange("r i (j c) -> r i j c", c=HD)
            pool.affine_select(out=hr, in_=hr, compare_op=ALU.not_equal, fill=1.0, base=0,
                               pattern=[[-HPT, 8], [-1, HPT], [0, HD]], channel_multiplier=1).then_inc(setup_pool, 1)
            pool.wait_ge(setup_pool, 3)
            pool.tensor_copy(identb[:, :], ident[:, :]).then_inc(setup_pool, 1)
            pool.memset(ctx_credit[:, :], 0.0).then_inc(ctx_free.sem, 1)
            pool.iota(iota_i[:, :], pattern=[[1, NE]], base=0, channel_multiplier=0)
            pool.iota(blk_i[:, :], pattern=[[1, NBLK]], base=0, channel_multiplier=0)
            pool.iota(tok_i[:, :], pattern=[[P, NT]], base=0, channel_multiplier=1)
            pool.iota(meta[:, :, 0], pattern=[[1, NSLOT // P]], base=0, channel_multiplier=NSLOT // P)
            pool.memset(meta[:, :, 1], 0)
            pool.memset(onesb[:, :], 1.0)
            pool.memset(ones_e[:, :], 1.0)
            pool.memset(keep[:, :, :], 1.0)
            pool.memset(tri_f[:, :], 1.0).then_inc(setup_iota, 1)
            pool.wait_ge(setup_iota, 1)
            pool.memset(keep[:, :, 0:1], 0.0)
            pool.affine_select(out=tri_f[:, :], in_=tri_f[:, :], compare_op=ALU.is_gt, fill=0.0, base=0,
                               pattern=[[1, P]], channel_multiplier=-1).then_inc(setup_iota, 1)
            pool.wait_ge(list_filled, 16)
            pool.wait_ge(slots_ready, 1)
            for t in range(NT):
                for j in range(TOPK):
                    pool.indirect_dma_start(listd, bass.IndirectOffsetOnAxis(slots[:, j, t:t + 1], 0), pairs[:, t, j, :], None)\
                        .then_inc(scattered, 16)
            pool.wait_ge(meta_loaded, 16)
            pool.wait_ge(h_stored.sem, h_stored.at(B, 0))
            pool.wait_ge(out_stored, 16 * (NT + 1))

            def settle():
                pool.sem_inc(pool_passed, 1)

            def gather(s, u, r):
                ge(pool, gt_ready, s - 1)
                ge(pool, gathered[u], 32 * r)
                pool.tensor_copy(gidx[:, u, :, 0], meta[:, ds2(s), 0]).then_inc(gidx_ready, 1)
                pool.wait_ge(gidx_ready, s + 1)
                settle()
                for q in range(2):
                    pool.indirect_dma_start(G[:, u, q], None, Hd, bass.IndirectOffsetOnAxis(gidx[:, u, q, 0:1].bitcast(U32), 0))\
                        .then_inc(gathered[u], 16)

            def block_dmas(s, r, u):
                if not isinstance(s, int) or s + 1 < NBLK:
                    gather(s + 1, 1 - u, r if u == 0 else r + 1)
                if not isinstance(s, int) or s >= 2:
                    add(s - 2, u)

            def add(s, u):
                ge(pool, added, 32 * s)
                pool.tensor_copy(aidx[:, :, 0], meta[:, ds2(s), 0]).then_inc(aidx_ready, 1)
                pool.wait_ge(aidx_ready, s + 1)
                pool.wait_ge(y_d, s + 1)
                pool.wait_ge(y_a, s + 1)
                settle()
                for q in range(2):
                    pool.indirect_dma_start(out, bass.IndirectOffsetOnAxis(aidx[:, q, 0:1].bitcast(U32), 0), Yb[:, u, q], None,
                                            compute_op=ALU.add).then_inc(added, 16)
                    if q == 0:
                        pool.wait_ge(added, 32 * s + 16)
                        settle()

            gather(0, 0, 0)
            steps(pool, block_dmas, 0, NBLK - 1)
            for s in range(NBLK - 2, NBLK):
                add(s, s % 2)

        @block.scalar
        def _(act):
            order = Order(act, act_order, ACT_STEPS)
            act.wait_ge(loaded, 16 * len(loads))
            act.wait_ge(setup_pool, 4)
            act.activation(tg[:, :], vec("gates", 0, 4), ACT.Tanh)
            act.activation(negA[:, :], vec("A_log", 0, KT * DS), ACT.Exp).then_inc(setup_act, 1)

            def settle():
                act.sem_inc(act_passed, 1)

            def ln_root(b, k):
                act.wait_ge(ln_mv.sem, ln_mv.at(b, k + 1))
                act.activation(std[:, :], mv[:, :, 1], ACT.Sqrt, bias=eps[:, 0:1]).then_inc(ln_std.sem, 1)

            with act.Fori(0, B) as b:
                order.enter(b)
                act.wait_ge(batch_done.sem, batch_done.at(b, 0))
                for e in range(KT):
                    act.wait_ge(xi_ready.sem, xi_ready.at(b, e + 1))
                    act.activation(xpad[:, e, 3:3 + L], ps[:, e, :], ACT.Copy).then_inc(xpad_ready.sem, 1)
                ln_root(b, 0)
                act.wait_ge(ln_coef.sem, ln_coef.at(b, 1))
                settle()
                for t in range(LT):
                    act.activation(siluz[:, t], X[:, b * LT + t, :], ACT.Silu, bias=nmr[:, t:t + 1],
                                   scale=rstd[:, t:t + 1]).then_inc(siluz_ready.sem, 1)
                for e in range(KT):
                    act.wait_ge(conv_ready.sem, conv_ready.at(b, e + 1))
                    act.activation(U[:, e], conv[:, e], ACT.Silu, bias=vec("conv_b", e)).then_inc(u_ready.sem, 1)
                act.wait_ge(dt_ready.sem, dt_ready.at(b, 1))
                for e in range(KT):
                    act.activation(sp_relu[:, e], ps[:, e, :], ACT.Relu, bias=vec("dt_b", e))
                    m = order.mark(act.activation(sp_abs[:, e], ps[:, e, :], ACT.Abs, bias=vec("dt_b", e)))
                order.wait(m)
                order.mark(act.activation(sp_exp, sp_abs, ACT.Exp, scale=-1.0))
                order.wait()
                act.activation(sp_ln, sp_exp, ACT.Ln, bias=1.0).then_inc(sp_ready.sem, 1)
                act.wait_ge(delta_ready.sem, delta_ready.at(b, 1))
                for n in range(DS):
                    if n >= 2:
                        act.wait_ge(scan_done.sem, scan_done.at(b, n - 1))
                    for e in range(KT):
                        i = act.activation(dA[n % 2][:, e, 1:L], delta[:, e, 1:L], ACT.Exp,
                                           scale=negA[:, e * DS + n:e * DS + n + 1])
                    i.then_inc(dA_ready.sem, 1)
                ln_root(b, 1)
                for t in range(LT):
                    act.wait_ge(ternT_ready.sem, ternT_ready.at(b, t + 1))
                    act.activation(ternT[:, :, t * P:(t + 1) * P],
                                   ps[:, t, :].bitcast(BF16)[:, 0:DM].rearrange("p (k l) -> p k l", k=KT),
                                   ACT.Copy).then_inc(ternT_sb.sem, 1)
                ln_root(b, 2)
                act.wait_ge(ln_coef.sem, ln_coef.at(b, 3))
                settle()
                for t in range(LT):
                    act.activation(xn[:, t], X[:, b * LT + t, :], ACT.Identity, bias=nmr[:, t:t + 1],
                                   scale=rstd[:, t:t + 1]).then_inc(xn_ready.sem, 1)
                for i in range(8):
                    act.wait_ge(proj_ready.sem, proj_ready.at(b, i + 1))
                    bank = (4 + i) % 8
                    if i < KT:
                        act.activation(qk[:, i], ps[:, bank, :], ACT.Identity,
                                       bias=qkbias[:, i:i + 1]).then_inc(qc_ready.sem, 1)
                    else:
                        act.activation(qk[:, i, 0:MAIN], ps[:, bank, 0:MAIN], ACT.Identity, bias=qkbias[:, i:i + 1])
                        act.activation(qk[:, i, MAIN:L], ps[:, bank, MAIN:L], ACT.Identity,
                                       bias=qkbias[:, i + KT:i + KT + 1]).then_inc(qc_ready.sem, 1)
                act.wait_ge(v_ready.sem, v_ready.at(b, 1))
                for j in range(LT - 1):
                    act.activation(Vn[:, j], ps[:, j, :], ACT.Copy)
                order.mark(act.activation(Vn[96:128, 3], ps[96:128, 5, :], ACT.Copy))
                order.wait()
                act.activation(Vn[0:MAIN - 3 * P, 3], ps[0:MAIN - 3 * P, 3, :], ACT.Copy).then_inc(v_sb.sem, 1)
                act.wait_ge(var_ready.sem, var_ready.at(b, 1))
                act.activation(sdr[:, :], ps[0:32, 4, :], ACT.Sqrt, bias=eps[0:32, 1:2]).then_inc(std_ready.sem, 1)
                for i in range(8):
                    act.wait_ge(rb_used.sem, rb_used.at(b, i + 1))
                    if i < KT:
                        act.activation(qk[:, i], qk[:, i], ACT.Identity, bias=aff[:, 1:2]).then_inc(qk_final.sem, 1)
                    else:
                        act.activation(qk[:, i, 0:MAIN], qk[:, i, 0:MAIN], ACT.Identity, bias=aff[:, 3:4])
                        act.activation(qk[:, i, MAIN:L], qk[:, i, MAIN:L], ACT.Identity,
                                       bias=aff[:, 5:6]).then_inc(qk_final.sem, 1)

                def exps(it):
                    qp, h = divmod(it, H)
                    s = it % 2
                    act.wait_ge(nm_ready.sem, nm_ready.at(b, it + 1))
                    if it >= 2:
                        act.wait_ge(t_ready.sem, t_ready.at(b, it - 1))
                    for q in range(2):
                        bank = 2 * s + q
                        act.activation(Pr[:, s, q, 0:MAIN], ps[:, bank, 0:MAIN], ACT.Exp, bias=nm[:, s, q:q + 1],
                                       accum_out=esum[:, s, q:q + 1])
                        i = act.activation(Pr[:, s, q, MAIN:L], ps[:, bank, MAIN:L], ACT.Exp,
                                           bias=nm[:, s, 2 + q:3 + q], accum_out=esum[:, s, 2 + q:3 + q])
                    i.then_inc(p_raw.sem, 1)

                exps(0)
                exps(1)
                for it in range(NIT):
                    act.wait_ge(t_ready.sem, t_ready.at(b, it + 1))
                    if it >= 2:
                        act.wait_ge(pv_done.sem, pv_done.at(b, it - 1))
                    act.activation(PT[:, it % 2, 1], ps[:, 5, :], ACT.Copy).then_inc(pt_a.sem, 1)
                    if it + 2 < NIT:
                        exps(it + 2)
            order.leave()

            with act.Fori(0, B) as b:
                act.wait_ge(ln4_mv.sem, ln4_mv.at(b, 1))
                act.activation(std[:, :], mv[:, :, 1], ACT.Sqrt, bias=eps[:, 0:1]).then_inc(ln4_std.sem, 1)
                act.wait_ge(hT_sb.sem, hT_sb.at(b, 0))
                act.wait_ge(h_stored.sem, h_stored.at(b, 0))
                act.wait_ge(ln4_coef.sem, ln4_coef.at(b, 1))
                settle()
                for t in range(LT):
                    act.activation(hn[:, t], X[:, b * LT + t, :], ACT.Identity, bias=nmr[:, t:t + 1],
                                   scale=rstd[:, t:t + 1]).then_inc(hn_ready.sem, 1)
            act.wait_ge(logits_ready, 1)
            act.activation(SC.rearrange("p t e -> p (t e)"), ps[:, 4, :], ACT.Sigmoid).then_inc(sc_ready, 1)
            with act.Fori(0, B) as c:
                for m in range(3):
                    act.wait_ge(shg_ready.sem, shg_ready.at(c, m + 1))
                    act.activation(sil[:, m], ps[:, 2 * m, :], ACT.Silu).then_inc(sil_ready.sem, 1)

            def block_act(s, r, u):
                for q in range(2):
                    act.wait_ge(gu_ready, 2 * s + q + 1)
                    ge(act, act_done, 2 * (s - 1) + q + 1)
                    act.activation(act_s[:, q, :], ps[:, 2 + q, 0:FE], ACT.Silu).then_inc(silu_done, 1)
                turned(s + 1, 1 - u)
                scaled(s - 1, 1 - u)

            def turned(s, u):
                if isinstance(s, int) and s >= NBLK:
                    return
                act.wait_ge(gt_ready, s + 1)
                ge(act, gu_ready, 2 * (s - 1))
                act.activation(GT[:, u, 2:4], ps[:, 1, :].rearrange("p (k l) -> p k l", k=2), ACT.Copy).then_inc(gt_a, 1)

            def scaled(s, u):
                if isinstance(s, int) and s < 0:
                    return
                act.wait_ge(y_ready, 2 * (s + 1))
                ge(act, added, 32 * (s - 1))
                settle()
                act.activation(Yb[:, u, 1], ps[:, 6, :], ACT.Copy, scale=meta[:, bass.ds(2 * s + 1, 1), 1].bitcast(F32))\
                    .then_inc(y_a, 1)

            turned(0, 0)
            steps(act, block_act, 0, NBLK - 1)
            scaled(NBLK - 1, 1)

        @block.tensor
        def _(pe):
            pe.wait_ge(loaded, 16 * len(loads))
            pe.wait_ge(setup_pool, 4)
            pe.wait_ge(setup_dve, 1)
            pe.matmul(ps[:, 0, 0:3 * KT], headmean[:, :], vec("bq", 0, 3 * KT), start=True, stop=True).then_inc(setup_pe, 1)
            with pe.Fori(0, B) as b:
                pe.wait_ge(batch_done.sem, batch_done.at(b, 0))
                pe.wait_ge(ctx_loaded.sem, ctx_loaded.at(b, 16))
                for e in range(KT):
                    for k in range(KC):
                        i = pe.matmul(ps[:, e, :], Win[:, k, e * P:(e + 1) * P], ctx[:, k, :], start=(k == 0), stop=(k == KC - 1))
                    i.then_inc(xi_ready.sem, 1)
                for k in range(KT):
                    pe.wait_ge(u_ready.sem, u_ready.at(b, k + 1))
                    i = pe.matmul(ps[0:DR + 2 * DS, 4, :], Wxp[:, k, :], U[:, k], start=(k == 0), stop=(k == KT - 1))
                i.then_inc(xd_ready.sem, 1)
                pe.wait_ge(xd_sb.sem, xd_sb.at(b, 1))
                for e in range(KT):
                    i = pe.matmul(ps[:, e, :], Wdt[:, e * P:(e + 1) * P], XD[0:DR, :], start=True, stop=True)
                i.then_inc(dt_ready.sem, 1)

                def spread(n, part, ready, used, bank):
                    if n >= 2:
                        pe.wait_ge(used.sem, used.at(b, n - 1))
                    row = ident[0:DR + 2 * DS, part + n:part + n + 1].to_broadcast([DR + 2 * DS, P])
                    pe.matmul(ps[:, bank + n % 2, :], row, XD[:, :], start=True, stop=True).then_inc(ready.sem, 1)

                def spread_b(n):
                    spread(n, DR, b_ready, b_used, 4)

                def spread_c(n):
                    spread(n, DR + DS, c_ready, hc_ready, 6)

                spread_b(0)
                spread_b(1)
                spread_c(0)
                spread_b(2)
                for n in range(DS):
                    if n + 3 < DS:
                        spread_b(n + 3)
                    if n + 1 < DS:
                        spread_c(n + 1)
                    pe.wait_ge(hc_ready.sem, hc_ready.at(b, n + 1))
                    for e in range(KT):
                        i = pe.matmul(ps[:, e, :], ident[:, :], hs[n % 3][:, e], start=(n == 0), stop=(n == DS - 1))
                    i.then_inc(hc_used.sem, 1)
                for e in range(KT):
                    pe.wait_ge(yz_ready.sem, yz_ready.at(b, e + 1))
                    for l in range(LT):
                        i = pe.transpose(ps[:, 4 + l, e * P:(e + 1) * P], yz[:, e, l * P:(l + 1) * P], ident[:, :])
                i.then_inc(yt_ready.sem, 1)

                pe.wait_ge(tern_ready.sem, tern_ready.at(b, 1))
                for t in range(LT):
                    for k in range(KT):
                        i = pe.transpose(ps[:, t, :].bitcast(BF16)[:, k * P:(k + 1) * P], tern[:, t, k * P:(k + 1) * P],
                                         identb[:, :])
                    i.then_inc(ternT_ready.sem, 1)
                for t in range(LT):
                    pe.wait_ge(ternT_sb.sem, ternT_sb.at(b, t + 1))
                    for k in range(KT):
                        for part in range(3):
                            i = pe.matmul(ps[:, 4 + t, :], ternT[:, k, t * P:(t + 1) * P], W3[:, part, k, :],
                                          start=(k == 0 and part == 0), stop=(k == KT - 1 and part == 2))
                    i.then_inc(ffn_ready.sem, 1)

                for t in range(LT):
                    pe.wait_ge(xn_ready.sem, xn_ready.at(b, t + 1))
                    for k in range(KT):
                        i = pe.transpose(ps[:, t, k * P:(k + 1) * P], xn[:, t, k * P:(k + 1) * P], ident[:, :])
                    i.then_inc(xT_ready.sem, 1)
                pe.wait_ge(xT_sb.sem, xT_sb.at(b, LT))
                for i8 in range(8):
                    if i8 < KT:
                        for k in range(KT):
                            i = pe.matmul(ps[:, 4 + i8, :], Wq[:, k, i8 * P:(i8 + 1) * P], xnT[:, k], start=(k == 0),
                                          stop=(k == KT - 1))
                    else:
                        e = i8 - KT
                        for k in range(KC):
                            pe.matmul(ps[:, e, 0:MAIN], Wk[:, k, e * P:(e + 1) * P], ctx[:, k, 0:MAIN], start=(k == 0),
                                      stop=(k == KC - 1))
                        for k in range(KC):
                            i = pe.matmul(ps[:, e, MAIN:L], Wkd[:, k, e * P:(e + 1) * P], ctx[:, k, MAIN:L],
                                          start=(k == 0), stop=(k == KC - 1))
                    i.then_inc(proj_ready.sem, 1)
                for i8 in range(8):
                    pe.wait_ge(sq_ready.sem, sq_ready.at(b, i8 + 1))
                    i = pe.matmul(ps[0:32, 4, :], headvar[:, i8, :], sq[:, i8], start=(i8 == 0), stop=(i8 == 7))
                i.then_inc(var_ready.sem, 1)
                pe.wait_ge(qc_ready.sem, qc_ready.at(b, 8))
                for j in range(LT):
                    n = P if j < LT - 1 else MAIN - 3 * P
                    for k in range(KC):
                        pe.matmul(ps[0:n, j, :], ctx[:, k, j * P:j * P + n], Wv[:, k, :], start=(k == 0), stop=(k == KC - 1))
                for k in range(KC):
                    i = pe.matmul(ps[96:128, 5, :], ctx[:, k, L - 32:L], Wvd[:, k, :], start=(k == 0), stop=(k == KC - 1))
                i.then_inc(v_ready.sem, 1)
                pe.wait_ge(v_ready.sem, v_ready.at(b, 1))
                pe.sem_inc(ctx_free.sem, 1)
                pe.wait_ge(rrow_ready.sem, rrow_ready.at(b, 1))
                for i8 in range(8):
                    if i8 >= 2:
                        pe.wait_ge(rb_used.sem, rb_used.at(b, i8 - 1))
                    pe.matmul(ps[:, 6 + i8 % 2, :], headrow[:, i8, :], rrow[:, :], start=True, stop=True)\
                        .then_inc(rb_ready.sem, 1)
                pe.wait_ge(v_sb.sem, v_sb.at(b, 1))

                def scores(it):
                    qp, h = divmod(it, H)
                    rows, tile = slice(HD * (h % HPT), HD * (h % HPT + 1)), h // HPT
                    pe.wait_ge(qk_final.sem, qk_final.at(b, KT + tile + 1))
                    if it >= 2:
                        pe.wait_ge(p_raw.sem, p_raw.at(b, it - 1))
                    for q in range(2):
                        t = 2 * qp + q
                        i = pe.matmul(ps[:, 2 * (it % 2) + q, :], qk[rows, tile, t * P:(t + 1) * P], qk[rows, KT + tile, :],
                                      start=True, stop=True)
                    i.then_inc(s_ready.sem, 1)

                def turn(it):
                    pe.wait_ge(p_final.sem, p_final.at(b, it + 1))
                    if it >= 1:
                        pe.wait_ge(pt_d.sem, pt_d.at(b, it))
                        pe.wait_ge(pt_a.sem, pt_a.at(b, it))
                    for q in range(2):
                        for j in range(LT):
                            i = pe.transpose(ps[:, 4 + q, j * P:(j + 1) * P], Pr[:, it % 2, q, j * P:(j + 1) * P], ident[:, :])
                    i.then_inc(t_ready.sem, 1)

                def weigh(it):
                    qp, h = divmod(it, H)
                    pe.wait_ge(pt_d.sem, pt_d.at(b, it + 1))
                    pe.wait_ge(pt_a.sem, pt_a.at(b, it + 1))
                    if it == H:
                        pe.wait_ge(cT_sb.sem, cT_sb.at(b, 2))
                    rows, tile = slice(HD * (h % HPT), HD * (h % HPT + 1)), h // HPT
                    for j in range(LT):
                        i = pe.matmul(ps[rows, 6 + tile // 2, (tile % 2) * 2 * P:(tile % 2 + 1) * 2 * P],
                                      Vn[:, j, h * HD:(h + 1) * HD], PT[:, it % 2, :, j * P:(j + 1) * P],
                                      start=(j == 0), stop=(j == LT - 1))
                    i.then_inc(pv_done.sem, 1)

                scores(0)
                scores(1)
                for it in range(NIT):
                    if it + 2 < NIT:
                        scores(it + 2)
                    turn(it)
                    if it >= 1:
                        weigh(it - 1)
                weigh(NIT - 1)
                for t in range(LT):
                    pe.wait_ge(cT_sb.sem, cT_sb.at(b, 2 * (t // 2 + 1)))
                    for k in range(KT):
                        pe.matmul(ps[:, 4 + t, :], ctxnT[:, k, t * P:(t + 1) * P], Wo[:, k, :], start=(k == 0), stop=False)
                    pe.matmul(ps[:, 4 + t, :], ones1[:, :], bo[:, :], start=False, stop=True).then_inc(o_ready.sem, 1)

            with pe.Fori(0, B) as b:
                for t in range(LT):
                    pe.wait_ge(hn_ready.sem, hn_ready.at(b, t + 1))
                    for k in range(KT):
                        i = pe.transpose(ps[:, t, k * P:(k + 1) * P], hn[:, t, k * P:(k + 1) * P], ident[:, :])
                    i.then_inc(hT_ready.sem, 1)
            pe.wait_ge(hT_sb.sem, hT_sb.at(B, 0))
            for t in range(NT):
                for k in range(KT):
                    i = pe.matmul(ps[:, 4, t * NE:(t + 1) * NE], HT[:, k, t * P:(t + 1) * P], Wg[:, k, :], start=(k == 0),
                                  stop=(k == KT - 1))
            i.then_inc(logits_ready, 1)
            pe.wait_ge(mask_ready, 1)
            pe.matmul(ps[:, 5, :], tri[:, :], Mb[:, :], start=True, stop=True)
            pe.matmul(ps[:, 6, :], onesb[:, :], Mb[:, :], start=True, stop=True).then_inc(prefix_ready, 1)
            pe.wait_ge(sh_loaded, 32)
            pe.wait_ge(slots_ready, 1)
            with pe.Fori(0, B) as c:
                for m in range(3):
                    for half in range(2):
                        for k in range(KT):
                            i = pe.matmul(ps[:, 2 * m + half, :], Wsh[:, k, half * FS + m * P:half * FS + (m + 1) * P],
                                          HT[:, k, bass.ds(c * L, L)], start=(k == 0), stop=(k == KT - 1))
                    i.then_inc(shg_ready.sem, 1)
                for t in range(LT):
                    if t >= 2:
                        pe.wait_ge(shx_done.sem, shx_done.at(c, t - 1))
                    for m in range(3):
                        if t == 0:
                            pe.wait_ge(aS_ready.sem, aS_ready.at(c, m + 1))
                        i = pe.matmul(ps[:, 6 + t % 2, :], aS[:, m, t * P:(t + 1) * P], Wsd[:, m, :], start=(m == 0),
                                      stop=(m == 2))
                    i.then_inc(shy_ready.sem, 1)
            pe.wait_ge(shx_done.sem, shx_done.at(B, 0))

            def turn_tokens(s, r, u):
                if isinstance(s, int) and s >= NBLK:
                    return
                pe.wait_ge(gathered[u], 32 * (r + 1))
                ge(pe, gt_a, s)
                ge(pe, gt_d, s)
                for k in range(KT):
                    for q in range(2):
                        i = pe.transpose(ps[:, k // 2, (k % 2) * BLK + q * P:(k % 2) * BLK + (q + 1) * P],
                                         G[:, u, q, k * P:(k + 1) * P], ident[:, :])
                i.then_inc(gt_ready, 1)

            def up(s, r, u):
                pe.wait_ge(gt_a, s + 1)
                pe.wait_ge(gt_d, s + 1)
                pe.wait_ge(wgu_loaded[u], 16 * (r + 1))
                for q in range(2):
                    ge(pe, act_done, 2 * (s - 1) + q + 1)
                    for k in range(KT):
                        i = pe.matmul(ps[:, 2 + q, 0:2 * FE], GT[:, u, k, q * P:(q + 1) * P], wgu[:, u, k], start=(k == 0),
                                      stop=(k == KT - 1))
                    i.then_inc(gu_ready, 1)

            def turn_act(s, r, u):
                if isinstance(s, int) and s < 0:
                    return
                pe.wait_ge(act_done, 2 * (s + 1))
                ge(pe, at_sb, s)
                for f in range(2):
                    for q in range(2):
                        i = pe.transpose(ps[0:FH, 4, f * BLK + q * P:f * BLK + (q + 1) * P], act_m[:, q, f * FH:(f + 1) * FH],
                                         ident[:, :])
                i.then_inc(at_ready, 1)

            def down(s, r, u):
                if isinstance(s, int) and s < 0:
                    return
                pe.wait_ge(at_sb, s + 1)
                pe.wait_ge(wdn_loaded[u], 16 * (r + 1))
                ge(pe, y_a, s)
                ge(pe, y_d, s)
                for q in range(2):
                    for f in range(2):
                        i = pe.matmul(ps[:, 5 + q, :], aT[:, f, q * P:(q + 1) * P], wdn[0:FH, u, f], start=(f == 0),
                                      stop=(f == 1))
                    i.then_inc(y_ready, 1)

            def block_pe(s, r, u):
                before = (s - 1, r - 1 if u == 0 else r, 1 - u)
                turn_act(*before)
                up(s, r, u)
                turn_tokens(s + 1, r if u == 0 else r + 1, 1 - u)
                down(*before)

            turn_tokens(0, 0, 0)
            steps(pe, block_pe, 0, NBLK - 1)
            last = (NBLK - 1, (NBLK - 1) // 2, 1)
            turn_act(*last)
            down(*last)

        @block.vector
        def _(dve):
            order = Order(dve, dve_order, DVE_STEPS)
            o = order
            dve.memset(headmean[:, :], 0.0)
            o.mark(dve.memset(headvar[:, :, :], 0.0))
            o.wait()
            dve.wait_ge(setup_iota, 2)
            dve.tensor_copy(iota_f[:, :], iota_i[:, :])
            dve.tensor_copy(blk_f[:, :], blk_i[:, :])
            dve.tensor_copy(tri[:, :], tri_f[:, :])
            o.mark(dve.tensor_scalar(meta[:, :, 0], meta[:, :, 0], BLK - 1, None, ALU.bitwise_and))
            o.wait()
            dve.tensor_scalar(meta[:, :, 0], meta[:, :, 0], float(NT * P), None, ALU.add).then_inc(fill_ready, 1)
            flat_var = headvar[:, :, :].rearrange("p i c -> p (i c)")
            for j in range(HPT):
                rows = slice(HD * j, HD * (j + 1))
                dve.memset(headmean[rows, rows], 1.0 / HD)
                i = dve.memset(flat_var[rows, j:j + 36 * 7 + 1:36], 1.0 / HD)
            i.then_inc(setup_dve, 1)
            dve.wait_ge(loaded, 16 * len(loads))
            w, r, lt, acc = wtmp
            a = o.mark(dve.tensor_scalar(lt, w, -TH_W, None, ALU.is_lt))
            o.wait(a)
            o.mark(dve.scalar_tensor_tensor(out=acc, in0=w, scalar=TH_W, in1=lt, op0=ALU.is_gt, op1=ALU.subtract))
            o.wait()
            o.mark(dve.scalar_tensor_tensor(out=acc, in0=acc, scalar=SC_W, in1=r, op0=ALU.mult, op1=ALU.add))
            o.wait()
            o.mark(dve.tensor_scalar(acc, acc, -SC_X, None, ALU.mult))
            for part in range(3):
                o.wait()
                o.mark(dve.tensor_copy(W3[:, part], acc))
                if part < 2:
                    o.wait()
                    o.mark(dve.tensor_tensor(acc, acc, W3[:, part], ALU.subtract))
            for W, kt in ((Wq, KT), (Wk, KC), (Wkd, KC)):
                heads = W[:, :, :].rearrange("p k (h d) -> p (k h) d", d=HD)
                o.mark(dve.tensor_reduce(wsum[:, 0:kt * H], heads, AX.X, ALU.add))
                o.wait()
                o.mark(dve.tensor_scalar(wsum[:, 0:kt * H], wsum[:, 0:kt * H], 1.0 / HD, None, ALU.mult))
                o.wait()
                o.mark(dve.tensor_tensor(heads, heads, wsum[:, 0:kt * H].unsqueeze(2).to_broadcast([P, kt * H, HD]),
                                         ALU.subtract))
                o.wait()
            dve.wait_ge(setup_pe, 1)
            dve.tensor_tensor(qkbias[:, :], vec("bq", 0, 3 * KT), ps[:, 0, 0:3 * KT], ALU.subtract)
            dve.tensor_tensor(bvsum[:, :], vec("bv", 0, KT), vec("bvd", 0, KT), ALU.add)
            dve.tensor_scalar(aff[:, 0:2], vec("qw", 0, 2), QK_SCALE, None, ALU.mult)
            dve.tensor_copy(aff[:, 2:6], vec("kw", 0, 4))
            dve.wait_ge(setup_act, 1)
            o.mark(dve.tensor_scalar(negA[:, :], negA[:, :], -1.0, None, ALU.mult))
            o.wait()
            dve.tensor_copy(std[:, 0:1], V_[:, 0:1]).then_inc(batch_done.sem, 1)

            def settle():
                dve.sem_inc(dve_passed, 1)

            def ln_stats(b, k):
                settle()
                for t in range(LT):
                    i = dve.bn_stats(st6[:, t, :], X[:, b * LT + t, :])
                o.mark(i)
                o.wait()
                settle()
                for t in range(LT):
                    i = dve.bn_aggr(mv[:, t, :], st6[:, t, :])
                i.then_inc(ln_mv.sem, 1)

            def ln_coefs(b, k):
                dve.wait_ge(ln_std.sem, ln_std.at(b, k + 1))
                o.mark(dve.reciprocal(rstd[:, :], std[:, :]))
                o.wait()
                dve.scalar_tensor_tensor(out=nmr[:, :], in0=mv[:, :, 0], scalar=-1.0, in1=rstd[:, :], op0=ALU.mult,
                                         op1=ALU.mult).then_inc(ln_coef.sem, 1)

            with dve.Fori(0, B) as b:
                o.enter(b)
                dve.wait_ge(batch_done.sem, batch_done.at(b, 0))
                pad = o.mark(dve.memset(xpad[:, :, 0:3], 0.0))
                ln_stats(b, 0)
                ln_coefs(b, 0)
                o.wait(pad)
                marks = []
                for tap in (3, 2, 1, 0):
                    for e in range(KT):
                        wk = vec("conv_w", e * TAPS + tap)
                        if tap == 3:
                            dve.wait_ge(xpad_ready.sem, xpad_ready.at(b, e + 1))
                            i = dve.tensor_scalar(conv[:, e], xpad[:, e, tap:tap + L], wk, None, ALU.mult)
                        else:
                            o.wait(marks[-KT])
                            i = dve.scalar_tensor_tensor(out=conv[:, e], in0=xpad[:, e, tap:tap + L], scalar=wk,
                                                         in1=conv[:, e], op0=ALU.mult, op1=ALU.add)
                        if tap:
                            marks.append(o.mark(i))
                        else:
                            i.then_inc(conv_ready.sem, 1)
                            marks.append(marks[-1])
                dve.wait_ge(xd_ready.sem, xd_ready.at(b, 1))
                dve.tensor_copy(XD[:, :], ps[0:DR + 2 * DS, 4, :]).then_inc(xd_sb.sem, 1)
                dve.wait_ge(conv_ready.sem, conv_ready.at(b, KT))
                for s in range(2):
                    i = dve.memset(dA[s][:, :, 0:1], 0.0)
                zero = o.mark(i)
                dve.wait_ge(sp_ready.sem, sp_ready.at(b, 1))
                dve.tensor_tensor(delta, sp_relu, sp_ln, ALU.add).then_inc(delta_ready.sem, 1)
                dve.wait_ge(delta_ready.sem, delta_ready.at(b, 1))
                o.mark(dve.tensor_tensor(du, delta, U, ALU.mult))
                o.wait()

                def flat(t):
                    return t.rearrange("p e l -> p (e l)")

                def inputs(n):
                    dve.wait_ge(b_ready.sem, b_ready.at(b, n + 1))
                    if n >= 2:
                        dve.wait_ge(scan_done.sem, scan_done.at(b, n - 1))
                    dve.tensor_tensor(dBu[n % 2], du, ps[:, 4 + n % 2, :].unsqueeze(1).to_broadcast([P, KT, L]),
                                      ALU.mult).then_inc(b_used.sem, 1)

                def scan(n):
                    dve.wait_ge(dA_ready.sem, dA_ready.at(b, n + 1))
                    dve.wait_ge(b_used.sem, b_used.at(b, n + 1))
                    if n >= 3:
                        dve.wait_ge(hc_used.sem, hc_used.at(b, n - 2))
                    dve.tensor_tensor_scan(flat(hs[n % 3]), flat(dA[n % 2]), flat(dBu[n % 2]), 0.0, ALU.mult,
                                           ALU.add).then_inc(scan_done.sem, 1)

                def outputs(n):
                    dve.wait_ge(c_ready.sem, c_ready.at(b, n + 1))
                    dve.wait_ge(scan_done.sem, scan_done.at(b, n + 1))
                    dve.tensor_tensor(hs[n % 3], hs[n % 3], ps[:, 6 + n % 2, :].unsqueeze(1).to_broadcast([P, KT, L]),
                                      ALU.mult).then_inc(hc_ready.sem, 1)

                inputs(0)
                for n in range(DS):
                    if n + 1 < DS:
                        inputs(n + 1)
                    scan(n)
                    if n >= 1:
                        outputs(n - 1)
                outputs(DS - 1)
                dve.wait_ge(hc_used.sem, hc_used.at(b, DS))
                dve.wait_ge(siluz_ready.sem, siluz_ready.at(b, LT))
                for e in range(KT):
                    m = o.mark(dve.scalar_tensor_tensor(out=yt[:, e], in0=U[:, e], scalar=vec("D", e), in1=ps[:, e, :],
                                                        op0=ALU.mult, op1=ALU.add))
                    if e:
                        o.wait(m - 1)
                        dve.tensor_tensor(yz[:, e - 1], yt[:, e - 1], siluz[:, e - 1], ALU.mult).then_inc(yz_ready.sem, 1)
                o.wait(m)
                dve.tensor_tensor(yz[:, KT - 1], yt[:, KT - 1], siluz[:, KT - 1], ALU.mult).then_inc(yz_ready.sem, 1)

                def add(bank, gate):
                    return o.mark(dve.scalar_tensor_tensor(
                        out=X[:, b * LT + bank - 4, :], in0=ps[:, bank, :], scalar=tg[:, gate:gate + 1],
                        in1=X[:, b * LT + bank - 4, :], op0=ALU.mult, op1=ALU.add))

                dve.wait_ge(yt_ready.sem, yt_ready.at(b, 1))
                for l in range(LT):
                    add(4 + l, 0)
                o.wait()
                ln_stats(b, 1)
                ln_coefs(b, 1)
                dve.wait_ge(ln_coef.sem, ln_coef.at(b, 2))
                for t in range(LT):
                    i = dve.tensor_scalar(xn[:, t], X[:, b * LT + t, :], mv[:, t, 0:1], rstd[:, t:t + 1], ALU.subtract,
                                          ALU.mult)
                o.mark(i)
                o.wait()
                o.mark(dve.tensor_scalar(gt, xn, TH_X, None, ALU.is_gt))
                o.wait()
                dve.scalar_tensor_tensor(out=tern, in0=xn, scalar=-TH_X, in1=gt, op0=ALU.is_lt,
                                         op1=ALU.subtract).then_inc(tern_ready.sem, 1)
                for t in range(LT):
                    dve.wait_ge(ffn_ready.sem, ffn_ready.at(b, t + 1))
                    add(4 + t, 1)
                o.wait()
                ln_stats(b, 2)
                ln_coefs(b, 2)
                for t in range(LT):
                    dve.wait_ge(xT_ready.sem, xT_ready.at(b, t + 1))
                    dve.tensor_copy(xnT[:, :, t * P:(t + 1) * P], ps[:, t, :].rearrange("p (k l) -> p k l", k=KT))\
                        .then_inc(xT_sb.sem, 1)
                for i8 in range(8):
                    dve.wait_ge(qc_ready.sem, qc_ready.at(b, i8 + 1))
                    dve.tensor_tensor(sq[:, i8], qk[:, i8], qk[:, i8], ALU.mult).then_inc(sq_ready.sem, 1)
                dve.wait_ge(std_ready.sem, std_ready.at(b, 1))
                dve.reciprocal(rrow[:, :], sdr[:, :]).then_inc(rrow_ready.sem, 1)
                for i8 in range(8):
                    dve.wait_ge(rb_ready.sem, rb_ready.at(b, i8 + 1))
                    bank = 6 + i8 % 2
                    if i8 < KT:
                        dve.scalar_tensor_tensor(out=qk[:, i8], in0=qk[:, i8], scalar=aff[:, 0:1], in1=ps[:, bank, :],
                                                 op0=ALU.mult, op1=ALU.mult).then_inc(rb_used.sem, 1)
                    else:
                        dve.scalar_tensor_tensor(out=qk[:, i8, 0:MAIN], in0=qk[:, i8, 0:MAIN], scalar=aff[:, 2:3],
                                                 in1=ps[:, bank, 0:MAIN], op0=ALU.mult, op1=ALU.mult)
                        dve.scalar_tensor_tensor(out=qk[:, i8, MAIN:L], in0=qk[:, i8, MAIN:L], scalar=aff[:, 4:5],
                                                 in1=ps[:, bank, MAIN:L], op0=ALU.mult, op1=ALU.mult)\
                            .then_inc(rb_used.sem, 1)

                def maxima(it):
                    s = it % 2
                    dve.wait_ge(s_ready.sem, s_ready.at(b, it + 1))
                    if it >= 2:
                        dve.wait_ge(p_raw.sem, p_raw.at(b, it - 1))
                    dve.tensor_reduce(nm[:, s, 0:2], ps[:, 2 * s:2 * s + 2, 0:MAIN], AX.X, ALU.max, negate=True)
                    dve.tensor_reduce(nm[:, s, 2:4], ps[:, 2 * s:2 * s + 2, MAIN:L], AX.X, ALU.max, negate=True)\
                        .then_inc(nm_ready.sem, 1)

                def normalise(it):
                    s = it % 2
                    dve.wait_ge(p_raw.sem, p_raw.at(b, it + 1))
                    o.mark(dve.reciprocal(escale[:, s, :], esum[:, s, :]))
                    o.wait()
                    for q in range(2):
                        dve.tensor_scalar(Pr[:, s, q, 0:MAIN], Pr[:, s, q, 0:MAIN], escale[:, s, q:q + 1], None, ALU.mult)
                    dve.tensor_tensor(Pr[:, s, :, MAIN:L], Pr[:, s, :, MAIN:L],
                                      escale[:, s, 2:4].unsqueeze(2).to_broadcast([P, 2, DCA]), ALU.mult)\
                        .then_inc(p_final.sem, 1)

                def heads_out(qp):
                    dve.wait_ge(pv_done.sem, pv_done.at(b, (qp + 1) * H))
                    for half in range(2):
                        dve.tensor_tensor(ctxnT[:, 2 * half:2 * half + 2, qp * 2 * P:(qp + 1) * 2 * P],
                                          ps[:, 6 + half, :].rearrange("p (k l) -> p k l", k=2),
                                          bvsum[:, 2 * half:2 * half + 2].unsqueeze(2).to_broadcast([P, 2, 2 * P]),
                                          ALU.add).then_inc(cT_sb.sem, 1)

                maxima(0)
                maxima(1)
                normalise(0)
                for it in range(NIT):
                    if it + 2 < NIT:
                        maxima(it + 2)
                    if it + 1 < NIT:
                        normalise(it + 1)
                    dve.wait_ge(t_ready.sem, t_ready.at(b, it + 1))
                    if it >= 2:
                        dve.wait_ge(pv_done.sem, pv_done.at(b, it - 1))
                    dve.tensor_copy(PT[:, it % 2, 0], ps[:, 4, :]).then_inc(pt_d.sem, 1)
                    if it == H:
                        heads_out(0)
                heads_out(1)
                for t in range(LT):
                    dve.wait_ge(o_ready.sem, o_ready.at(b, t + 1))
                    add(4 + t, 2)
                o.wait()
                dve.tensor_copy(std[:, 0:1], rstd[:, 0:1]).then_inc(batch_done.sem, 1)
            o.leave()

            dve.wait_ge(batch_done.sem, B + 1)
            dve.memset(zero_rows, 0.0).then_inc(zero_ready, 1)
            dve.tensor_copy(std[:, 0:1], rstd[:, 0:1]).then_inc(hT_sb.sem, 1)
            with dve.Fori(0, B) as b:
                for t in range(LT):
                    i = dve.bn_stats(st6[:, t, :], X[:, b * LT + t, :])
                i.then_inc(prep_order, 1)
                dve.wait_ge(prep_order, 2 * b + 1)
                settle()
                for t in range(LT):
                    i = dve.bn_aggr(mv[:, t, :], st6[:, t, :])
                i.then_inc(ln4_mv.sem, 1)
                dve.wait_ge(ln4_std.sem, ln4_std.at(b, 1))
                dve.reciprocal(rstd[:, :], std[:, :]).then_inc(prep_order, 1)
                dve.wait_ge(prep_order, 2 * b + 2)
                dve.scalar_tensor_tensor(out=nmr[:, :], in0=mv[:, :, 0], scalar=-1.0, in1=rstd[:, :], op0=ALU.mult,
                                         op1=ALU.mult).then_inc(ln4_coef.sem, 1)
                for t in range(LT):
                    dve.wait_ge(hT_ready.sem, hT_ready.at(b, t + 1))
                    dve.tensor_copy(HT[:, :, bass.ds(b * L + t * P, P)], ps[:, t, :].rearrange("p (k l) -> p k l", k=KT))\
                        .then_inc(hT_sb.sem, 1)

            def chain(ins):
                o.mark(ins)
                o.wait()

            dve.wait_ge(sc_ready, 1)
            for t in range(NT):
                i = dve.max(top[:, t, :], SC[:, t, :])
            chain(i)
            for t in range(NT):
                i = dve.max_index(topi[:, t, :], top[:, t, :], SC[:, t, :])
            chain(i)
            o.mark(dve.tensor_reduce(den[:, :], top[:, :, 0:TOPK], AX.X, ALU.add))
            chain(dve.tensor_copy(topf[:, :, :], topi[:, :, :]))
            chain(dve.tensor_scalar(den[:, :], den[:, :], 1e-20, None, ALU.add))
            chain(dve.reciprocal(den[:, :], den[:, :]))
            chain(dve.tensor_scalar(den[:, :], den[:, :], tg[:, 3:4], None, ALU.mult))
            dve.tensor_tensor(pairs[:, :, :, 1].bitcast(F32), top[:, :, 0:TOPK],
                              den[:, :].unsqueeze(2).to_broadcast([P, NT, TOPK]), ALU.mult)
            dve.tensor_copy(pairs[:, :, :, 0], tok_i[:, :].unsqueeze(2).to_broadcast([P, NT, TOPK]))
            for j in range(TOPK):
                i = dve.tensor_tensor(pick[:, j], iota_f[:, :].unsqueeze(1).to_broadcast([P, NT, NE]),
                                      topf[:, :, j:j + 1].to_broadcast([P, NT, NE]), ALU.is_equal)
            chain(i)
            chain(dve.tensor_tensor(msum, pick[:, 0], pick[:, 1], ALU.add))
            for j in range(2, TOPK):
                chain(dve.tensor_tensor(msum, msum, pick[:, j], ALU.add))
            dve.tensor_copy(Mb[:, :], msum.rearrange("p t e -> p (t e)")).then_inc(mask_ready, 1)
            dve.wait_ge(prefix_ready, 1)
            chain(dve.tensor_copy(tot, ps[:, 6, :].rearrange("p (t e) -> p e t", e=NE)))
            chain(dve.tensor_tensor_scan(cum.rearrange("p e t -> p (e t)"), keep[:, :, :].rearrange("p e t -> p (e t)"),
                                         tot.rearrange("p e t -> p (e t)"), 0.0, ALU.mult, ALU.add))
            o.mark(dve.tensor_scalar(nb_i[:, :], cum[:, :, NT - 1], float(BLK - 1), None, ALU.add))
            chain(dve.tensor_tensor(tot, cum, tot, ALU.subtract))
            chain(dve.tensor_scalar(nb_i[:, :], nb_i[:, :], BLK.bit_length() - 1, None, ALU.logical_shift_right))
            chain(dve.tensor_copy(nb_f[:, :], nb_i[:, :]))
            chain(dve.tensor_tensor_scan(end_b[:, :], ones_e[:, :], nb_f[:, :], 0.0, ALU.mult, ALU.add))
            chain(dve.tensor_tensor(start_b[:, :], end_b[:, :], nb_f[:, :], ALU.subtract))
            chain(dve.tensor_scalar(start_b[:, :], start_b[:, :], float(BLK), None, ALU.mult))
            chain(dve.tensor_tensor(slot, ps[:, 5, :].rearrange("p (t e) -> p t e", e=NE), tot.rearrange("p e t -> p t e"),
                                    ALU.add))
            chain(dve.tensor_tensor(slot, slot, start_b[:, :].unsqueeze(1).to_broadcast([P, NT, NE]), ALU.add))
            for j in range(TOPK):
                chain(dve.tensor_tensor(tmp, pick[:, j], slot, ALU.mult))
                chain(dve.tensor_reduce(slots_f[:, j, :], tmp, AX.X, ALU.add))
            dve.tensor_copy(slots[:, :, :], slots_f[:, :, :]).then_inc(slots_ready, 1)
            chain(dve.tensor_tensor(le[:, :, :], end_b[0:1, :].unsqueeze(1).to_broadcast([1, NBLK, NE]),
                                    blk_f[:, :].unsqueeze(2).to_broadcast([1, NBLK, NE]), ALU.is_le))
            chain(dve.tensor_reduce(expert_f[:, :], le[:, :, :], AX.X, ALU.add))
            dve.tensor_scalar(expert_i[:, :], expert_f[:, :], float(NE - 1), None, ALU.min).then_inc(expert_ready, 1)

            with dve.Fori(0, B) as c:
                for m in range(3):
                    dve.wait_ge(sil_ready.sem, sil_ready.at(c, m + 1))
                    dve.tensor_tensor(aS[:, m], sil[:, m], ps[:, 2 * m + 1, :], ALU.mult).then_inc(aS_ready.sem, 1)
                for t in range(LT):
                    dve.wait_ge(shy_ready.sem, shy_ready.at(c, t + 1))
                    dve.scalar_tensor_tensor(out=X[:, c * LT + t, :], in0=ps[:, 6 + t % 2, :], scalar=tg[:, 3:4],
                                             in1=X[:, c * LT + t, :], op0=ALU.mult, op1=ALU.add).then_inc(shx_done.sem, 1)
            dve.wait_ge(meta_loaded, 16)

            def turned(s, u):
                if isinstance(s, int) and s >= NBLK:
                    return
                dve.wait_ge(gt_ready, s + 1)
                ge(dve, gu_ready, 2 * (s - 1))
                dve.tensor_copy(GT[:, u, 0:2], ps[:, 0, :].rearrange("p (k l) -> p k l", k=2)).then_inc(gt_d, 1)

            def block_dve(s, r, u):
                if not isinstance(s, int) or s >= 1:
                    dve.wait_ge(at_ready, s)
                    ge(dve, y_ready, 2 * (s - 1))
                    dve.tensor_copy(aT[:, :, :], ps[0:FH, 4, :].rearrange("p (f l) -> p f l", f=2)).then_inc(at_sb, 1)
                for q in range(2):
                    dve.wait_ge(silu_done, 2 * s + q + 1)
                    ge(dve, at_ready, s)
                    dve.tensor_tensor(act_m[:, q, :], act_s[:, q, :], ps[:, 2 + q, FE:2 * FE], ALU.mult)\
                        .then_inc(act_done, 1)
                turned(s + 1, 1 - u)
                scaled(s - 1, 1 - u)

            def scaled(s, u):
                if isinstance(s, int) and s < 0:
                    return
                dve.wait_ge(y_ready, 2 * s + 1)
                ge(dve, added, 32 * (s - 1))
                dve.tensor_scalar(Yb[:, u, 0], ps[:, 5, :], meta[:, bass.ds(2 * s, 1), 1].bitcast(F32), None, ALU.mult)\
                    .then_inc(y_d, 1)

            turned(0, 0)
            steps(dve, block_dve, 0, NBLK - 1)
            dve.wait_ge(at_ready, NBLK)
            dve.tensor_copy(aT[:, :, :], ps[0:FH, 4, :].rearrange("p (f l) -> p f l", f=2)).then_inc(at_sb, 1)
            scaled(NBLK - 1, 1)


_INS = ["x", "ctxT", "vecs", "w_in", "w_xp", "w_dt", "ffn_w", "ffn_r", "w_q", "w_k", "w_v", "w_kd", "w_vd", "w_o", "b_o", "w_g",
        "w_sh", "w_sd", "w_gu", "w_dn"]
_OUTS = [((B * L + BLK, DM), "float32")]


def _by_row(w, p=P):
    k = w.shape[0] // p
    return w.reshape(k, p, -1).transpose(1, 0, 2)


def lay_out(a):
    g = {}
    g["x"] = a["x"].reshape(B * L, DM)
    g["ctxT"] = a["ctx_1024"].transpose(0, 2, 1).reshape(B, KC, P, L).transpose(0, 2, 1, 3)
    g["w_in"] = _by_row(a["L0_xattn_in_proj_w"].T)
    g["w_xp"] = _by_row(a["L0_xattn_x_proj_w"].T)
    g["w_dt"] = a["L0_xattn_dt_proj_w"].T
    g["ffn_w"] = _by_row(a["L0_ffn_weight"].T)
    g["ffn_r"] = _by_row(a["L0_ffn_rram_variation"].T)
    g["w_q"] = _by_row(a["L1_xattn_Wq"])
    kv = np.concatenate([a["L1_xattn_Wk"], a["L1_xattn_Wv"]], 1).reshape(DC, H, 2, HD)
    bkv = np.concatenate([a["L1_xattn_bk"], a["L1_xattn_bv"]]).reshape(H, 2, HD)
    g["w_k"] = _by_row(kv[:, :, 0].reshape(DC, DM))
    g["w_v"] = _by_row(kv[:, :, 1].reshape(DC, DM))
    g["w_kd"] = _by_row(a["L1_xattn_Wkv_dca"][:, :DM])
    g["w_vd"] = _by_row(a["L1_xattn_Wkv_dca"][:, DM:])
    g["w_o"] = _by_row(a["L1_xattn_Wo"])
    g["b_o"] = a["L1_xattn_bo"].reshape(1, DM)
    g["w_g"] = _by_row(a["L1_ffn_gate_w"])
    g["w_sh"] = _by_row(np.concatenate([a["L1_ffn_sg"], a["L1_ffn_su"]], 1))
    g["w_sd"] = _by_row(a["L1_ffn_sd"])
    gu = np.concatenate([a["L1_ffn_wg"], a["L1_ffn_wu"]], 2)
    g["w_gu"] = gu.reshape(NE, KT, P, 2 * FE).transpose(0, 2, 1, 3)
    g["w_dn"] = a["L1_ffn_wd"].reshape(NE, 2, FH, DM).transpose(0, 2, 1, 3)
    vecs = np.empty((P, NVEC), np.float32)

    def put(name, v):
        vecs[:, VEC[name][0]:VEC[name][1]] = v

    put("conv_w", _by_row(a["L0_xattn_conv_w"]).reshape(P, -1))
    put("conv_b", a["L0_xattn_conv_b"].reshape(KT, P).T)
    put("dt_b", a["L0_xattn_dt_proj_b"].reshape(KT, P).T)
    put("A_log", _by_row(a["L0_xattn_A_log"]).reshape(P, -1))
    put("D", a["L0_xattn_D"].reshape(KT, P).T)
    put("bq", a["L1_xattn_bq"].reshape(KT, P).T)
    put("bk", bkv[:, 0].reshape(KT, P).T)
    put("bkd", a["L1_xattn_bkv_dca"][:DM].reshape(KT, P).T)
    put("bv", bkv[:, 1].reshape(KT, P).T)
    put("bvd", a["L1_xattn_bkv_dca"][DM:].reshape(KT, P).T)
    for name, src in (("qw", "qn_w"), ("qb", "qn_b"), ("kw", "kn_w"), ("kb", "kn_b"), ("kdw", "kn_dca_w"), ("kdb", "kn_dca_b")):
        put(name, np.tile(a["L1_xattn_" + src], HPT).reshape(P, 1))
    for i, (src, j) in enumerate((("g_xattn", 0), ("g_ffn", 0), ("g_xattn", 1), ("g_ffn", 1))):
        vecs[:, VEC["gates"][0] + i] = a[src][j]
    g["vecs"] = vecs
    return g


def kernel(**inputs):
    import concourse.bacc as _bacc
    from concourse.bass_utils import run_bass_kernel_spmd as _run

    nc = _bacc.Bacc("TRN2", target_bir_lowering=False, num_devices=1)
    laid = lay_out({k: np.asarray(v) for k, v in inputs.items()})
    arrays, args = {}, []
    for name in _INS:
        a = np.ascontiguousarray(laid[name])
        arrays[f"in_{name}"] = a
        args.append(nc.dram_tensor(f"in_{name}", a.shape, mybir.dt.from_np(a.dtype), kind="ExternalInput").ap())
    for i, (shape, dtype) in enumerate(_OUTS):
        args.append(nc.dram_tensor(f"out_{i}", shape, mybir.dt.from_np(np.dtype(dtype)), kind="ExternalOutput").ap())
    program(nc, *args)
    r = _run(nc, [arrays], core_ids=[0])
    return r.results[0]["out_0"][:B * L].reshape(B, L, DM)
```

```python
import numpy as np
import concourse.bass as bass
from concourse import mybir

F32 = mybir.dt.float32
F32R = mybir.dt.float32r
BF16 = mybir.dt.bfloat16
I32 = mybir.dt.int32
U32 = mybir.dt.uint32
ALU = mybir.AluOpType
ACT = mybir.ActivationFunctionType
AX = mybir.AxisListType

P = 128
B, L, DM = 4, 512, 512
DC = 256
KC = DC // P
KT = DM // P
LT = L // P
DS, DR, TAPS = 16, 16, 4
H, HD = 16, 32
HPT = P // HD
DCA = 16
MAIN = L - DCA
LN_EPS, QK_EPS = 1e-5, 1e-6
QK_SCALE = HD ** -0.5
TH_X, TH_W, SC_X, SC_W = 0.33, 0.2, 0.5, 0.6

NE, TOPK, FE, FS = 32, 6, 192, 384
FH = FE // 2
NT = B * LT
BLK = 256
NBLK = 80
assert (NT * P * TOPK + NE * (BLK - 1)) // BLK <= NBLK and NBLK % 2 == 0
NSLOT = NBLK * BLK

VEC = {}
_at = 0
for _name, _n in (("conv_w", KT * TAPS), ("conv_b", KT), ("dt_b", KT), ("A_log", KT * DS), ("D", KT),
                  ("bq", KT), ("bk", KT), ("bkd", KT), ("bv", KT), ("bvd", KT),
                  ("qw", 1), ("qb", 1), ("kw", 1), ("kb", 1), ("kdw", 1), ("kdb", 1), ("gates", 4)):
    VEC[_name] = (_at, _at + _n)
    _at += _n
NVEC = _at


K_THEN_Q = [4, 5, 6, 7, 0, 1, 2, 3]


class Signal:

    def __init__(self, sem, per, first=0):
        self.sem, self.per, self.first = sem, per, first

    def at(self, b, n):
        return b * self.per + (self.first + n)


class Order:

    def __init__(self, eng, sem, per):
        self.eng, self.sem, self.per = eng, sem, per
        self.first = self.n = 0
        self.b = None

    def enter(self, b):
        self.first, self.n, self.b = self.n, 0, b

    def leave(self):
        assert self.n == self.per, (self.sem, self.n, self.per)
        self.first, self.n, self.b = self.first + self.per * B, 0, None

    def mark(self, ins):
        ins.then_inc(self.sem, 1)
        self.n += 1
        return self.n

    def wait(self, n=None):
        n = self.n if n is None else n
        value = self.first + n if self.b is None else self.b * self.per + (self.first + n)
        self.eng.wait_ge(self.sem, value)

DVE_STEPS = 74
ACT_STEPS = 6


def program(nc, x, ctxT, vecs, w_in, w_xp, w_dt, ffn_w, ffn_r, w_q, w_k, w_v, w_kd, w_vd, w_o, b_o, w_g, w_sh, w_sd,
            w_gu, w_dn, out):
    def sb(name, shape, dt=F32):
        return nc.alloc_sbuf_tensor(name, shape, dt)

    def sem(name):
        return nc.alloc_semaphore(name)

    X = sb("X", [P, B * LT, DM])
    ps = nc.alloc_psum_tensor("ps", [P, 8, 512], F32)
    ctx = sb("ctx", [P, KC, L])
    V_ = sb("vecs_sb", [P, NVEC])
    region = sb("region", [P, 12288])

    def carve(at, *shape):
        n = int(np.prod(shape))
        v = region[:, at:at + n]
        if len(shape) == 2:
            v = v.rearrange("p (a c) -> p a c", c=shape[1])
        elif len(shape) == 3:
            v = v.rearrange("p (a t c) -> p a t c", t=shape[1], c=shape[2])
        return v

    Win, Wk, Wv, Wkd, Wvd = (carve(1024 * i, KC, DM) for i in range(5))
    Wq, Wo = carve(5120, KT, DM), carve(7168, KT, DM)
    W3 = region[:, 9216:12288].bitcast(BF16).rearrange("p (a t c) -> p a t c", a=3, t=KT)
    wgu = carve(0, 2, KT, 2 * FE)
    wdn = carve(3072, 2, 2, DM)
    G = carve(5120, 2, 2, DM)
    Yb = carve(9216, 2, 2, DM)
    Wxp = sb("Wxp", [P, KT, DR + 2 * DS])
    Wdt = sb("Wdt", [DR, DM])
    bo = sb("bo", [1, DM])
    Wg = sb("Wg", [P, KT, NE])
    ident = sb("ident", [P, P])
    identb = sb("identb", [P, P], BF16)
    ones1 = sb("ones1", [1, P])
    ctx_credit = sb("ctx_credit", [1, 1])
    negA = sb("negA", [P, KT * DS])
    tg = sb("tg", [P, 4])
    eps = sb("eps", [P, 2])
    headmean = sb("headmean", [P, P])
    headvar = sb("headvar", [P, 8, 32])
    headrow = sb("headrow", [32, 8, P], F32R)
    bvsum = sb("bvsum", [P, KT])
    qkbias = sb("qkbias", [P, 3 * KT])
    aff = sb("aff", [P, 6])
    wsum = sb("wsum", [P, KT * H])
    st6 = sb("st6", [P, LT, 6])
    mv = sb("mv", [P, LT, 2])
    std = sb("std", [P, LT])
    rstd = sb("rstd", [P, LT])
    nmr = sb("nmr", [P, LT])
    XD = sb("XD", [DR + 2 * DS, L])
    XDr = sb("XDr", [DR + 2 * DS, 2, L], F32R)
    Cr = sb("Cr", [P, 2, L])
    identr = sb("identr", [P, P], F32R)
    sdr = sb("sdr", [32, L])
    rrow = sb("rrow", [32, L])
    nm = sb("nm", [P, 2, 4])
    esum = sb("prob_sums", [P, 2, 4])
    escale = sb("prob_scale", [P, 2, 4])
    arena_offset = nc.sbuf_base
    arena = sb("arena", [P, 11, KT, L])
    arena_bytes = 11 * KT * L * 4
    assert nc.sbuf_base == arena_offset + arena_bytes
    siluz, U, delta, du = (arena[:, i] for i in range(4))
    conv = du
    xpad = arena[:, 4:6].rearrange("p a t l -> p (a t l)")[:, 0:KT * 516].rearrange("p (e l) -> p e l", l=516)
    dA = [arena[:, 4], arena[:, 5]]
    dBu = [arena[:, 6], arena[:, 7]]
    hs = [arena[:, 8], arena[:, 9], arena[:, 10]]
    sp_abs, sp_exp, sp_relu, sp_ln = dBu[0], dBu[1], hs[0], hs[1]
    yt, yz = dBu[0], dBu[1]
    xn, gt = arena[:, 0], arena[:, 1]
    tern = arena[:, 2].bitcast(BF16)[:, 0:2].rearrange("p a (t l) -> p (a t) l", l=L)
    ternT = arena[:, 3].bitcast(BF16)[:, 0:2].rearrange("p a (t l) -> p (a t) l", l=L)
    xnT = arena[:, 1]
    qk = arena[:, 2:4].rearrange("p a t l -> p (a t) l")
    sq = arena[:, 4:6].rearrange("p a t l -> p (a t) l")
    Vn = arena[:, 6]
    Pr = arena[:, 7].rearrange("p (s q) l -> p s q l", s=2)
    PT = arena[:, 8].rearrange("p (s q) l -> p s q l", s=2)
    ctxnT = arena[:, 10]
    headrow_f = arena[0:32, 10].rearrange("r t l -> r (t l)")[:, 0:8 * P].rearrange("r (i c) -> r i c", i=8)
    rrow_parts = nc.alloc_sbuf_tensor_at("rrow_parts", [32, 2, L], F32R, offset=arena_offset + 9 * KT * L * 4)
    wtmp = [arena[:, i] for i in range(4)]

    HT = arena[:, 0:4].rearrange("p k t l -> p k (t l)")
    hn = arena[:, 4]
    Wsh = arena[:, 5:7].rearrange("p a t l -> p (a t l)")[:, 0:KT * 2 * FS].rearrange("p (k f) -> p k f", k=KT)
    Wsd = arena[:, 7, 0:3]
    sil, aS = arena[:, 8, 0:3], arena[:, 9, 0:3]
    pick = region[:, 0:TOPK * NT * NE].rearrange("p (j t e) -> p j t e", t=NT, e=NE)
    SC = arena[:, 10, 0].rearrange("p (t e) -> p t e", e=NE)
    msum = arena[:, 10, 1].rearrange("p (t e) -> p t e", e=NE)
    slot = arena[:, 10, 2].rearrange("p (t e) -> p t e", e=NE)
    tmp = arena[:, 10, 3].rearrange("p (t e) -> p t e", e=NE)
    tot = arena[:, 9, 3].rearrange("p (e t) -> p e t", t=NT)
    cum = arena[:, 8, 3].rearrange("p (e t) -> p e t", t=NT)
    spare = arena[:, 5:7].rearrange("p a t l -> p (a t l)")[:, KT * 2 * FS:]
    Mb = spare[:, 0:NT * NE // 2].bitcast(BF16)
    top, topi, topf = (spare[:, n:n + NT * 8].rearrange("p (t e) -> p t e", e=8) for n in (512, 640, 768))
    topi = topi.bitcast(U32)
    lists = arena[:, 7, 3]
    slots_f = lists[:, 0:TOPK * NT].rearrange("p (j t) -> p j t", t=NT)
    slots = lists[:, 128:128 + TOPK * NT].rearrange("p (j t) -> p j t", t=NT).bitcast(U32)
    pairs = lists[:, 256:256 + 2 * TOPK * NT].rearrange("p (t j c) -> p t j c", j=TOPK, c=2).bitcast(I32)
    den = sb("den", [P, NT])
    keep = sb("keep", [P, NE, NT])
    iota_i = sb("iota_i", [P, NE], I32)
    iota_f = sb("iota_f", [P, NE])
    blk_i = sb("blk_i", [1, NBLK], I32)
    blk_f = sb("blk_f", [1, NBLK])
    tri_f = sb("tri_f", [P, P])
    tri = sb("tri", [P, P], BF16)
    onesb = sb("onesb", [P, P], BF16)
    nb_f = sb("nb_f", [P, NE])
    nb_i = sb("nb_i", [P, NE], I32)
    end_b = sb("end_b", [P, NE])
    start_b = sb("start_b", [P, NE])
    ones_e = sb("ones_e", [P, NE])
    tok_i = sb("tok_i", [P, NT], I32)
    le = region[0:1, 0:NBLK * NE].rearrange("p (n e) -> p n e", e=NE)
    expert_f = sb("expert_f", [1, NBLK])
    expert_i = sb("expert_i", [1, NBLK], I32)
    meta = sb("meta", [P, NSLOT // P, 2], I32)
    gidx = sb("gidx", [P, 2, 2, 2], I32)
    aidx = sb("aidx", [P, 2, 2], I32)
    arena_flat = arena[:, :, :, :].rearrange("p s t l -> p (s t l)")
    act_s = arena_flat[:, 0:2 * FE].rearrange("p (q f) -> p q f", q=2)
    act_m = arena_flat[:, 512:512 + 2 * FE].rearrange("p (q f) -> p q f", q=2)
    parts_at = arena_offset + 4096

    def two_parts(name, rows, buffers, tiles, n):
        nonlocal parts_at
        t = nc.alloc_sbuf_tensor_at(name, [rows, buffers, 2, tiles, n], F32R, offset=parts_at)
        parts_at += buffers * 2 * tiles * n * 4
        assert parts_at <= arena_offset + arena_bytes
        return t

    GTp = two_parts("GTp", P, 1, KT, BLK)
    wgup = two_parts("wgup", P, 2, KT, 2 * FE)
    wdnp = two_parts("wdnp", FH, 2, 2, DM)
    aTp = two_parts("aTp", FH, 1, 2, BLK)
    Hd = nc.dram_tensor("Hd", [NT * P + BLK, DM], F32, kind="Internal").ap()
    listd = nc.dram_tensor("listd", [NSLOT, 2], I32, kind="Internal").ap()

    ln4_mv, ln4_std, ln4_coef = (Signal(sem(n), 1) for n in ("ln4_mv", "ln4_std", "ln4_coef"))
    hn_ready, hT_ready = (Signal(sem(n), LT) for n in ("hn_ready", "hT_ready"))
    hT_sb = Signal(sem("hT_sb"), LT, 1)
    h_stored = Signal(sem("h_stored"), 16 * LT, 16)
    setup_iota, zero_ready, fill_ready, list_filled = (sem(n) for n in ("setup_iota", "zero_ready", "fill_ready", "list_filled"))
    logits_ready, sc_ready, mask_ready, prefix_ready, slots_ready, scattered, meta_loaded, expert_ready = (
        sem(n) for n in ("logits_ready", "sc_ready", "mask_ready", "prefix_ready", "slots_ready", "scattered",
                         "meta_loaded", "expert_ready"))
    sh_loaded = sem("sh_loaded")
    shg_ready, sil_ready, aS_ready = (Signal(sem(n), 3) for n in ("shg_ready", "sil_ready", "aS_ready"))
    shy_ready, shx_done = (Signal(sem(n), LT) for n in ("shy_ready", "shx_done"))
    out_stored = sem("out_stored")
    wgu_loaded = [sem(f"wgu_loaded{u}") for u in range(2)]
    wdn_loaded = [sem(f"wdn_loaded{u}") for u in range(2)]
    gathered = [sem(f"gathered{u}") for u in range(2)]
    gt_ready, gt_hi, gt_lo, gu_ready, silu_done, act_done, at_ready, at_hi, at_lo, y_ready, y_a, y_d, gidx_ready = (
        sem(n) for n in ("gt_ready", "gt_hi", "gt_lo", "gu_ready", "silu_done", "act_done", "at_ready", "at_hi", "at_lo", "y_ready",
                         "y_a", "y_d", "gidx_ready"))
    wgu_hi, wgu_lo, wdn_hi, wdn_lo = (sem(n) for n in ("wgu_hi", "wgu_lo", "wdn_hi", "wdn_lo"))
    added = sem("added")
    prep_order = sem("prep_order")
    aidx_ready = sem("aidx_ready")
    zero_rows = Yb[:, 1]

    def ds2(s):
        return bass.ds(2 * s, 2)

    def ds1(s):
        return bass.ds(s, 1)

    def ge(eng, s, value):
        if not (isinstance(value, int) and value <= 0):
            eng.wait_ge(s, value)

    def steps(eng, step, first, last):
        lo, hi = first + first % 2, last + 1 - (last + 1) % 2
        lo += 4
        hi -= 2
        for s in range(first, lo):
            step(s, s // 2, s % 2)
        with eng.Fori(lo // 2, hi // 2) as r:
            for u in range(2):
                step(2 * r + u, r, u)
        for s in range(hi, last + 1):
            step(s, s // 2, s % 2)

    setup_pool = sem("setup_pool")
    setup_act = sem("setup_act")
    setup_pe = sem("setup_pe")
    setup_dve = sem("setup_dve")
    batch_done = Signal(sem("batch_done"), 1, 1)
    ctx_loaded = Signal(sem("ctx_loaded"), 16)
    ctx_free = Signal(sem("ctx_free"), 1, 1)
    ln_mv, ln_std, ln_coef = (Signal(sem(n), 3) for n in ("ln_mv", "ln_std", "ln_coef"))
    xi_ready, xpad_ready, conv_ready, u_ready = (Signal(sem(n), KT) for n in ("xi_ready", "xpad_ready", "conv_ready", "u_ready"))
    siluz_ready = Signal(sem("siluz_ready"), LT)
    xd_ready, xd_sb, xdr_ready, dt_ready, sp_ready, delta_ready = (Signal(sem(n), 1) for n in ("xd_ready", "xd_sb", "xdr_ready", "dt_ready", "sp_ready", "delta_ready"))
    dA_ready, b_ready, c_ready, b_used, scan_done, c_sb, hc_ready, hc_used = (
        Signal(sem(n), DS) for n in ("dA_ready", "b_ready", "c_ready", "b_used", "scan_done", "c_sb", "hc_ready", "hc_used"))
    yz_ready = Signal(sem("yz_ready"), KT)
    yt_ready = Signal(sem("yt_ready"), 1)
    tern_ready = Signal(sem("tern_ready"), 1)
    ternT_ready, ternT_sb, ffn_ready = (Signal(sem(n), LT) for n in ("ternT_ready", "ternT_sb", "ffn_ready"))
    xn_ready, xT_ready, xT_sb = (Signal(sem(n), LT) for n in ("xn_ready", "xT_ready", "xT_sb"))
    proj_ready, qc_ready, sq_ready, rb_ready, rb_used, qk_final = (
        Signal(sem(n), 8) for n in ("proj_ready", "qc_ready", "sq_ready", "rb_ready", "rb_used", "qk_final"))
    var_ready, std_ready, rrow_ready, v_ready, v_sb = (Signal(sem(n), 1) for n in ("var_ready", "std_ready", "rrow_ready", "v_ready", "v_sb"))
    NIT = 2 * H
    s_ready, nm_ready, p_raw, p_final, t_ready, pt_d, pt_a, pv_done = (
        Signal(sem(n), NIT) for n in ("s_ready", "nm_ready", "p_raw", "p_final", "t_ready", "pt_d", "pt_a", "pv_done"))
    cT_sb, o_ready = (Signal(sem(n), LT) for n in ("cT_sb", "o_ready"))
    dve_order, act_order = sem("dve_order"), sem("act_order")
    act_passed, dve_passed, pool_passed = sem("act_passed"), sem("dve_passed"), sem("pool_passed")

    def vec(name, i=0, n=1):
        return V_[:, VEC[name][0] + i:VEC[name][0] + i + n]

    vecs_loaded, ffn_loaded, wqk_loaded, loaded = (sem(n) for n in ("vecs_loaded", "ffn_loaded", "wqk_loaded", "loaded"))
    first_loads = [
        (V_[:, :], vecs, vecs_loaded), (wtmp[0], ffn_w, ffn_loaded), (wtmp[1], ffn_r, ffn_loaded),
        (Wq[:, :, :], w_q, wqk_loaded), (Wk[:, :, :], w_k, wqk_loaded), (Wkd[:, :, :], w_kd, wqk_loaded)]
    loads = [
        (Win[:, :, :], w_in), (Wxp[:, :, :], w_xp), (Wdt[:, :], w_dt),
        (X[:, 0:LT, :], x[0:L, :].rearrange("(t p) d -> p t d", p=P)),
        (X[:, LT:, :], x[L:, :].rearrange("(t p) d -> p t d", p=P)),
        (Wv[:, :, :], w_v), (Wvd[:, :, :], w_vd), (Wo[:, :, :], w_o), (bo[:, :], b_o), (Wg[:, :, :], w_g),
    ]

    with nc.Block() as block:
        @block.sync
        def _(sp):
            for dst, src, done in first_loads:
                sp.dma_start(dst, src).then_inc(done, 16)
            for dst, src in loads:
                sp.dma_start(dst, src).then_inc(loaded, 16)
            with sp.Fori(0, B) as b:
                sp.wait_ge(ctx_free.sem, ctx_free.at(b, 0))
                sp.dma_start(ctx[:, :, :], ctxT[b]).then_inc(ctx_loaded.sem, 16)
            sp.wait_ge(fill_ready, 1)
            sp.dma_start(listd.rearrange("(p n) c -> p n c", p=P), meta[:, :, :]).then_inc(list_filled, 16)
            sp.wait_ge(batch_done.sem, B + 1)
            sp.dma_start(Wsh, w_sh).then_inc(sh_loaded, 16)
            sp.dma_start(Wsd, w_sd).then_inc(sh_loaded, 16)
            sp.wait_ge(zero_ready, 1)
            sp.dma_start(Hd[NT * P:NT * P + BLK, :].rearrange("(a p) d -> p a d", p=P), zero_rows).then_inc(h_stored.sem, 16)
            sp.dma_start(out[NT * P:NT * P + BLK, :].rearrange("(a p) d -> p a d", p=P), zero_rows).then_inc(out_stored, 16)
            with sp.Fori(0, B) as b:
                for t in range(LT):
                    sp.wait_ge(hn_ready.sem, hn_ready.at(b, t + 1))
                    sp.dma_start(Hd.rearrange("(t p) d -> t p d", p=P)[b * LT + t], hn[:, t]).then_inc(h_stored.sem, 16)
            sp.wait_ge(scattered, 16 * NT * TOPK)
            sp.dma_start(meta[:, :, :], listd.rearrange("(n p) c -> p n c", p=P), allow_slow_non_contiguous=True)\
                .then_inc(meta_loaded, 16)
            with sp.Fori(0, B) as b:
                for t in range(LT):
                    sp.wait_ge(shx_done.sem, shx_done.at(b, t + 1))
                    sp.dma_start(out[0:NT * P, :].rearrange("(t p) d -> t p d", p=P)[b * LT + t], X[:, b * LT + t, :])\
                        .then_inc(out_stored, 16)
            sp.wait_ge(expert_ready, 1)

            def load_weights(s, r, u):
                e = sp.value_load(expert_i[0:1, ds1(s)], min_val=0, max_val=NE - 1)
                ge(sp, wgu_lo, s - 1)
                sp.dma_start(wgu[:, u], w_gu[e]).then_inc(wgu_loaded[u], 16)
                ge(sp, wdn_lo, s - 1)
                sp.dma_start(wdn[0:FH, u], w_dn[e]).then_inc(wdn_loaded[u], 16)

            steps(sp, load_weights, 0, NBLK - 1)
            sp.wait_ge(added, 16 * 2 * NBLK)

        @block.gpsimd
        def _(pool):
            pool.memset(ident[:, :], 0.0).then_inc(setup_pool, 1)
            pool.memset(ones1[:, :], 1.0)
            pool.memset(eps[:, 0:1], LN_EPS)
            pool.memset(eps[:, 1:2], QK_EPS)
            pool.memset(headrow_f, 0.0).then_inc(setup_pool, 1)
            pool.wait_ge(setup_pool, 2)
            pool.affine_select(out=ident[:, :], in_=ident[:, :], compare_op=ALU.not_equal, fill=1.0, base=0,
                               pattern=[[-1, P]], channel_multiplier=1)
            hr = headrow_f.rearrange("r i (j c) -> r i j c", c=HD)
            pool.affine_select(out=hr, in_=hr, compare_op=ALU.not_equal, fill=1.0, base=0,
                               pattern=[[-HPT, 8], [-1, HPT], [0, HD]], channel_multiplier=1).then_inc(setup_pool, 1)
            pool.wait_ge(setup_pool, 3)
            pool.tensor_copy(identr[:, :], ident[:, :])
            pool.tensor_copy(headrow[:, :, :], headrow_f)
            pool.tensor_copy(identb[:, :], ident[:, :]).then_inc(setup_pool, 1)
            pool.memset(ctx_credit[:, :], 0.0).then_inc(ctx_free.sem, 1)
            pool.iota(iota_i[:, :], pattern=[[1, NE]], base=0, channel_multiplier=0)
            pool.iota(blk_i[:, :], pattern=[[1, NBLK]], base=0, channel_multiplier=0)
            pool.iota(tok_i[:, :], pattern=[[P, NT]], base=0, channel_multiplier=1)
            pool.iota(meta[:, :, 0], pattern=[[1, NSLOT // P]], base=0, channel_multiplier=NSLOT // P)
            pool.memset(meta[:, :, 1], 0)
            pool.memset(onesb[:, :], 1.0)
            pool.memset(ones_e[:, :], 1.0)
            pool.memset(keep[:, :, :], 1.0)
            pool.memset(tri_f[:, :], 1.0).then_inc(setup_iota, 1)
            pool.wait_ge(setup_iota, 1)
            pool.memset(keep[:, :, 0:1], 0.0)
            pool.affine_select(out=tri_f[:, :], in_=tri_f[:, :], compare_op=ALU.is_gt, fill=0.0, base=0,
                               pattern=[[1, P]], channel_multiplier=-1).then_inc(setup_iota, 1)
            with pool.Fori(0, B) as b:
                for n in range(DS):
                    pool.wait_ge(c_sb.sem, c_sb.at(b, n + 1))
                    pool.wait_ge(scan_done.sem, scan_done.at(b, n + 1))
                    pool.tensor_tensor(hs[n % 3], hs[n % 3], Cr[:, n % 2, :].unsqueeze(1).to_broadcast([P, KT, L]),
                                       ALU.mult).then_inc(hc_ready.sem, 1)
            pool.wait_ge(list_filled, 16)
            pool.wait_ge(slots_ready, 1)
            for t in range(NT):
                for j in range(TOPK):
                    pool.indirect_dma_start(listd, bass.IndirectOffsetOnAxis(slots[:, j, t:t + 1], 0), pairs[:, t, j, :], None)\
                        .then_inc(scattered, 16)
            pool.wait_ge(meta_loaded, 16)
            pool.wait_ge(h_stored.sem, h_stored.at(B, 0))
            pool.wait_ge(out_stored, 16 * (NT + 1))

            def settle():
                pool.sem_inc(pool_passed, 1)

            def gather(s, u, r):
                ge(pool, gt_ready, s - 1)
                ge(pool, gathered[u], 32 * r)
                pool.tensor_copy(gidx[:, u, :, 0], meta[:, ds2(s), 0]).then_inc(gidx_ready, 1)
                pool.wait_ge(gidx_ready, s + 1)
                settle()
                for q in range(2):
                    pool.indirect_dma_start(G[:, u, q], None, Hd, bass.IndirectOffsetOnAxis(gidx[:, u, q, 0:1].bitcast(U32), 0))\
                        .then_inc(gathered[u], 16)

            def block_dmas(s, r, u):
                if not isinstance(s, int) or s + 1 < NBLK:
                    gather(s + 1, 1 - u, r if u == 0 else r + 1)
                if not isinstance(s, int) or s >= 2:
                    add(s - 2, u)

            def add(s, u):
                ge(pool, added, 32 * s)
                pool.tensor_copy(aidx[:, :, 0], meta[:, ds2(s), 0]).then_inc(aidx_ready, 1)
                pool.wait_ge(aidx_ready, s + 1)
                pool.wait_ge(y_d, s + 1)
                pool.wait_ge(y_a, s + 1)
                settle()
                for q in range(2):
                    pool.indirect_dma_start(out, bass.IndirectOffsetOnAxis(aidx[:, q, 0:1].bitcast(U32), 0), Yb[:, u, q], None,
                                            compute_op=ALU.add).then_inc(added, 16)

            gather(0, 0, 0)
            steps(pool, block_dmas, 0, NBLK - 1)
            for s in range(NBLK - 2, NBLK):
                add(s, s % 2)

        @block.scalar
        def _(act):
            order = Order(act, act_order, ACT_STEPS)
            act.wait_ge(vecs_loaded, 16)
            act.wait_ge(setup_pool, 4)
            act.activation(tg[:, :], vec("gates", 0, 4), ACT.Tanh)
            act.activation(negA[:, :], vec("A_log", 0, KT * DS), ACT.Exp).then_inc(setup_act, 1)

            def settle():
                act.sem_inc(act_passed, 1)

            def ln_root(b, k):
                act.wait_ge(ln_mv.sem, ln_mv.at(b, k + 1))
                act.activation(std[:, :], mv[:, :, 1], ACT.Sqrt, bias=eps[:, 0:1]).then_inc(ln_std.sem, 1)

            act.wait_ge(loaded, 16 * len(loads))
            with act.Fori(0, B) as b:
                order.enter(b)
                act.wait_ge(batch_done.sem, batch_done.at(b, 0))
                for e in range(KT):
                    act.wait_ge(xi_ready.sem, xi_ready.at(b, e + 1))
                    act.activation(xpad[:, e, 3:3 + L], ps[:, e, :], ACT.Copy).then_inc(xpad_ready.sem, 1)
                ln_root(b, 0)
                act.wait_ge(ln_coef.sem, ln_coef.at(b, 1))
                settle()
                for t in range(LT):
                    act.activation(siluz[:, t], X[:, b * LT + t, :], ACT.Silu, bias=nmr[:, t:t + 1],
                                   scale=rstd[:, t:t + 1]).then_inc(siluz_ready.sem, 1)
                for e in range(KT):
                    act.wait_ge(conv_ready.sem, conv_ready.at(b, e + 1))
                    act.activation(U[:, e], conv[:, e], ACT.Silu, bias=vec("conv_b", e)).then_inc(u_ready.sem, 1)
                act.wait_ge(dt_ready.sem, dt_ready.at(b, 1))
                for e in range(KT):
                    act.activation(sp_relu[:, e], ps[:, e, :], ACT.Relu, bias=vec("dt_b", e))
                    m = order.mark(act.activation(sp_abs[:, e], ps[:, e, :], ACT.Abs, bias=vec("dt_b", e)))
                order.wait(m)
                order.mark(act.activation(sp_exp, sp_abs, ACT.Exp, scale=-1.0))
                order.wait()
                act.activation(sp_ln, sp_exp, ACT.Ln, bias=1.0).then_inc(sp_ready.sem, 1)
                act.wait_ge(delta_ready.sem, delta_ready.at(b, 1))
                for n in range(DS):
                    if n >= 2:
                        act.wait_ge(scan_done.sem, scan_done.at(b, n - 1))
                    for e in range(KT):
                        i = act.activation(dA[n % 2][:, e, 1:L], delta[:, e, 1:L], ACT.Exp,
                                           scale=negA[:, e * DS + n:e * DS + n + 1])
                    i.then_inc(dA_ready.sem, 1)
                    act.wait_ge(c_ready.sem, c_ready.at(b, n + 1))
                    if n >= 2:
                        act.wait_ge(hc_ready.sem, hc_ready.at(b, n - 1))
                    act.activation(Cr[:, n % 2, :], ps[:, 6 + n % 2, :], ACT.Copy).then_inc(c_sb.sem, 1)
                ln_root(b, 1)
                for t in range(LT):
                    act.wait_ge(ternT_ready.sem, ternT_ready.at(b, t + 1))
                    act.activation(ternT[:, :, t * P:(t + 1) * P],
                                   ps[:, t, :].bitcast(BF16)[:, 0:DM].rearrange("p (k l) -> p k l", k=KT),
                                   ACT.Copy).then_inc(ternT_sb.sem, 1)
                ln_root(b, 2)
                act.wait_ge(ln_coef.sem, ln_coef.at(b, 3))
                settle()
                for t in range(LT):
                    act.activation(xn[:, t], X[:, b * LT + t, :], ACT.Identity, bias=nmr[:, t:t + 1],
                                   scale=rstd[:, t:t + 1]).then_inc(xn_ready.sem, 1)
                for n, i in enumerate(K_THEN_Q):
                    act.wait_ge(proj_ready.sem, proj_ready.at(b, n + 1))
                    bank = (4 + i) % 8
                    if i < KT:
                        act.activation(qk[:, i], ps[:, bank, :], ACT.Identity,
                                       bias=qkbias[:, i:i + 1]).then_inc(qc_ready.sem, 1)
                    else:
                        act.activation(qk[:, i, 0:MAIN], ps[:, bank, 0:MAIN], ACT.Identity, bias=qkbias[:, i:i + 1])
                        act.activation(qk[:, i, MAIN:L], ps[:, bank, MAIN:L], ACT.Identity,
                                       bias=qkbias[:, i + KT:i + KT + 1]).then_inc(qc_ready.sem, 1)
                act.wait_ge(var_ready.sem, var_ready.at(b, 1))
                act.activation(sdr[:, :], ps[0:32, 4, :], ACT.Sqrt, bias=eps[0:32, 1:2]).then_inc(std_ready.sem, 1)
                act.wait_ge(v_ready.sem, v_ready.at(b, 1))
                for j in range(LT - 1):
                    act.activation(Vn[:, j], ps[:, j, :], ACT.Copy)
                order.mark(act.activation(Vn[96:128, 3], ps[96:128, 5, :], ACT.Copy))
                order.wait()
                act.activation(Vn[0:MAIN - 3 * P, 3], ps[0:MAIN - 3 * P, 3, :], ACT.Copy).then_inc(v_sb.sem, 1)
                for i in range(8):
                    act.wait_ge(rb_used.sem, rb_used.at(b, i + 1))
                    if i < KT:
                        act.activation(qk[:, i], qk[:, i], ACT.Identity, bias=aff[:, 1:2]).then_inc(qk_final.sem, 1)
                    else:
                        act.activation(qk[:, i, 0:MAIN], qk[:, i, 0:MAIN], ACT.Identity, bias=aff[:, 3:4])
                        act.activation(qk[:, i, MAIN:L], qk[:, i, MAIN:L], ACT.Identity,
                                       bias=aff[:, 5:6]).then_inc(qk_final.sem, 1)

                def exps(it):
                    qp, h = divmod(it, H)
                    s = it % 2
                    act.wait_ge(nm_ready.sem, nm_ready.at(b, it + 1))
                    if it >= 2:
                        act.wait_ge(t_ready.sem, t_ready.at(b, it - 1))
                    for q in range(2):
                        bank = 2 * s + q
                        act.activation(Pr[:, s, q, 0:MAIN], ps[:, bank, 0:MAIN], ACT.Exp, bias=nm[:, s, q:q + 1],
                                       accum_out=esum[:, s, q:q + 1])
                        i = act.activation(Pr[:, s, q, MAIN:L], ps[:, bank, MAIN:L], ACT.Exp,
                                           bias=nm[:, s, 2 + q:3 + q], accum_out=esum[:, s, 2 + q:3 + q])
                    i.then_inc(p_raw.sem, 1)

                exps(0)
                exps(1)
                for it in range(NIT):
                    act.wait_ge(t_ready.sem, t_ready.at(b, it + 1))
                    if it >= 2:
                        act.wait_ge(pv_done.sem, pv_done.at(b, it - 1))
                    act.activation(PT[:, it % 2, 1], ps[:, 5, :], ACT.Copy).then_inc(pt_a.sem, 1)
                    if it + 2 < NIT:
                        exps(it + 2)
            order.leave()

            with act.Fori(0, B) as b:
                act.wait_ge(ln4_mv.sem, ln4_mv.at(b, 1))
                act.activation(std[:, :], mv[:, :, 1], ACT.Sqrt, bias=eps[:, 0:1]).then_inc(ln4_std.sem, 1)
                act.wait_ge(hT_sb.sem, hT_sb.at(b, 0))
                act.wait_ge(h_stored.sem, h_stored.at(b, 0))
                act.wait_ge(ln4_coef.sem, ln4_coef.at(b, 1))
                settle()
                for t in range(LT):
                    act.activation(hn[:, t], X[:, b * LT + t, :], ACT.Identity, bias=nmr[:, t:t + 1],
                                   scale=rstd[:, t:t + 1]).then_inc(hn_ready.sem, 1)
            act.wait_ge(logits_ready, 1)
            act.activation(SC.rearrange("p t e -> p (t e)"), ps[:, 4, :], ACT.Sigmoid).then_inc(sc_ready, 1)
            with act.Fori(0, B) as c:
                for m in range(3):
                    act.wait_ge(shg_ready.sem, shg_ready.at(c, m + 1))
                    act.activation(sil[:, m], ps[:, 2 * m, :], ACT.Silu).then_inc(sil_ready.sem, 1)

            def block_act(s, r, u):
                if not isinstance(s, int) or s >= 1:
                    act.wait_ge(at_ready, s)
                    ge(act, y_ready, 2 * (s - 1))
                    act.activation(aTp[:, 0, 0], ps[0:FH, 4, :].rearrange("p (f l) -> p f l", f=2), ACT.Copy).then_inc(at_hi, 1)
                split_up(s + 1, r if u == 0 else r + 1, 1 - u)
                for q in range(2):
                    act.wait_ge(gu_ready, 2 * s + q + 1)
                    ge(act, act_done, 2 * (s - 1) + q + 1)
                    act.activation(act_s[:, q, :], ps[:, 2 + q, 0:FE], ACT.Silu).then_inc(silu_done, 1)
                    if q == 0:
                        act.wait_ge(wdn_loaded[u], 16 * (r + 1))
                        ge(act, y_ready, 2 * (s - 1))
                        act.activation(wdnp[:, u, 0], wdn[0:FH, u], ACT.Copy).then_inc(wdn_hi, 1)
                turned(s + 1)
                scaled(s - 1, 1 - u)

            def split_up(s, r, u):
                if isinstance(s, int) and s >= NBLK:
                    return
                act.wait_ge(wgu_loaded[u], 16 * (r + 1))
                ge(act, gu_ready, 2 * (s - 1))
                act.activation(wgup[:, u, 0], wgu[:, u], ACT.Copy).then_inc(wgu_hi, 1)

            def turned(s):
                if isinstance(s, int) and s >= NBLK:
                    return
                act.wait_ge(gt_ready, s + 1)
                ge(act, gu_ready, 2 * s)
                act.activation(GTp[:, 0, 0], ps[:, 0:2, :].rearrange("p a (k l) -> p (a k) l", k=2), ACT.Copy).then_inc(gt_hi, 1)

            def scaled(s, u):
                if isinstance(s, int) and s < 0:
                    return
                act.wait_ge(y_ready, 2 * (s + 1))
                ge(act, added, 32 * (s - 1))
                settle()
                act.activation(Yb[:, u, 1], ps[:, 6, :], ACT.Copy, scale=meta[:, bass.ds(2 * s + 1, 1), 1].bitcast(F32))\
                    .then_inc(y_a, 1)

            act.wait_ge(shx_done.sem, shx_done.at(B, 0))
            split_up(0, 0, 0)
            turned(0)
            steps(act, block_act, 0, NBLK - 1)
            act.wait_ge(at_ready, NBLK)
            act.wait_ge(y_ready, 2 * (NBLK - 1))
            act.activation(aTp[:, 0, 0], ps[0:FH, 4, :].rearrange("p (f l) -> p f l", f=2), ACT.Copy).then_inc(at_hi, 1)
            scaled(NBLK - 1, 1)

        @block.tensor
        def _(pe):
            pe.wait_ge(vecs_loaded, 16)
            pe.wait_ge(setup_pool, 4)
            pe.wait_ge(setup_dve, 1)
            pe.matmul(ps[:, 0, 0:3 * KT], headmean[:, :], vec("bq", 0, 3 * KT), start=True, stop=True).then_inc(setup_pe, 1)
            pe.wait_ge(loaded, 16 * len(loads))
            with pe.Fori(0, B) as b:
                pe.wait_ge(batch_done.sem, batch_done.at(b, 0))
                pe.wait_ge(ctx_loaded.sem, ctx_loaded.at(b, 16))
                for e in range(KT):
                    for k in range(KC):
                        i = pe.matmul(ps[:, e, :], Win[:, k, e * P:(e + 1) * P], ctx[:, k, :], start=(k == 0), stop=(k == KC - 1))
                    i.then_inc(xi_ready.sem, 1)
                for k in range(KT):
                    pe.wait_ge(u_ready.sem, u_ready.at(b, k + 1))
                    i = pe.matmul(ps[0:DR + 2 * DS, 4, :], Wxp[:, k, :], U[:, k], start=(k == 0), stop=(k == KT - 1))
                i.then_inc(xd_ready.sem, 1)
                pe.wait_ge(xd_sb.sem, xd_sb.at(b, 1))
                for e in range(KT):
                    i = pe.matmul(ps[:, e, :], Wdt[:, e * P:(e + 1) * P], XD[0:DR, :], start=True, stop=True)
                i.then_inc(dt_ready.sem, 1)

                def spread(n, part, ready, used, bank):
                    if n >= 2:
                        pe.wait_ge(used.sem, used.at(b, n - 1))
                    row = identr[0:DR + 2 * DS, part + n:part + n + 1].to_broadcast([DR + 2 * DS, P])
                    pe.matmul(ps[:, bank + n % 2, :], row, XDr[:, 0, :], start=True, stop=False)
                    pe.matmul(ps[:, bank + n % 2, :], row, XDr[:, 1, :], start=False, stop=True).then_inc(ready.sem, 1)

                def spread_b(n):
                    spread(n, DR, b_ready, b_used, 4)

                def spread_c(n):
                    spread(n, DR + DS, c_ready, c_sb, 6)

                pe.wait_ge(xdr_ready.sem, xdr_ready.at(b, 1))
                spread_b(0)
                spread_b(1)
                spread_c(0)
                spread_b(2)
                for n in range(DS):
                    if n + 3 < DS:
                        spread_b(n + 3)
                    if n + 1 < DS:
                        spread_c(n + 1)
                    pe.wait_ge(hc_ready.sem, hc_ready.at(b, n + 1))
                    for e in range(KT):
                        i = pe.matmul(ps[:, e, :], ident[:, :], hs[n % 3][:, e], start=(n == 0), stop=(n == DS - 1))
                    i.then_inc(hc_used.sem, 1)
                for e in range(KT):
                    pe.wait_ge(yz_ready.sem, yz_ready.at(b, e + 1))
                    for l in range(LT):
                        i = pe.transpose(ps[:, 4 + l, e * P:(e + 1) * P], yz[:, e, l * P:(l + 1) * P], ident[:, :])
                i.then_inc(yt_ready.sem, 1)

                pe.wait_ge(tern_ready.sem, tern_ready.at(b, 1))
                for t in range(LT):
                    for k in range(KT):
                        i = pe.transpose(ps[:, t, :].bitcast(BF16)[:, k * P:(k + 1) * P], tern[:, t, k * P:(k + 1) * P],
                                         identb[:, :])
                    i.then_inc(ternT_ready.sem, 1)
                for t in range(LT):
                    pe.wait_ge(ternT_sb.sem, ternT_sb.at(b, t + 1))
                    for k in range(KT):
                        for part in range(3):
                            i = pe.matmul(ps[:, 4 + t, :], ternT[:, k, t * P:(t + 1) * P], W3[:, part, k, :],
                                          start=(k == 0 and part == 0), stop=(k == KT - 1 and part == 2))
                    i.then_inc(ffn_ready.sem, 1)

                for e in range(KT):
                    for k in range(KC):
                        pe.matmul(ps[:, e, 0:MAIN], Wk[:, k, e * P:(e + 1) * P], ctx[:, k, 0:MAIN], start=(k == 0),
                                  stop=(k == KC - 1))
                    for k in range(KC):
                        i = pe.matmul(ps[:, e, MAIN:L], Wkd[:, k, e * P:(e + 1) * P], ctx[:, k, MAIN:L],
                                      start=(k == 0), stop=(k == KC - 1))
                    i.then_inc(proj_ready.sem, 1)
                for t in range(LT):
                    pe.wait_ge(xn_ready.sem, xn_ready.at(b, t + 1))
                    for k in range(KT):
                        i = pe.transpose(ps[:, 4 + t, k * P:(k + 1) * P], xn[:, t, k * P:(k + 1) * P], ident[:, :])
                    i.then_inc(xT_ready.sem, 1)
                pe.wait_ge(xT_sb.sem, xT_sb.at(b, LT))
                for e in range(KT):
                    for k in range(KT):
                        i = pe.matmul(ps[:, 4 + e, :], Wq[:, k, e * P:(e + 1) * P], xnT[:, k], start=(k == 0),
                                      stop=(k == KT - 1))
                    i.then_inc(proj_ready.sem, 1)
                pe.wait_ge(qc_ready.sem, qc_ready.at(b, 5))
                for n, i8 in enumerate(K_THEN_Q):
                    pe.wait_ge(sq_ready.sem, sq_ready.at(b, n + 1))
                    i = pe.matmul(ps[0:32, 4, :], headvar[:, i8, :], sq[:, i8], start=(n == 0), stop=(n == 7))
                i.then_inc(var_ready.sem, 1)
                pe.wait_ge(qc_ready.sem, qc_ready.at(b, 8))
                for j in range(LT):
                    n = P if j < LT - 1 else MAIN - 3 * P
                    for k in range(KC):
                        pe.matmul(ps[0:n, j, :], ctx[:, k, j * P:j * P + n], Wv[:, k, :], start=(k == 0), stop=(k == KC - 1))
                for k in range(KC):
                    i = pe.matmul(ps[96:128, 5, :], ctx[:, k, L - 32:L], Wvd[:, k, :], start=(k == 0), stop=(k == KC - 1))
                i.then_inc(v_ready.sem, 1)
                pe.wait_ge(v_ready.sem, v_ready.at(b, 1))
                pe.sem_inc(ctx_free.sem, 1)
                pe.wait_ge(rrow_ready.sem, rrow_ready.at(b, 1))
                for i8 in range(8):
                    if i8 >= 2:
                        pe.wait_ge(rb_used.sem, rb_used.at(b, i8 - 1))
                    pe.matmul(ps[:, 6 + i8 % 2, :], headrow[:, i8, :], rrow_parts[:, 0, :], start=True, stop=False)
                    pe.matmul(ps[:, 6 + i8 % 2, :], headrow[:, i8, :], rrow_parts[:, 1, :], start=False, stop=True)\
                        .then_inc(rb_ready.sem, 1)
                pe.wait_ge(v_sb.sem, v_sb.at(b, 1))

                def scores(it):
                    qp, h = divmod(it, H)
                    rows, tile = slice(HD * (h % HPT), HD * (h % HPT + 1)), h // HPT
                    pe.wait_ge(qk_final.sem, qk_final.at(b, KT + tile + 1))
                    if it >= 2:
                        pe.wait_ge(p_raw.sem, p_raw.at(b, it - 1))
                    for q in range(2):
                        t = 2 * qp + q
                        i = pe.matmul(ps[:, 2 * (it % 2) + q, :], qk[rows, tile, t * P:(t + 1) * P], qk[rows, KT + tile, :],
                                      start=True, stop=True)
                    i.then_inc(s_ready.sem, 1)

                def turn(it):
                    pe.wait_ge(p_final.sem, p_final.at(b, it + 1))
                    if it >= 1:
                        pe.wait_ge(pt_d.sem, pt_d.at(b, it))
                        pe.wait_ge(pt_a.sem, pt_a.at(b, it))
                    for q in range(2):
                        for j in range(LT):
                            i = pe.transpose(ps[:, 4 + q, j * P:(j + 1) * P], Pr[:, it % 2, q, j * P:(j + 1) * P], ident[:, :])
                    i.then_inc(t_ready.sem, 1)

                def weigh(it):
                    qp, h = divmod(it, H)
                    pe.wait_ge(pt_d.sem, pt_d.at(b, it + 1))
                    pe.wait_ge(pt_a.sem, pt_a.at(b, it + 1))
                    if it == H:
                        pe.wait_ge(cT_sb.sem, cT_sb.at(b, 2))
                    rows, tile = slice(HD * (h % HPT), HD * (h % HPT + 1)), h // HPT
                    for j in range(LT):
                        i = pe.matmul(ps[rows, 6 + tile // 2, (tile % 2) * 2 * P:(tile % 2 + 1) * 2 * P],
                                      Vn[:, j, h * HD:(h + 1) * HD], PT[:, it % 2, :, j * P:(j + 1) * P],
                                      start=(j == 0), stop=(j == LT - 1))
                    i.then_inc(pv_done.sem, 1)

                scores(0)
                scores(1)
                for it in range(NIT):
                    if it + 2 < NIT:
                        scores(it + 2)
                    turn(it)
                    if it >= 1:
                        weigh(it - 1)
                weigh(NIT - 1)
                for t in range(LT):
                    pe.wait_ge(cT_sb.sem, cT_sb.at(b, 2 * (t // 2 + 1)))
                    for k in range(KT):
                        pe.matmul(ps[:, 4 + t, :], ctxnT[:, k, t * P:(t + 1) * P], Wo[:, k, :], start=(k == 0), stop=False)
                    pe.matmul(ps[:, 4 + t, :], ones1[:, :], bo[:, :], start=False, stop=True).then_inc(o_ready.sem, 1)

            with pe.Fori(0, B) as b:
                for t in range(LT):
                    pe.wait_ge(hn_ready.sem, hn_ready.at(b, t + 1))
                    for k in range(KT):
                        i = pe.transpose(ps[:, t, k * P:(k + 1) * P], hn[:, t, k * P:(k + 1) * P], ident[:, :])
                    i.then_inc(hT_ready.sem, 1)
            pe.wait_ge(hT_sb.sem, hT_sb.at(B, 0))
            for t in range(NT):
                for k in range(KT):
                    i = pe.matmul(ps[:, 4, t * NE:(t + 1) * NE], HT[:, k, t * P:(t + 1) * P], Wg[:, k, :], start=(k == 0),
                                  stop=(k == KT - 1))
            i.then_inc(logits_ready, 1)
            pe.wait_ge(mask_ready, 1)
            pe.matmul(ps[:, 5, :], tri[:, :], Mb[:, :], start=True, stop=True)
            pe.matmul(ps[:, 6, :], onesb[:, :], Mb[:, :], start=True, stop=True).then_inc(prefix_ready, 1)
            pe.wait_ge(sh_loaded, 32)
            pe.wait_ge(slots_ready, 1)
            with pe.Fori(0, B) as c:
                for m in range(3):
                    for half in range(2):
                        for k in range(KT):
                            i = pe.matmul(ps[:, 2 * m + half, :], Wsh[:, k, half * FS + m * P:half * FS + (m + 1) * P],
                                          HT[:, k, bass.ds(c * L, L)], start=(k == 0), stop=(k == KT - 1))
                    i.then_inc(shg_ready.sem, 1)
                for t in range(LT):
                    if t >= 2:
                        pe.wait_ge(shx_done.sem, shx_done.at(c, t - 1))
                    for m in range(3):
                        if t == 0:
                            pe.wait_ge(aS_ready.sem, aS_ready.at(c, m + 1))
                        i = pe.matmul(ps[:, 6 + t % 2, :], aS[:, m, t * P:(t + 1) * P], Wsd[:, m, :], start=(m == 0),
                                      stop=(m == 2))
                    i.then_inc(shy_ready.sem, 1)
            pe.wait_ge(shx_done.sem, shx_done.at(B, 0))

            def turn_tokens(s, r, u):
                if isinstance(s, int) and s >= NBLK:
                    return
                pe.wait_ge(gathered[u], 32 * (r + 1))
                ge(pe, gt_lo, s)
                for k in range(KT):
                    for q in range(2):
                        i = pe.transpose(ps[:, k // 2, (k % 2) * BLK + q * P:(k % 2) * BLK + (q + 1) * P],
                                         G[:, u, q, k * P:(k + 1) * P], ident[:, :])
                i.then_inc(gt_ready, 1)

            def product(out, a, w, first, last):
                for i, (pa, pw) in enumerate(((0, 0), (0, 1), (1, 0))):
                    ins = pe.matmul(out, a(pa), w(pw), start=(first and i == 0), stop=(last and i == 2))
                return ins

            def up(s, r, u):
                pe.wait_ge(gt_lo, s + 1)
                pe.wait_ge(wgu_lo, s + 1)
                for q in range(2):
                    ge(pe, act_done, 2 * (s - 1) + q + 1)
                    for k in range(KT):
                        i = product(ps[:, 2 + q, 0:2 * FE], lambda h: GTp[:, 0, h, k, q * P:(q + 1) * P],
                                    lambda h: wgup[:, u, h, k], k == 0, k == KT - 1)
                    i.then_inc(gu_ready, 1)

            def turn_act(s, r, u):
                if isinstance(s, int) and s < 0:
                    return
                pe.wait_ge(act_done, 2 * (s + 1))
                ge(pe, at_lo, s)
                for f in range(2):
                    for q in range(2):
                        i = pe.transpose(ps[0:FH, 4, f * BLK + q * P:f * BLK + (q + 1) * P], act_m[:, q, f * FH:(f + 1) * FH],
                                         ident[:, :])
                i.then_inc(at_ready, 1)

            def down(s, r, u):
                if isinstance(s, int) and s < 0:
                    return
                pe.wait_ge(at_lo, s + 1)
                pe.wait_ge(wdn_lo, s + 1)
                ge(pe, y_a, s)
                ge(pe, y_d, s)
                for q in range(2):
                    for f in range(2):
                        i = product(ps[:, 5 + q, :], lambda h: aTp[:, 0, h, f, q * P:(q + 1) * P],
                                    lambda h: wdnp[:, u, h, f], f == 0, f == 1)
                    i.then_inc(y_ready, 1)

            def block_pe(s, r, u):
                before = (s - 1, r - 1 if u == 0 else r, 1 - u)
                turn_act(*before)
                up(s, r, u)
                turn_tokens(s + 1, r if u == 0 else r + 1, 1 - u)
                down(*before)

            turn_tokens(0, 0, 0)
            steps(pe, block_pe, 0, NBLK - 1)
            last = (NBLK - 1, (NBLK - 1) // 2, 1)
            turn_act(*last)
            down(*last)

        @block.vector
        def _(dve):
            order = Order(dve, dve_order, DVE_STEPS)
            o = order
            dve.memset(headmean[:, :], 0.0)
            o.mark(dve.memset(headvar[:, :, :], 0.0))
            o.wait()
            dve.wait_ge(setup_iota, 2)
            dve.tensor_copy(iota_f[:, :], iota_i[:, :])
            dve.tensor_copy(blk_f[:, :], blk_i[:, :])
            dve.tensor_copy(tri[:, :], tri_f[:, :])
            o.mark(dve.tensor_scalar(meta[:, :, 0], meta[:, :, 0], BLK - 1, None, ALU.bitwise_and))
            o.wait()
            dve.tensor_scalar(meta[:, :, 0], meta[:, :, 0], float(NT * P), None, ALU.add).then_inc(fill_ready, 1)
            flat_var = headvar[:, :, :].rearrange("p i c -> p (i c)")
            for j in range(HPT):
                rows = slice(HD * j, HD * (j + 1))
                dve.memset(headmean[rows, rows], 1.0 / HD)
                i = dve.memset(flat_var[rows, j:j + 36 * 7 + 1:36], 1.0 / HD)
            i.then_inc(setup_dve, 1)
            dve.wait_ge(vecs_loaded, 16)
            dve.wait_ge(ffn_loaded, 32)
            w, r, lt, acc = wtmp
            a = o.mark(dve.tensor_scalar(lt, w, -TH_W, None, ALU.is_lt))
            o.wait(a)
            o.mark(dve.scalar_tensor_tensor(out=acc, in0=w, scalar=TH_W, in1=lt, op0=ALU.is_gt, op1=ALU.subtract))
            o.wait()
            o.mark(dve.scalar_tensor_tensor(out=acc, in0=acc, scalar=SC_W, in1=r, op0=ALU.mult, op1=ALU.add))
            o.wait()
            o.mark(dve.tensor_scalar(acc, acc, -SC_X, None, ALU.mult))
            for part in range(3):
                o.wait()
                o.mark(dve.tensor_copy(W3[:, part], acc))
                if part < 2:
                    o.wait()
                    o.mark(dve.tensor_tensor(acc, acc, W3[:, part], ALU.subtract))
            dve.wait_ge(wqk_loaded, 48)
            for W, kt in ((Wq, KT), (Wk, KC), (Wkd, KC)):
                heads = W[:, :, :].rearrange("p k (h d) -> p (k h) d", d=HD)
                o.mark(dve.tensor_reduce(wsum[:, 0:kt * H], heads, AX.X, ALU.add))
                o.wait()
                o.mark(dve.tensor_scalar(wsum[:, 0:kt * H], wsum[:, 0:kt * H], 1.0 / HD, None, ALU.mult))
                o.wait()
                o.mark(dve.tensor_tensor(heads, heads, wsum[:, 0:kt * H].unsqueeze(2).to_broadcast([P, kt * H, HD]),
                                         ALU.subtract))
                o.wait()
            dve.wait_ge(setup_pe, 1)
            dve.tensor_tensor(qkbias[:, :], vec("bq", 0, 3 * KT), ps[:, 0, 0:3 * KT], ALU.subtract)
            dve.tensor_tensor(bvsum[:, :], vec("bv", 0, KT), vec("bvd", 0, KT), ALU.add)
            dve.tensor_scalar(aff[:, 0:2], vec("qw", 0, 2), QK_SCALE, None, ALU.mult)
            dve.tensor_copy(aff[:, 2:6], vec("kw", 0, 4))
            dve.wait_ge(setup_act, 1)
            o.mark(dve.tensor_scalar(negA[:, :], negA[:, :], -1.0, None, ALU.mult))
            o.wait()
            dve.wait_ge(loaded, 16 * len(loads))
            dve.tensor_copy(std[:, 0:1], V_[:, 0:1]).then_inc(batch_done.sem, 1)

            def settle():
                dve.sem_inc(dve_passed, 1)

            def ln_stats(b, k):
                settle()
                for t in range(LT):
                    i = dve.bn_stats(st6[:, t, :], X[:, b * LT + t, :])
                o.mark(i)
                o.wait()
                settle()
                for t in range(LT):
                    i = dve.bn_aggr(mv[:, t, :], st6[:, t, :])
                i.then_inc(ln_mv.sem, 1)

            def ln_coefs(b, k):
                dve.wait_ge(ln_std.sem, ln_std.at(b, k + 1))
                o.mark(dve.reciprocal(rstd[:, :], std[:, :]))
                o.wait()
                dve.scalar_tensor_tensor(out=nmr[:, :], in0=mv[:, :, 0], scalar=-1.0, in1=rstd[:, :], op0=ALU.mult,
                                         op1=ALU.mult).then_inc(ln_coef.sem, 1)

            with dve.Fori(0, B) as b:
                o.enter(b)
                dve.wait_ge(batch_done.sem, batch_done.at(b, 0))
                pad = o.mark(dve.memset(xpad[:, :, 0:3], 0.0))
                ln_stats(b, 0)
                ln_coefs(b, 0)
                o.wait(pad)
                marks = []
                for tap in (3, 2, 1, 0):
                    for e in range(KT):
                        wk = vec("conv_w", e * TAPS + tap)
                        if tap == 3:
                            dve.wait_ge(xpad_ready.sem, xpad_ready.at(b, e + 1))
                            i = dve.tensor_scalar(conv[:, e], xpad[:, e, tap:tap + L], wk, None, ALU.mult)
                        else:
                            o.wait(marks[-KT])
                            i = dve.scalar_tensor_tensor(out=conv[:, e], in0=xpad[:, e, tap:tap + L], scalar=wk,
                                                         in1=conv[:, e], op0=ALU.mult, op1=ALU.add)
                        if tap:
                            marks.append(o.mark(i))
                        else:
                            i.then_inc(conv_ready.sem, 1)
                            marks.append(marks[-1])
                dve.wait_ge(xd_ready.sem, xd_ready.at(b, 1))
                dve.tensor_copy(XD[:, :], ps[0:DR + 2 * DS, 4, :]).then_inc(xd_sb.sem, 1)
                xd_hi = o.mark(dve.tensor_copy(XDr[:, 0, :], ps[0:DR + 2 * DS, 4, :]))
                o.wait(xd_hi)
                dve.tensor_tensor(XDr[:, 1, :], ps[0:DR + 2 * DS, 4, :], XDr[:, 0, :], ALU.subtract)\
                    .then_inc(xdr_ready.sem, 1)
                dve.wait_ge(conv_ready.sem, conv_ready.at(b, KT))
                for s in range(2):
                    i = dve.memset(dA[s][:, :, 0:1], 0.0)
                zero = o.mark(i)
                dve.wait_ge(sp_ready.sem, sp_ready.at(b, 1))
                dve.tensor_tensor(delta, sp_relu, sp_ln, ALU.add).then_inc(delta_ready.sem, 1)
                dve.wait_ge(delta_ready.sem, delta_ready.at(b, 1))
                o.mark(dve.tensor_tensor(du, delta, U, ALU.mult))
                o.wait()

                def flat(t):
                    return t.rearrange("p e l -> p (e l)")

                def inputs(n):
                    dve.wait_ge(b_ready.sem, b_ready.at(b, n + 1))
                    if n >= 2:
                        dve.wait_ge(scan_done.sem, scan_done.at(b, n - 1))
                    dve.tensor_tensor(dBu[n % 2], du, ps[:, 4 + n % 2, :].unsqueeze(1).to_broadcast([P, KT, L]),
                                      ALU.mult).then_inc(b_used.sem, 1)

                def scan(n):
                    dve.wait_ge(dA_ready.sem, dA_ready.at(b, n + 1))
                    dve.wait_ge(b_used.sem, b_used.at(b, n + 1))
                    if n >= 3:
                        dve.wait_ge(hc_used.sem, hc_used.at(b, n - 2))
                    dve.tensor_tensor_scan(flat(hs[n % 3]), flat(dA[n % 2]), flat(dBu[n % 2]), 0.0, ALU.mult,
                                           ALU.add).then_inc(scan_done.sem, 1)

                inputs(0)
                for n in range(DS):
                    if n + 1 < DS:
                        inputs(n + 1)
                    scan(n)
                dve.wait_ge(hc_used.sem, hc_used.at(b, DS))
                dve.wait_ge(siluz_ready.sem, siluz_ready.at(b, LT))
                for e in range(KT):
                    m = o.mark(dve.scalar_tensor_tensor(out=yt[:, e], in0=U[:, e], scalar=vec("D", e), in1=ps[:, e, :],
                                                        op0=ALU.mult, op1=ALU.add))
                    if e:
                        o.wait(m - 1)
                        dve.tensor_tensor(yz[:, e - 1], yt[:, e - 1], siluz[:, e - 1], ALU.mult).then_inc(yz_ready.sem, 1)
                o.wait(m)
                dve.tensor_tensor(yz[:, KT - 1], yt[:, KT - 1], siluz[:, KT - 1], ALU.mult).then_inc(yz_ready.sem, 1)

                def add(bank, gate):
                    return o.mark(dve.scalar_tensor_tensor(
                        out=X[:, b * LT + bank - 4, :], in0=ps[:, bank, :], scalar=tg[:, gate:gate + 1],
                        in1=X[:, b * LT + bank - 4, :], op0=ALU.mult, op1=ALU.add))

                dve.wait_ge(yt_ready.sem, yt_ready.at(b, 1))
                for l in range(LT):
                    add(4 + l, 0)
                o.wait()
                ln_stats(b, 1)
                ln_coefs(b, 1)
                dve.wait_ge(ln_coef.sem, ln_coef.at(b, 2))
                for t in range(LT):
                    i = dve.tensor_scalar(xn[:, t], X[:, b * LT + t, :], mv[:, t, 0:1], rstd[:, t:t + 1], ALU.subtract,
                                          ALU.mult)
                o.mark(i)
                o.wait()
                o.mark(dve.tensor_scalar(gt, xn, TH_X, None, ALU.is_gt))
                o.wait()
                dve.scalar_tensor_tensor(out=tern, in0=xn, scalar=-TH_X, in1=gt, op0=ALU.is_lt,
                                         op1=ALU.subtract).then_inc(tern_ready.sem, 1)
                for t in range(LT):
                    dve.wait_ge(ffn_ready.sem, ffn_ready.at(b, t + 1))
                    add(4 + t, 1)
                o.wait()
                ln_stats(b, 2)
                ln_coefs(b, 2)
                for t in range(LT):
                    dve.wait_ge(xT_ready.sem, xT_ready.at(b, t + 1))
                    dve.tensor_copy(xnT[:, :, t * P:(t + 1) * P], ps[:, 4 + t, :].rearrange("p (k l) -> p k l", k=KT))\
                        .then_inc(xT_sb.sem, 1)
                for n, i8 in enumerate(K_THEN_Q):
                    dve.wait_ge(qc_ready.sem, qc_ready.at(b, n + 1))
                    dve.tensor_tensor(sq[:, i8], qk[:, i8], qk[:, i8], ALU.mult).then_inc(sq_ready.sem, 1)
                dve.wait_ge(std_ready.sem, std_ready.at(b, 1))
                o.mark(dve.reciprocal(rrow[:, :], sdr[:, :]))
                o.wait()
                o.mark(dve.tensor_copy(rrow_parts[:, 0, :], rrow[:, :]))
                o.wait()
                dve.tensor_tensor(rrow_parts[:, 1, :], rrow[:, :], rrow_parts[:, 0, :], ALU.subtract)\
                    .then_inc(rrow_ready.sem, 1)
                for i8 in range(8):
                    dve.wait_ge(rb_ready.sem, rb_ready.at(b, i8 + 1))
                    bank = 6 + i8 % 2
                    if i8 < KT:
                        dve.scalar_tensor_tensor(out=qk[:, i8], in0=qk[:, i8], scalar=aff[:, 0:1], in1=ps[:, bank, :],
                                                 op0=ALU.mult, op1=ALU.mult).then_inc(rb_used.sem, 1)
                    else:
                        dve.scalar_tensor_tensor(out=qk[:, i8, 0:MAIN], in0=qk[:, i8, 0:MAIN], scalar=aff[:, 2:3],
                                                 in1=ps[:, bank, 0:MAIN], op0=ALU.mult, op1=ALU.mult)
                        dve.scalar_tensor_tensor(out=qk[:, i8, MAIN:L], in0=qk[:, i8, MAIN:L], scalar=aff[:, 4:5],
                                                 in1=ps[:, bank, MAIN:L], op0=ALU.mult, op1=ALU.mult)\
                            .then_inc(rb_used.sem, 1)

                def maxima(it):
                    s = it % 2
                    dve.wait_ge(s_ready.sem, s_ready.at(b, it + 1))
                    if it >= 2:
                        dve.wait_ge(p_raw.sem, p_raw.at(b, it - 1))
                    dve.tensor_reduce(nm[:, s, 0:2], ps[:, 2 * s:2 * s + 2, 0:MAIN], AX.X, ALU.max, negate=True)
                    dve.tensor_reduce(nm[:, s, 2:4], ps[:, 2 * s:2 * s + 2, MAIN:L], AX.X, ALU.max, negate=True)\
                        .then_inc(nm_ready.sem, 1)

                def normalise(it):
                    s = it % 2
                    dve.wait_ge(p_raw.sem, p_raw.at(b, it + 1))
                    o.mark(dve.reciprocal(escale[:, s, :], esum[:, s, :]))
                    o.wait()
                    for q in range(2):
                        dve.tensor_scalar(Pr[:, s, q, 0:MAIN], Pr[:, s, q, 0:MAIN], escale[:, s, q:q + 1], None, ALU.mult)
                    dve.tensor_tensor(Pr[:, s, :, MAIN:L], Pr[:, s, :, MAIN:L],
                                      escale[:, s, 2:4].unsqueeze(2).to_broadcast([P, 2, DCA]), ALU.mult)\
                        .then_inc(p_final.sem, 1)

                def heads_out(qp):
                    dve.wait_ge(pv_done.sem, pv_done.at(b, (qp + 1) * H))
                    for half in range(2):
                        dve.tensor_tensor(ctxnT[:, 2 * half:2 * half + 2, qp * 2 * P:(qp + 1) * 2 * P],
                                          ps[:, 6 + half, :].rearrange("p (k l) -> p k l", k=2),
                                          bvsum[:, 2 * half:2 * half + 2].unsqueeze(2).to_broadcast([P, 2, 2 * P]),
                                          ALU.add).then_inc(cT_sb.sem, 1)

                maxima(0)
                maxima(1)
                normalise(0)
                for it in range(NIT):
                    if it + 2 < NIT:
                        maxima(it + 2)
                    if it + 1 < NIT:
                        normalise(it + 1)
                    dve.wait_ge(t_ready.sem, t_ready.at(b, it + 1))
                    if it >= 2:
                        dve.wait_ge(pv_done.sem, pv_done.at(b, it - 1))
                    dve.tensor_copy(PT[:, it % 2, 0], ps[:, 4, :]).then_inc(pt_d.sem, 1)
                    if it == H:
                        heads_out(0)
                heads_out(1)
                for t in range(LT):
                    dve.wait_ge(o_ready.sem, o_ready.at(b, t + 1))
                    add(4 + t, 2)
                o.wait()
                dve.tensor_copy(std[:, 0:1], rstd[:, 0:1]).then_inc(batch_done.sem, 1)
            o.leave()

            dve.wait_ge(batch_done.sem, B + 1)
            dve.memset(zero_rows, 0.0).then_inc(zero_ready, 1)
            dve.tensor_copy(std[:, 0:1], rstd[:, 0:1]).then_inc(hT_sb.sem, 1)
            with dve.Fori(0, B) as b:
                for t in range(LT):
                    i = dve.bn_stats(st6[:, t, :], X[:, b * LT + t, :])
                i.then_inc(prep_order, 1)
                dve.wait_ge(prep_order, 2 * b + 1)
                settle()
                for t in range(LT):
                    i = dve.bn_aggr(mv[:, t, :], st6[:, t, :])
                i.then_inc(ln4_mv.sem, 1)
                dve.wait_ge(ln4_std.sem, ln4_std.at(b, 1))
                dve.reciprocal(rstd[:, :], std[:, :]).then_inc(prep_order, 1)
                dve.wait_ge(prep_order, 2 * b + 2)
                dve.scalar_tensor_tensor(out=nmr[:, :], in0=mv[:, :, 0], scalar=-1.0, in1=rstd[:, :], op0=ALU.mult,
                                         op1=ALU.mult).then_inc(ln4_coef.sem, 1)
                for t in range(LT):
                    dve.wait_ge(hT_ready.sem, hT_ready.at(b, t + 1))
                    dve.tensor_copy(HT[:, :, bass.ds(b * L + t * P, P)], ps[:, t, :].rearrange("p (k l) -> p k l", k=KT))\
                        .then_inc(hT_sb.sem, 1)

            def chain(ins):
                o.mark(ins)
                o.wait()

            dve.wait_ge(sc_ready, 1)
            for t in range(NT):
                i = dve.max(top[:, t, :], SC[:, t, :])
            chain(i)
            for t in range(NT):
                i = dve.max_index(topi[:, t, :], top[:, t, :], SC[:, t, :])
            chain(i)
            o.mark(dve.tensor_reduce(den[:, :], top[:, :, 0:TOPK], AX.X, ALU.add))
            chain(dve.tensor_copy(topf[:, :, :], topi[:, :, :]))
            chain(dve.tensor_scalar(den[:, :], den[:, :], 1e-20, None, ALU.add))
            chain(dve.reciprocal(den[:, :], den[:, :]))
            chain(dve.tensor_scalar(den[:, :], den[:, :], tg[:, 3:4], None, ALU.mult))
            dve.tensor_tensor(pairs[:, :, :, 1].bitcast(F32), top[:, :, 0:TOPK],
                              den[:, :].unsqueeze(2).to_broadcast([P, NT, TOPK]), ALU.mult)
            dve.tensor_copy(pairs[:, :, :, 0], tok_i[:, :].unsqueeze(2).to_broadcast([P, NT, TOPK]))
            for j in range(TOPK):
                i = dve.tensor_tensor(pick[:, j], iota_f[:, :].unsqueeze(1).to_broadcast([P, NT, NE]),
                                      topf[:, :, j:j + 1].to_broadcast([P, NT, NE]), ALU.is_equal)
            chain(i)
            chain(dve.tensor_tensor(msum, pick[:, 0], pick[:, 1], ALU.add))
            for j in range(2, TOPK):
                chain(dve.tensor_tensor(msum, msum, pick[:, j], ALU.add))
            dve.tensor_copy(Mb[:, :], msum.rearrange("p t e -> p (t e)")).then_inc(mask_ready, 1)
            dve.wait_ge(prefix_ready, 1)
            chain(dve.tensor_copy(tot, ps[:, 6, :].rearrange("p (t e) -> p e t", e=NE)))
            chain(dve.tensor_tensor_scan(cum.rearrange("p e t -> p (e t)"), keep[:, :, :].rearrange("p e t -> p (e t)"),
                                         tot.rearrange("p e t -> p (e t)"), 0.0, ALU.mult, ALU.add))
            o.mark(dve.tensor_scalar(nb_i[:, :], cum[:, :, NT - 1], float(BLK - 1), None, ALU.add))
            chain(dve.tensor_tensor(tot, cum, tot, ALU.subtract))
            chain(dve.tensor_scalar(nb_i[:, :], nb_i[:, :], BLK.bit_length() - 1, None, ALU.logical_shift_right))
            chain(dve.tensor_copy(nb_f[:, :], nb_i[:, :]))
            chain(dve.tensor_tensor_scan(end_b[:, :], ones_e[:, :], nb_f[:, :], 0.0, ALU.mult, ALU.add))
            chain(dve.tensor_tensor(start_b[:, :], end_b[:, :], nb_f[:, :], ALU.subtract))
            chain(dve.tensor_scalar(start_b[:, :], start_b[:, :], float(BLK), None, ALU.mult))
            chain(dve.tensor_tensor(slot, ps[:, 5, :].rearrange("p (t e) -> p t e", e=NE), tot.rearrange("p e t -> p t e"),
                                    ALU.add))
            chain(dve.tensor_tensor(slot, slot, start_b[:, :].unsqueeze(1).to_broadcast([P, NT, NE]), ALU.add))
            for j in range(TOPK):
                chain(dve.tensor_tensor(tmp, pick[:, j], slot, ALU.mult))
                chain(dve.tensor_reduce(slots_f[:, j, :], tmp, AX.X, ALU.add))
            dve.tensor_copy(slots[:, :, :], slots_f[:, :, :]).then_inc(slots_ready, 1)
            chain(dve.tensor_tensor(le[:, :, :], end_b[0:1, :].unsqueeze(1).to_broadcast([1, NBLK, NE]),
                                    blk_f[:, :].unsqueeze(2).to_broadcast([1, NBLK, NE]), ALU.is_le))
            chain(dve.tensor_reduce(expert_f[:, :], le[:, :, :], AX.X, ALU.add))
            dve.tensor_scalar(expert_i[:, :], expert_f[:, :], float(NE - 1), None, ALU.min).then_inc(expert_ready, 1)

            with dve.Fori(0, B) as c:
                for m in range(3):
                    dve.wait_ge(sil_ready.sem, sil_ready.at(c, m + 1))
                    dve.tensor_tensor(aS[:, m], sil[:, m], ps[:, 2 * m + 1, :], ALU.mult).then_inc(aS_ready.sem, 1)
                for t in range(LT):
                    dve.wait_ge(shy_ready.sem, shy_ready.at(c, t + 1))
                    dve.scalar_tensor_tensor(out=X[:, c * LT + t, :], in0=ps[:, 6 + t % 2, :], scalar=tg[:, 3:4],
                                             in1=X[:, c * LT + t, :], op0=ALU.mult, op1=ALU.add).then_inc(shx_done.sem, 1)
            dve.wait_ge(meta_loaded, 16)

            def turned(s):
                if isinstance(s, int) and s >= NBLK:
                    return
                dve.wait_ge(gt_hi, s + 1)
                ge(dve, gu_ready, 2 * s)
                dve.tensor_tensor(GTp[:, 0, 1], ps[:, 0:2, :].rearrange("p a (k l) -> p (a k) l", k=2), GTp[:, 0, 0], ALU.subtract)\
                    .then_inc(gt_lo, 1)

            def split_up(s, u):
                if isinstance(s, int) and s >= NBLK:
                    return
                dve.wait_ge(wgu_hi, s + 1)
                ge(dve, gu_ready, 2 * (s - 1))
                dve.tensor_tensor(wgup[:, u, 1], wgu[:, u], wgup[:, u, 0], ALU.subtract).then_inc(wgu_lo, 1)

            def turned_act(s):
                dve.wait_ge(at_hi, s + 1)
                ge(dve, y_ready, 2 * s)
                dve.tensor_tensor(aTp[:, 0, 1], ps[0:FH, 4, :].rearrange("p (f l) -> p f l", f=2), aTp[:, 0, 0], ALU.subtract)\
                    .then_inc(at_lo, 1)

            def block_dve(s, r, u):
                if not isinstance(s, int) or s >= 1:
                    turned_act(s - 1)
                split_up(s + 1, 1 - u)
                for q in range(2):
                    dve.wait_ge(silu_done, 2 * s + q + 1)
                    ge(dve, at_ready, s)
                    dve.tensor_tensor(act_m[:, q, :], act_s[:, q, :], ps[:, 2 + q, FE:2 * FE], ALU.mult)\
                        .then_inc(act_done, 1)
                    if q == 0:
                        dve.wait_ge(wdn_hi, s + 1)
                        ge(dve, y_ready, 2 * (s - 1))
                        dve.tensor_tensor(wdnp[:, u, 1], wdn[0:FH, u], wdnp[:, u, 0], ALU.subtract).then_inc(wdn_lo, 1)
                turned(s + 1)
                scaled(s - 1, 1 - u)

            def scaled(s, u):
                if isinstance(s, int) and s < 0:
                    return
                dve.wait_ge(y_ready, 2 * s + 1)
                ge(dve, added, 32 * (s - 1))
                dve.tensor_scalar(Yb[:, u, 0], ps[:, 5, :], meta[:, bass.ds(2 * s, 1), 1].bitcast(F32), None, ALU.mult)\
                    .then_inc(y_d, 1)

            split_up(0, 0)
            turned(0)
            steps(dve, block_dve, 0, NBLK - 1)
            turned_act(NBLK - 1)
            scaled(NBLK - 1, 1)


_INS = ["x", "ctxT", "vecs", "w_in", "w_xp", "w_dt", "ffn_w", "ffn_r", "w_q", "w_k", "w_v", "w_kd", "w_vd", "w_o", "b_o", "w_g",
        "w_sh", "w_sd", "w_gu", "w_dn"]
_OUTS = [((B * L + BLK, DM), "float32")]


def _by_row(w, p=P):
    k = w.shape[0] // p
    return w.reshape(k, p, -1).transpose(1, 0, 2)


def lay_out(a):
    g = {}
    g["x"] = a["x"].reshape(B * L, DM)
    g["ctxT"] = a["ctx_1024"].transpose(0, 2, 1).reshape(B, KC, P, L).transpose(0, 2, 1, 3)
    g["w_in"] = _by_row(a["L0_xattn_in_proj_w"].T)
    g["w_xp"] = _by_row(a["L0_xattn_x_proj_w"].T)
    g["w_dt"] = a["L0_xattn_dt_proj_w"].T
    g["ffn_w"] = _by_row(a["L0_ffn_weight"].T)
    g["ffn_r"] = _by_row(a["L0_ffn_rram_variation"].T)
    g["w_q"] = _by_row(a["L1_xattn_Wq"])
    kv = np.concatenate([a["L1_xattn_Wk"], a["L1_xattn_Wv"]], 1).reshape(DC, H, 2, HD)
    bkv = np.concatenate([a["L1_xattn_bk"], a["L1_xattn_bv"]]).reshape(H, 2, HD)
    g["w_k"] = _by_row(kv[:, :, 0].reshape(DC, DM))
    g["w_v"] = _by_row(kv[:, :, 1].reshape(DC, DM))
    g["w_kd"] = _by_row(a["L1_xattn_Wkv_dca"][:, :DM])
    g["w_vd"] = _by_row(a["L1_xattn_Wkv_dca"][:, DM:])
    g["w_o"] = _by_row(a["L1_xattn_Wo"])
    g["b_o"] = a["L1_xattn_bo"].reshape(1, DM)
    g["w_g"] = _by_row(a["L1_ffn_gate_w"])
    g["w_sh"] = _by_row(np.concatenate([a["L1_ffn_sg"], a["L1_ffn_su"]], 1))
    g["w_sd"] = _by_row(a["L1_ffn_sd"])
    gu = np.concatenate([a["L1_ffn_wg"], a["L1_ffn_wu"]], 2)
    g["w_gu"] = gu.reshape(NE, KT, P, 2 * FE).transpose(0, 2, 1, 3)
    g["w_dn"] = a["L1_ffn_wd"].reshape(NE, 2, FH, DM).transpose(0, 2, 1, 3)
    vecs = np.empty((P, NVEC), np.float32)

    def put(name, v):
        vecs[:, VEC[name][0]:VEC[name][1]] = v

    put("conv_w", _by_row(a["L0_xattn_conv_w"]).reshape(P, -1))
    put("conv_b", a["L0_xattn_conv_b"].reshape(KT, P).T)
    put("dt_b", a["L0_xattn_dt_proj_b"].reshape(KT, P).T)
    put("A_log", _by_row(a["L0_xattn_A_log"]).reshape(P, -1))
    put("D", a["L0_xattn_D"].reshape(KT, P).T)
    put("bq", a["L1_xattn_bq"].reshape(KT, P).T)
    put("bk", bkv[:, 0].reshape(KT, P).T)
    put("bkd", a["L1_xattn_bkv_dca"][:DM].reshape(KT, P).T)
    put("bv", bkv[:, 1].reshape(KT, P).T)
    put("bvd", a["L1_xattn_bkv_dca"][DM:].reshape(KT, P).T)
    for name, src in (("qw", "qn_w"), ("qb", "qn_b"), ("kw", "kn_w"), ("kb", "kn_b"), ("kdw", "kn_dca_w"), ("kdb", "kn_dca_b")):
        put(name, np.tile(a["L1_xattn_" + src], HPT).reshape(P, 1))
    for i, (src, j) in enumerate((("g_xattn", 0), ("g_ffn", 0), ("g_xattn", 1), ("g_ffn", 1))):
        vecs[:, VEC["gates"][0] + i] = a[src][j]
    g["vecs"] = vecs
    return g


def kernel(**inputs):
    import concourse.bacc as _bacc
    from concourse.bass_utils import run_bass_kernel_spmd as _run

    nc = _bacc.Bacc("TRN2", target_bir_lowering=False, num_devices=1)
    laid = lay_out({k: np.asarray(v) for k, v in inputs.items()})
    arrays, args = {}, []
    for name in _INS:
        a = np.ascontiguousarray(laid[name])
        arrays[f"in_{name}"] = a
        args.append(nc.dram_tensor(f"in_{name}", a.shape, mybir.dt.from_np(a.dtype), kind="ExternalInput").ap())
    for i, (shape, dtype) in enumerate(_OUTS):
        args.append(nc.dram_tensor(f"out_{i}", shape, mybir.dt.from_np(np.dtype(dtype)), kind="ExternalOutput").ap())
    program(nc, *args)
    r = _run(nc, [arrays], core_ids=[0])
    return r.results[0]["out_0"][:B * L].reshape(B, L, DM)
```

```python
import numpy as np
import concourse.bass as bass
from concourse import mybir

F32 = mybir.dt.float32
F32R = mybir.dt.float32r
BF16 = mybir.dt.bfloat16
I32 = mybir.dt.int32
U32 = mybir.dt.uint32
ALU = mybir.AluOpType
ACT = mybir.ActivationFunctionType
AX = mybir.AxisListType

P = 128
B, L, DM = 4, 512, 512
DC = 256
KC = DC // P
KT = DM // P
LT = L // P
DS, DR, TAPS = 16, 16, 4
H, HD = 16, 32
HPT = P // HD
DCA = 16
MAIN = L - DCA
LN_EPS, QK_EPS = 1e-5, 1e-6
QK_SCALE = HD ** -0.5
TH_X, TH_W, SC_X, SC_W = 0.33, 0.2, 0.5, 0.6

NE, TOPK, FE, FS = 32, 6, 192, 384
FH = FE // 2
NT = B * LT
BLK = 256
NBLK = 79
assert (NT * P * TOPK + NE * (BLK - 1)) // BLK <= NBLK
NSLOT = NBLK * BLK

VEC = {}
_at = 0
for _name, _n in (("conv_w", KT * TAPS), ("conv_b", KT), ("dt_b", KT), ("A_log", KT * DS), ("D", KT),
                  ("bq", KT), ("bk", KT), ("bkd", KT), ("bv", KT), ("bvd", KT),
                  ("qw", 1), ("qb", 1), ("kw", 1), ("kb", 1), ("kdw", 1), ("kdb", 1), ("gates", 4)):
    VEC[_name] = (_at, _at + _n)
    _at += _n
NVEC = _at


ENDS, HALF = (0, DS - 2, DS - 1), 2
K_THEN_Q = [4, 5, 6, 7, 0, 1, 2, 3]


class Signal:

    def __init__(self, sem, per, first=0):
        self.sem, self.per, self.first = sem, per, first

    def at(self, b, n):
        return b * self.per + (self.first + n)


class Order:

    def __init__(self, eng, sem, per):
        self.eng, self.sem, self.per = eng, sem, per
        self.first = self.n = 0
        self.b = None

    def enter(self, b):
        self.first, self.n, self.b = self.n, 0, b

    def leave(self):
        assert self.n == self.per, (self.sem, self.n, self.per)
        self.first, self.n, self.b = self.first + self.per * B, 0, None

    def mark(self, ins):
        ins.then_inc(self.sem, 1)
        self.n += 1
        return self.n

    def wait(self, n=None):
        n = self.n if n is None else n
        value = self.first + n if self.b is None else self.b * self.per + (self.first + n)
        self.eng.wait_ge(self.sem, value)

DVE_STEPS = 51
ACT_STEPS = 2


def program(nc, x, ctxT, vecs, w_in, w_xp, w_dt, ffn_w, ffn_r, w_q, w_k, w_v, w_kd, w_vd, w_o, b_o, w_g, w_sh, w_sd,
            w_gu, w_dn, out):
    def sb(name, shape, dt=F32):
        return nc.alloc_sbuf_tensor(name, shape, dt)

    def sem(name):
        return nc.alloc_semaphore(name)

    X = sb("X", [P, B * LT, DM])
    ps = nc.alloc_psum_tensor("ps", [P, 8, 512], F32)
    ctx = sb("ctx", [P, KC, L])
    V_ = sb("vecs_sb", [P, NVEC])
    region = sb("region", [P, 12288])

    def carve(at, *shape):
        n = int(np.prod(shape))
        v = region[:, at:at + n]
        if len(shape) == 2:
            v = v.rearrange("p (a c) -> p a c", c=shape[1])
        elif len(shape) == 3:
            v = v.rearrange("p (a t c) -> p a t c", t=shape[1], c=shape[2])
        return v

    Win, Wk, Wv, Wkd, Wvd = (carve(1024 * i, KC, DM) for i in range(5))
    Wq, Wo = carve(5120, KT, DM), carve(7168, KT, DM)
    W3 = region[:, 9216:12288].bitcast(BF16).rearrange("p (a t c) -> p a t c", a=3, t=KT)
    wgu = carve(0, 2, KT, 2 * FE)
    wdn = carve(3072, 2, 2, DM)
    G = carve(5120, 2, 2, DM)
    Yb = carve(9216, 2, 2, DM)
    Wxp = sb("Wxp", [P, KT, DR + 2 * DS])
    Wdt = sb("Wdt", [DR, DM])
    bo = sb("bo", [1, DM])
    Wg = sb("Wg", [P, KT, NE])
    ident = sb("ident", [P, P])
    identb = sb("identb", [P, P], BF16)
    ones1 = sb("ones1", [1, P])
    negA = sb("negA", [P, KT * DS])
    tg = sb("tg", [P, 4])
    eps = sb("eps", [P, 2])
    headmean = sb("headmean", [P, P])
    headvar = sb("headvar", [P, 8, 32])
    headrow = sb("headrow", [32, 8, P], F32R)
    bvsum = sb("bvsum", [P, KT])
    qkbias = sb("qkbias", [P, 3 * KT])
    aff = sb("aff", [P, 6])
    wsum = sb("wsum", [P, (KT + 2 * KC) * H])
    st6 = sb("st6", [P, LT, 6])
    mv = sb("mv", [P, LT, 2])
    std = sb("std", [P, LT])
    rstd = sb("rstd", [P, LT])
    nmr = sb("nmr", [P, LT])
    XD = sb("XD", [DR + 2 * DS, L])
    XDr = sb("XDr", [DR + 2 * DS, 2, L], F32R)
    Cr = sb("Cr", [P, 2, L])
    identr = sb("identr", [P, P], F32R)
    sdr = sb("sdr", [32, L])
    rrow = sb("rrow", [32, L])
    mv4 = sb("mv4", [P, B * LT, 2])
    table_scratch = sb("table_scratch", [1, 16])
    std4, rstd4, nmr4 = (sb(n, [P, B * LT]) for n in ("std4", "rstd4", "nmr4"))
    nm = sb("nm", [P, 2, 4])
    esum = sb("prob_sums", [P, 2, 4])
    escale = sb("prob_scale", [P, 2, 4])
    arena_offset = nc.sbuf_base
    arena = sb("arena", [P, 11, KT, L])
    arena_bytes = 11 * KT * L * 4
    assert nc.sbuf_base == arena_offset + arena_bytes
    siluz, U, delta, du = (arena[:, i] for i in range(4))
    conv = du
    xpad = arena[:, 4:6].rearrange("p a t l -> p (a t l)")[:, 0:KT * 516].rearrange("p (e l) -> p e l", l=516)
    dA = [arena[:, 4], arena[:, 5]]
    dBu = [arena[:, 6], arena[:, 7]]
    hs = [arena[:, 8], arena[:, 9], arena[:, 10]]
    sp_abs, sp_exp, sp_relu, sp_ln = dBu[0], dBu[1], hs[0], hs[1]
    yt, yz = dBu[0], dBu[1]
    xn, gt = arena[:, 0], arena[:, 1]
    tern = arena[:, 2].bitcast(BF16)[:, 0:2].rearrange("p a (t l) -> p (a t) l", l=L)
    ternT = arena[:, 3].bitcast(BF16)[:, 0:2].rearrange("p a (t l) -> p (a t) l", l=L)
    xnT = arena[:, 1]
    qk = arena[:, 2:4].rearrange("p a t l -> p (a t) l")
    sq = arena[:, 4:6].rearrange("p a t l -> p (a t) l")
    Vn = arena[:, 6]
    Pr = arena[:, 7].rearrange("p (s q) l -> p s q l", s=2)
    PT = arena[:, 8].rearrange("p (s q) l -> p s q l", s=2)
    ctxnT = arena[:, 10]
    headrow_f = arena[0:32, 10].rearrange("r t l -> r (t l)")[:, 0:8 * P].rearrange("r (i c) -> r i c", i=8)
    rrow_parts = nc.alloc_sbuf_tensor_at("rrow_parts", [32, 2, L], F32R, offset=arena_offset + 9 * KT * L * 4)
    wtmp = [arena[:, i] for i in range(4)]

    HT = arena[:, 0:4].rearrange("p k t l -> p k (t l)")
    hn = [arena[:, 4], arena[:, 9]]
    Wsh = arena[:, 5:7].rearrange("p a t l -> p (a t l)")[:, 0:KT * 2 * FS].rearrange("p (k f) -> p k f", k=KT)
    Wsd = arena[:, 7, 0:3]
    sil, aS = arena[:, 8, 0:3], arena[:, 9, 0:3]
    pick = region[:, 0:TOPK * NT * NE].rearrange("p (j t e) -> p j t e", t=NT, e=NE)
    SC = arena[:, 10, 0].rearrange("p (t e) -> p t e", e=NE)
    msum = arena[:, 10, 1].rearrange("p (t e) -> p t e", e=NE)
    pair_sums = [region[:, 3072 + 512 * j:3584 + 512 * j].rearrange("p (t e) -> p t e", e=NE) for j in range(TOPK // 2)]
    slot = arena[:, 10, 2].rearrange("p (t e) -> p t e", e=NE)
    tot = arena[:, 9, 3].rearrange("p (e t) -> p e t", t=NT)
    cum = arena[:, 8, 3].rearrange("p (e t) -> p e t", t=NT)
    spare = arena[:, 5:7].rearrange("p a t l -> p (a t l)")[:, KT * 2 * FS:]
    Mb = spare[:, 0:NT * NE // 2].bitcast(BF16)
    top, topi, topf = (spare[:, n:n + NT * 8].rearrange("p (t e) -> p t e", e=8) for n in (512, 640, 768))
    topi = topi.bitcast(U32)
    lists = arena[:, 7, 3]
    slots_f = lists[:, 0:TOPK * NT].rearrange("p (j t) -> p j t", t=NT)
    slots = lists[:, 128:128 + TOPK * NT].rearrange("p (j t) -> p j t", t=NT).bitcast(I32)
    slot_p = spare[:, 896:896 + TOPK * NT].rearrange("p (j t) -> p j t", t=NT).bitcast(I32)
    pairs = lists[:, 256:256 + 2 * TOPK * NT].rearrange("p (t j c) -> p t j c", j=TOPK, c=2).bitcast(I32)
    den = sb("den", [P, NT])
    keep = sb("keep", [P, NE, NT])
    iota_i = sb("iota_i", [P, NE], I32)
    iota_f = sb("iota_f", [P, NE])
    blk_i = sb("blk_i", [1, NBLK], I32)
    blk_f = sb("blk_f", [1, NBLK])
    tri_f = sb("tri_f", [P, P])
    tri = sb("tri", [P, P], BF16)
    onesb = sb("onesb", [P, P], BF16)
    nb_f = sb("nb_f", [P, NE])
    nb_i = sb("nb_i", [P, NE], I32)
    end_b = sb("end_b", [P, NE])
    start_b = sb("start_b", [P, NE])
    ones_e = sb("ones_e", [P, NE])
    tok_i = sb("tok_i", [P, NT], I32)
    le = region[0:1, 0:NBLK * NE].rearrange("p (n e) -> p n e", e=NE)
    expert_f = sb("expert_f", [1, NBLK])
    expert_i = sb("expert_i", [1, NBLK], I32)
    meta = sb("meta", [P, NSLOT // P, 2], I32)
    gidx = sb("gidx", [P, 2, 2, 2], I32)
    aidx = sb("aidx", [P, 2, 2], I32)
    arena_flat = arena[:, :, :, :].rearrange("p s t l -> p (s t l)")
    act_s = arena_flat[:, 0:2 * FE].rearrange("p (q f) -> p q f", q=2)
    act_m = arena_flat[:, 512:512 + 2 * FE].rearrange("p (q f) -> p q f", q=2)
    parts_at = arena_offset + 4096

    def two_parts(name, rows, buffers, tiles, n):
        nonlocal parts_at
        t = nc.alloc_sbuf_tensor_at(name, [rows, buffers, 2, tiles, n], F32R, offset=parts_at)
        parts_at += buffers * 2 * tiles * n * 4
        assert parts_at <= arena_offset + arena_bytes
        return t

    GTp = two_parts("GTp", P, 1, KT, BLK)
    wgup = two_parts("wgup", P, 2, KT, 2 * FE)
    wdnp = two_parts("wdnp", FH, 2, 2, DM)
    aTp = two_parts("aTp", FH, 1, 2, BLK)
    Hd = nc.dram_tensor("Hd", [NT * P + BLK, DM], F32, kind="Internal").ap()
    listd = nc.dram_tensor("listd", [NSLOT, 2], I32, kind="Internal").ap()

    ln4_std, ln4_coef = sem("ln4_std"), sem("ln4_coef")
    hn_ready, hT_ready = (Signal(sem(n), LT) for n in ("hn_ready", "hT_ready"))
    hT_sb = Signal(sem("hT_sb"), LT)
    h_stored = [Signal(sem(f"h_stored{u}"), 16 * LT) for u in range(2)]
    setup_iota, zero_ready, list_filled = (sem(n) for n in ("setup_iota", "zero_ready", "list_filled"))
    logits_ready, sc_ready, mask_ready, prefix_ready, slots_ready, scattered, meta_loaded, expert_ready = (
        sem(n) for n in ("logits_ready", "sc_ready", "mask_ready", "prefix_ready", "slots_ready", "scattered",
                         "meta_loaded", "expert_ready"))
    sh_loaded = sem("sh_loaded")
    shg_ready, sil_ready, aS_ready = (Signal(sem(n), 3) for n in ("shg_ready", "sil_ready", "aS_ready"))
    shy_ready, shx_done = (Signal(sem(n), LT) for n in ("shy_ready", "shx_done"))
    out_stored, zeros_stored = sem("out_stored"), sem("zeros_stored")
    wgu_loaded = [sem(f"wgu_loaded{u}") for u in range(2)]
    wdn_loaded = [sem(f"wdn_loaded{u}") for u in range(2)]
    gathered = [sem(f"gathered{u}") for u in range(2)]
    gt_ready, gt_hi, gt_lo, gu_ready, silu_done, act_done, at_ready, at_hi, at_lo, y_ready, y_a, y_d, gidx_ready = (
        sem(n) for n in ("gt_ready", "gt_hi", "gt_lo", "gu_ready", "silu_done", "act_done", "at_ready", "at_hi", "at_lo", "y_ready",
                         "y_a", "y_d", "gidx_ready"))
    wgu_hi, wgu_lo, wdn_hi, wdn_lo = (sem(n) for n in ("wgu_hi", "wgu_lo", "wdn_hi", "wdn_lo"))
    added = sem("added")
    prep_order = sem("prep_order")
    aidx_ready = sem("aidx_ready")
    zero_rows = Yb[:, 1]

    def ds2(s):
        return bass.ds(2 * s, 2)

    def ds1(s):
        return bass.ds(s, 1)

    def ge(eng, s, value):
        if not (isinstance(value, int) and value <= 0):
            eng.wait_ge(s, value)

    def steps(eng, step, first, last):
        lo, hi = first + first % 2, last + 1 - (last + 1) % 2
        lo += 4
        hi -= 2
        for s in range(first, lo):
            step(s, s // 2, s % 2)
        with eng.Fori(lo // 2, hi // 2) as r:
            for u in range(2):
                step(2 * r + u, r, u)
        for s in range(hi, last + 1):
            step(s, s // 2, s % 2)

    setup_pool = sem("setup_pool")
    setup_act = sem("setup_act")
    setup_pe = sem("setup_pe")
    setup_dve = sem("setup_dve")
    batch_done = Signal(sem("batch_done"), 1, 1)
    ctx_loaded = Signal(sem("ctx_loaded"), 16)
    ctx_free = Signal(sem("ctx_free"), 1)
    ln_mv, ln_std, ln_coef = (Signal(sem(n), 3) for n in ("ln_mv", "ln_std", "ln_coef"))
    xi_ready, xpad_ready, conv_ready, u_ready, sp_abs_ready = (Signal(sem(n), KT) for n in ("xi_ready", "xpad_ready", "conv_ready", "u_ready", "sp_abs_ready"))
    siluz_ready = Signal(sem("siluz_ready"), LT)
    xd_ready, xd_sb, xdr_ready, dt_ready, sp_ready, delta_ready = (Signal(sem(n), 1) for n in ("xd_ready", "xd_sb", "xdr_ready", "dt_ready", "sp_ready", "delta_ready"))
    dA_ready, b_ready, c_ready, b_used, scan_done, c_sb, hc_ready, hc_used = (
        Signal(sem(n), DS) for n in ("dA_ready", "b_ready", "c_ready", "b_used", "scan_done", "c_sb", "hc_ready", "hc_used"))
    hc_half = Signal(sem("hc_half"), len(ENDS))
    yz_ready = Signal(sem("yz_ready"), KT)
    yt_ready = Signal(sem("yt_ready"), 1)
    tern_ready = Signal(sem("tern_ready"), LT)
    ternT_ready, ternT_sb, ffn_ready = (Signal(sem(n), LT) for n in ("ternT_ready", "ternT_sb", "ffn_ready"))
    xn_ready, xT_ready, xT_sb = (Signal(sem(n), LT) for n in ("xn_ready", "xT_ready", "xT_sb"))
    proj_ready, qc_ready, sq_ready, rb_ready, rb_used, qk_final = (
        Signal(sem(n), 8) for n in ("proj_ready", "qc_ready", "sq_ready", "rb_ready", "rb_used", "qk_final"))
    var_ready, std_ready, rrow_ready, v_ready, v_sb = (Signal(sem(n), 1) for n in ("var_ready", "std_ready", "rrow_ready", "v_ready", "v_sb"))
    NIT = 2 * H
    s_ready, nm_ready, p_raw, scale_ready, p_final, p_final1, t_ready, pt_d, pt_a, pv_done = (
        Signal(sem(n), NIT) for n in ("s_ready", "nm_ready", "p_raw", "scale_ready", "p_final", "p_final1", "t_ready", "pt_d", "pt_a", "pv_done"))
    cT_sb, o_ready = (Signal(sem(n), LT) for n in ("cT_sb", "o_ready"))
    dve_order, act_order = sem("dve_order"), sem("act_order")
    act_passed, dve_passed, pool_passed = sem("act_passed"), sem("dve_passed"), sem("pool_passed")

    def vec(name, i=0, n=1):
        return V_[:, VEC[name][0] + i:VEC[name][0] + i + n]

    vecs_loaded, ffn_loaded, wqk_loaded, mixer_loaded, loaded = (
        sem(n) for n in ("vecs_loaded", "ffn_loaded", "wqk_loaded", "mixer_loaded", "loaded"))
    first_loads = [
        (V_[:, :], vecs, vecs_loaded), (wtmp[0], ffn_w, ffn_loaded), (wtmp[1], ffn_r, ffn_loaded),
        (Wq[:, :, :], w_q, wqk_loaded), (Wk[:, :, :], w_k, wqk_loaded), (Wkd[:, :, :], w_kd, wqk_loaded),
        (Win[:, :, :], w_in, mixer_loaded), (Wxp[:, :, :], w_xp, mixer_loaded), (Wdt[:, :], w_dt, mixer_loaded),
        (ctx[:, :, :], ctxT[0], ctx_loaded.sem)]
    loads = [
        (X[:, 0:LT, :], x[0:L, :].rearrange("(t p) d -> p t d", p=P)),
        (X[:, LT:, :], x[L:, :].rearrange("(t p) d -> p t d", p=P)),
        (Wv[:, :, :], w_v), (Wvd[:, :, :], w_vd), (Wo[:, :, :], w_o), (bo[:, :], b_o), (Wg[:, :, :], w_g),
    ]

    centred = ((Wq, KT, 0), (Wk, KC, KT * H), (Wkd, KC, (KT + KC) * H))
    means_ready, centred_ready = sem("means_ready"), sem("centred_ready")

    def by_head(W):
        return W[:, :, :].rearrange("p k (h d) -> p (k h) d", d=HD)

    with nc.Block() as block:
        @block.sync
        def _(sp):
            for dst, src, done in first_loads:
                sp.dma_start(dst, src).then_inc(done, 16)
            for dst, src in loads:
                sp.dma_start(dst, src).then_inc(loaded, 16)
            with sp.Fori(1, B) as b:
                sp.wait_ge(ctx_free.sem, ctx_free.at(b, 0))
                sp.dma_start(ctx[:, :, :], ctxT[b]).then_inc(ctx_loaded.sem, 16)
            sp.wait_ge(setup_iota, 1)
            sp.dma_start(listd.rearrange("(p n) c -> p n c", p=P), meta[:, :, :]).then_inc(list_filled, 16)
            sp.wait_ge(batch_done.sem, B + 1)
            sp.dma_start(Wsh, w_sh).then_inc(sh_loaded, 16)
            sp.dma_start(Wsd, w_sd).then_inc(sh_loaded, 16)
            sp.wait_ge(zero_ready, 1)
            sp.dma_start(Hd[NT * P:NT * P + BLK, :].rearrange("(a p) d -> p a d", p=P), zero_rows).then_inc(zeros_stored, 16)
            sp.dma_start(out[NT * P:NT * P + BLK, :].rearrange("(a p) d -> p a d", p=P), zero_rows).then_inc(zeros_stored, 16)
            with sp.Fori(0, B // 2) as r:
                for u in range(2):
                    b = 2 * r + u
                    for t in range(LT):
                        sp.wait_ge(hn_ready.sem, hn_ready.at(b, t + 1))
                        sp.dma_start(Hd.rearrange("(t p) d -> t p d", p=P)[b * LT + t], hn[u][:, t])\
                            .then_inc(h_stored[u].sem, 16)
            with sp.Fori(0, B) as b:
                for t in range(LT):
                    sp.wait_ge(shx_done.sem, shx_done.at(b, t + 1))
                    sp.dma_start(out[0:NT * P, :].rearrange("(t p) d -> t p d", p=P)[b * LT + t], X[:, b * LT + t, :])\
                        .then_inc(out_stored, 16)
            sp.wait_ge(expert_ready, 1)

            def load_weights(s, r, u):
                e = sp.value_load(expert_i[0:1, ds1(s)], min_val=0, max_val=NE - 1)
                ge(sp, wgu_lo, s - 1)
                sp.dma_start(wgu[:, u], w_gu[e]).then_inc(wgu_loaded[u], 16)
                ge(sp, wdn_lo, s - 1)
                sp.dma_start(wdn[0:FH, u], w_dn[e]).then_inc(wdn_loaded[u], 16)

            for s in range(2):
                load_weights(s, 0, s)
            sp.wait_ge(scattered, 16 * NT * TOPK)
            sp.dma_start(meta[:, :, :], listd.rearrange("(p n) c -> p n c", p=P)).then_inc(meta_loaded, 16)
            steps(sp, load_weights, 2, NBLK - 1)
            sp.wait_ge(added, 16 * 2 * NBLK)

        @block.gpsimd
        def _(pool):
            pool.memset(ident[:, :], 0.0).then_inc(setup_pool, 1)
            pool.memset(ones1[:, :], 1.0)
            pool.memset(eps[:, 0:1], LN_EPS)
            pool.memset(eps[:, 1:2], QK_EPS)
            pool.memset(headrow_f, 0.0).then_inc(setup_pool, 1)
            pool.wait_ge(setup_pool, 2)
            pool.affine_select(out=ident[:, :], in_=ident[:, :], compare_op=ALU.not_equal, fill=1.0, base=0,
                               pattern=[[-1, P]], channel_multiplier=1)
            hr = headrow_f.rearrange("r i (j c) -> r i j c", c=HD)
            pool.affine_select(out=hr, in_=hr, compare_op=ALU.not_equal, fill=1.0, base=0,
                               pattern=[[-HPT, 8], [-1, HPT], [0, HD]], channel_multiplier=1).then_inc(setup_pool, 1)
            pool.wait_ge(setup_pool, 3)
            pool.tensor_copy(identr[:, :], ident[:, :])
            pool.tensor_copy(headrow[:, :, :], headrow_f)
            pool.tensor_copy(identb[:, :], ident[:, :]).then_inc(setup_pool, 1)

            pool.iota(iota_i[:, :], pattern=[[1, NE]], base=0, channel_multiplier=0)
            pool.iota(blk_i[:, :], pattern=[[1, NBLK]], base=0, channel_multiplier=0)
            pool.iota(tok_i[:, :], pattern=[[P, NT]], base=0, channel_multiplier=1)
            pool.iota(meta[:, :, 0].rearrange("p (n q) -> p n q", q=2), pattern=[[0, NBLK], [P, 2]], base=NT * P,
                      channel_multiplier=1)
            pool.memset(meta[:, :, 1], 0)
            pool.memset(onesb[:, :], 1.0)
            pool.memset(ones_e[:, :], 1.0)
            pool.memset(keep[:, :, :], 1.0)
            pool.memset(tri_f[:, :], 1.0).then_inc(setup_iota, 1)
            pool.wait_ge(setup_iota, 1)
            pool.memset(keep[:, :, 0:1], 0.0)
            pool.affine_select(out=tri_f[:, :], in_=tri_f[:, :], compare_op=ALU.is_gt, fill=0.0, base=0,
                               pattern=[[1, P]], channel_multiplier=-1).then_inc(setup_iota, 1)
            for m, (W, kt, at) in enumerate(centred):
                pool.wait_ge(means_ready, m + 1)
                pool.tensor_tensor(by_head(W), by_head(W), wsum[:, at:at + kt * H].unsqueeze(2).to_broadcast([P, kt * H, HD]),
                                   ALU.subtract).then_inc(centred_ready, 1)
            with pool.Fori(0, B) as b:
                for n in range(DS):
                    pool.wait_ge(c_sb.sem, c_sb.at(b, n + 1))
                    pool.wait_ge(scan_done.sem, scan_done.at(b, n + 1))
                    e = HALF if n in ENDS else 0
                    pool.tensor_tensor(hs[n % 3][:, e:], hs[n % 3][:, e:],
                                       Cr[:, n % 2, :].unsqueeze(1).to_broadcast([P, KT - e, L]),
                                       ALU.mult).then_inc(hc_ready.sem, 1)
                for it in range(NIT):
                    s = it % 2
                    pool.wait_ge(scale_ready.sem, scale_ready.at(b, it + 1))
                    pool.tensor_tensor(Pr[:, s, 1, 0:MAIN], Pr[:, s, 1, 0:MAIN],
                                       escale[:, s, 1:2].to_broadcast([P, MAIN]), ALU.mult).then_inc(p_final1.sem, 1)
            pool.wait_ge(list_filled, 16)
            pool.wait_ge(slots_ready, 1)
            for t in range(NT):
                for j in range(TOPK):
                    pool.indirect_dma_start(listd, bass.IndirectOffsetOnAxis(slots[:, j, t:t + 1].bitcast(U32), 0), pairs[:, t, j, :], None)\
                        .then_inc(scattered, 16)
            pool.wait_ge(meta_loaded, 16)
            for u in range(2):
                pool.wait_ge(h_stored[u].sem, h_stored[u].at(B // 2, 0))
            pool.wait_ge(zeros_stored, 32)

            def settle():
                pool.sem_inc(pool_passed, 1)

            def gather(s, u, r):
                ge(pool, gt_ready, s - 1)
                ge(pool, gathered[u], 32 * r)
                pool.tensor_copy(gidx[:, u, :, 0], meta[:, ds2(s), 0]).then_inc(gidx_ready, 1)
                pool.wait_ge(gidx_ready, s + 1)
                settle()
                for q in range(2):
                    pool.indirect_dma_start(G[:, u, q], None, Hd, bass.IndirectOffsetOnAxis(gidx[:, u, q, 0:1].bitcast(U32), 0))\
                        .then_inc(gathered[u], 16)

            def block_dmas(s, r, u):
                if not isinstance(s, int) or 1 < s + 1 < NBLK:
                    gather(s + 1, 1 - u, r if u == 0 else r + 1)
                if not isinstance(s, int) or s >= 2:
                    add(s - 2, u)

            def add(s, u):
                ge(pool, added, 32 * s)
                pool.tensor_copy(aidx[:, :, 0], meta[:, ds2(s), 0]).then_inc(aidx_ready, 1)
                pool.wait_ge(aidx_ready, s + 1)
                pool.wait_ge(y_d, s + 1)
                pool.wait_ge(y_a, s + 1)
                settle()
                for q in range(2):
                    pool.indirect_dma_start(out, bass.IndirectOffsetOnAxis(aidx[:, q, 0:1].bitcast(U32), 0), Yb[:, u, q], None,
                                            compute_op=ALU.add).then_inc(added, 16)

            gather(0, 0, 0)
            gather(1, 1, 0)
            pool.wait_ge(out_stored, 16 * NT)
            steps(pool, block_dmas, 0, NBLK - 1)
            for s in range(NBLK - 2, NBLK):
                add(s, s % 2)

        @block.scalar
        def _(act):
            order = Order(act, act_order, ACT_STEPS)
            act.wait_ge(vecs_loaded, 16)
            act.wait_ge(setup_pool, 4)
            act.activation(tg[:, :], vec("gates", 0, 4), ACT.Tanh)
            act.activation(negA[:, :], vec("A_log", 0, KT * DS), ACT.Exp).then_inc(setup_act, 1)

            def settle():
                act.sem_inc(act_passed, 1)

            warmed = [0]

            def load_table(func):
                i = warmed[0]
                warmed[0] += 1
                act.activation(table_scratch[:, i:i + 1], eps[0:1, 0:1], func)

            def ln_root(b, k):
                act.wait_ge(ln_mv.sem, ln_mv.at(b, k + 1))
                act.activation(std[:, :], mv[:, :, 1], ACT.Sqrt, bias=eps[:, 0:1]).then_inc(ln_std.sem, 1)

            with act.Fori(0, B) as b:
                order.enter(b)
                for e in range(KT):
                    act.wait_ge(xi_ready.sem, xi_ready.at(b, e + 1))
                    act.activation(xpad[:, e, 3:3 + L], ps[:, e, :], ACT.Copy).then_inc(xpad_ready.sem, 1)
                load_table(ACT.Silu)
                for e in range(KT):
                    act.wait_ge(conv_ready.sem, conv_ready.at(b, e + 1))
                    act.activation(U[:, e], conv[:, e], ACT.Silu, bias=vec("conv_b", e)).then_inc(u_ready.sem, 1)
                load_table(ACT.Exp)
                act.wait_ge(dt_ready.sem, dt_ready.at(b, 1))
                for e in range(KT):
                    act.activation(sp_abs[:, e], ps[:, e, :], ACT.Abs, bias=vec("dt_b", e)).then_inc(sp_abs_ready.sem, 1)
                act.wait_ge(sp_abs_ready.sem, sp_abs_ready.at(b, KT))
                order.mark(act.activation(sp_exp, sp_abs, ACT.Exp, scale=-1.0))
                order.wait()
                act.activation(sp_ln, sp_exp, ACT.Ln, bias=1.0).then_inc(sp_ready.sem, 1)
                load_table(ACT.Exp)
                act.wait_ge(delta_ready.sem, delta_ready.at(b, 1))
                for n in range(DS):
                    if n >= 2:
                        act.wait_ge(scan_done.sem, scan_done.at(b, n - 1))
                    for e in range(KT):
                        i = act.activation(dA[n % 2][:, e, 1:L], delta[:, e, 1:L], ACT.Exp,
                                           scale=negA[:, e * DS + n:e * DS + n + 1])
                    i.then_inc(dA_ready.sem, 1)
                    act.wait_ge(c_ready.sem, c_ready.at(b, n + 1))
                    if n >= 2:
                        act.wait_ge(hc_ready.sem, hc_ready.at(b, n - 1))
                    if n - 2 in ENDS:
                        act.wait_ge(hc_half.sem, hc_half.at(b, ENDS.index(n - 2) + 1))
                    act.activation(Cr[:, n % 2, :], ps[:, 6 + n % 2, :], ACT.Copy).then_inc(c_sb.sem, 1)
                ln_root(b, 0)
                load_table(ACT.Silu)
                act.wait_ge(ln_coef.sem, ln_coef.at(b, 1))
                settle()
                for t in range(LT):
                    act.activation(siluz[:, t], X[:, b * LT + t, :], ACT.Silu, bias=nmr[:, t:t + 1],
                                   scale=rstd[:, t:t + 1]).then_inc(siluz_ready.sem, 1)
                load_table(ACT.Sqrt)
                ln_root(b, 1)
                for t in range(LT):
                    act.wait_ge(ternT_ready.sem, ternT_ready.at(b, t + 1))
                    act.activation(ternT[:, :, t * P:(t + 1) * P],
                                   ps[:, t, :].bitcast(BF16)[:, 0:DM].rearrange("p (k l) -> p k l", k=KT),
                                   ACT.Copy).then_inc(ternT_sb.sem, 1)
                ln_root(b, 2)
                act.wait_ge(ln_coef.sem, ln_coef.at(b, 3))
                settle()
                for t in range(LT):
                    act.activation(xn[:, t], X[:, b * LT + t, :], ACT.Identity, bias=nmr[:, t:t + 1],
                                   scale=rstd[:, t:t + 1]).then_inc(xn_ready.sem, 1)
                for n, i in enumerate(K_THEN_Q):
                    act.wait_ge(proj_ready.sem, proj_ready.at(b, n + 1))
                    bank = (4 + i) % 8
                    if i < KT:
                        act.activation(qk[:, i], ps[:, bank, :], ACT.Identity,
                                       bias=qkbias[:, i:i + 1]).then_inc(qc_ready.sem, 1)
                    else:
                        act.activation(qk[:, i, 0:MAIN], ps[:, bank, 0:MAIN], ACT.Identity, bias=qkbias[:, i:i + 1])
                        act.activation(qk[:, i, MAIN:L], ps[:, bank, MAIN:L], ACT.Identity,
                                       bias=qkbias[:, i + KT:i + KT + 1]).then_inc(qc_ready.sem, 1)
                act.wait_ge(var_ready.sem, var_ready.at(b, 1))
                act.activation(sdr[:, :], ps[0:32, 4, :], ACT.Sqrt, bias=eps[0:32, 1:2]).then_inc(std_ready.sem, 1)
                load_table(ACT.Exp)
                act.wait_ge(v_ready.sem, v_ready.at(b, 1))
                for j in range(LT - 1):
                    act.activation(Vn[:, j], ps[:, j, :], ACT.Copy)
                order.mark(act.activation(Vn[96:128, 3], ps[96:128, 5, :], ACT.Copy))
                order.wait()
                act.activation(Vn[0:MAIN - 3 * P, 3], ps[0:MAIN - 3 * P, 3, :], ACT.Copy).then_inc(v_sb.sem, 1)
                for i in range(8):
                    act.wait_ge(rb_used.sem, rb_used.at(b, i + 1))
                    if i < KT:
                        act.activation(qk[:, i], qk[:, i], ACT.Identity, bias=aff[:, 1:2]).then_inc(qk_final.sem, 1)
                    else:
                        act.activation(qk[:, i, 0:MAIN], qk[:, i, 0:MAIN], ACT.Identity, bias=aff[:, 3:4])
                        act.activation(qk[:, i, MAIN:L], qk[:, i, MAIN:L], ACT.Identity,
                                       bias=aff[:, 5:6]).then_inc(qk_final.sem, 1)

                def exps(it):
                    qp, h = divmod(it, H)
                    s = it % 2
                    act.wait_ge(nm_ready.sem, nm_ready.at(b, it + 1))
                    if it >= 2:
                        act.wait_ge(t_ready.sem, t_ready.at(b, it - 1))
                    for q in range(2):
                        bank = 2 * s + q
                        act.activation(Pr[:, s, q, 0:MAIN], ps[:, bank, 0:MAIN], ACT.Exp, bias=nm[:, s, q:q + 1],
                                       accum_out=esum[:, s, q:q + 1])
                        i = act.activation(Pr[:, s, q, MAIN:L], ps[:, bank, MAIN:L], ACT.Exp,
                                           bias=nm[:, s, 2 + q:3 + q], accum_out=esum[:, s, 2 + q:3 + q])
                    i.then_inc(p_raw.sem, 1)

                exps(0)
                exps(1)
                for it in range(NIT):
                    act.wait_ge(t_ready.sem, t_ready.at(b, it + 1))
                    if it >= 2:
                        act.wait_ge(pv_done.sem, pv_done.at(b, it - 1))
                    act.activation(PT[:, it % 2, 1], ps[:, 5, :], ACT.Copy).then_inc(pt_a.sem, 1)
                    if it + 2 < NIT:
                        exps(it + 2)
            order.leave()

            act.wait_ge(batch_done.sem, B + 1)
            act.activation(std4[:, :], mv4[:, :, 1], ACT.Sqrt, bias=eps[:, 0:1]).then_inc(ln4_std, 1)
            act.wait_ge(ln4_coef, 1)

            def norm(b, u):
                for t in range(LT):
                    act.activation(hn[u][:, t], X[:, b * LT + t, :], ACT.Identity, bias=nmr4[:, bass.ds(b * LT + t, 1)],
                                   scale=rstd4[:, bass.ds(b * LT + t, 1)]).then_inc(hn_ready.sem, 1)

            for b in range(2):
                norm(b, b)
            with act.Fori(1, B // 2) as r:
                for u in range(2):
                    b = 2 * r + u
                    act.wait_ge(hT_sb.sem, hT_sb.at(b, 0) - LT)
                    act.wait_ge(h_stored[u].sem, h_stored[u].at(r, 0))
                    settle()
                    norm(b, u)
            load_table(ACT.Sigmoid)
            act.wait_ge(logits_ready, 1)
            act.activation(SC.rearrange("p t e -> p (t e)"), ps[:, 7, :], ACT.Sigmoid).then_inc(sc_ready, 1)
            load_table(ACT.Silu)
            with act.Fori(0, B) as c:
                for m in range(3):
                    act.wait_ge(shg_ready.sem, shg_ready.at(c, m + 1))
                    act.activation(sil[:, m], ps[:, 2 * m, :], ACT.Silu).then_inc(sil_ready.sem, 1)

            def block_act(s, r, u):
                if not isinstance(s, int) or s >= 1:
                    act.wait_ge(at_ready, s)
                    ge(act, y_ready, 2 * (s - 1))
                    act.activation(aTp[:, 0, 0], ps[0:FH, 4, :].rearrange("p (f l) -> p f l", f=2), ACT.Copy).then_inc(at_hi, 1)
                split_up(s + 1, r if u == 0 else r + 1, 1 - u)
                for q in range(2):
                    act.wait_ge(gu_ready, 2 * s + q + 1)
                    ge(act, act_done, 2 * (s - 1) + q + 1)
                    act.activation(act_s[:, q, :], ps[:, 2 + q, 0:FE], ACT.Silu).then_inc(silu_done, 1)
                    if q == 0:
                        act.wait_ge(wdn_loaded[u], 16 * (r + 1))
                        ge(act, y_ready, 2 * (s - 1))
                        act.activation(wdnp[:, u, 0], wdn[0:FH, u], ACT.Copy).then_inc(wdn_hi, 1)
                turned(s + 1)
                scaled(s - 1, 1 - u)

            def split_up(s, r, u):
                if isinstance(s, int) and s >= NBLK:
                    return
                act.wait_ge(wgu_loaded[u], 16 * (r + 1))
                ge(act, gu_ready, 2 * (s - 1))
                act.activation(wgup[:, u, 0], wgu[:, u], ACT.Copy).then_inc(wgu_hi, 1)

            def turned(s):
                if isinstance(s, int) and s >= NBLK:
                    return
                act.wait_ge(gt_ready, s + 1)
                ge(act, gu_ready, 2 * s)
                act.activation(GTp[:, 0, 0], ps[:, 0:2, :].rearrange("p a (k l) -> p (a k) l", k=2), ACT.Copy).then_inc(gt_hi, 1)

            def scaled(s, u):
                if isinstance(s, int) and s < 0:
                    return
                act.wait_ge(y_ready, 2 * (s + 1))
                ge(act, added, 32 * (s - 1))
                settle()
                act.activation(Yb[:, u, 1], ps[:, 6, :], ACT.Copy, scale=meta[:, bass.ds(2 * s + 1, 1), 1].bitcast(F32))\
                    .then_inc(y_a, 1)

            act.wait_ge(shx_done.sem, shx_done.at(B, 0))
            split_up(0, 0, 0)
            turned(0)
            steps(act, block_act, 0, NBLK - 1)
            act.wait_ge(at_ready, NBLK)
            act.wait_ge(y_ready, 2 * (NBLK - 1))
            act.activation(aTp[:, 0, 0], ps[0:FH, 4, :].rearrange("p (f l) -> p f l", f=2), ACT.Copy).then_inc(at_hi, 1)
            scaled(NBLK - 1, (NBLK - 1) % 2)

        @block.tensor
        def _(pe):
            pe.wait_ge(vecs_loaded, 16)
            pe.wait_ge(setup_pool, 4)
            pe.wait_ge(setup_dve, 1)
            pe.matmul(ps[:, 7, 0:3 * KT], headmean[:, :], vec("bq", 0, 3 * KT), start=True, stop=True).then_inc(setup_pe, 1)
            pe.wait_ge(mixer_loaded, 16 * 3)
            with pe.Fori(0, B) as b:
                pe.wait_ge(ctx_loaded.sem, ctx_loaded.at(b, 16))
                for e in range(KT):
                    for k in range(KC):
                        i = pe.matmul(ps[:, e, :], Win[:, k, e * P:(e + 1) * P], ctx[:, k, :], start=(k == 0), stop=(k == KC - 1))
                    i.then_inc(xi_ready.sem, 1)
                for k in range(KT):
                    pe.wait_ge(u_ready.sem, u_ready.at(b, k + 1))
                    i = pe.matmul(ps[0:DR + 2 * DS, 4, :], Wxp[:, k, :], U[:, k], start=(k == 0), stop=(k == KT - 1))
                i.then_inc(xd_ready.sem, 1)
                pe.wait_ge(xd_sb.sem, xd_sb.at(b, 1))
                for e in range(KT):
                    i = pe.matmul(ps[:, e, :], Wdt[:, e * P:(e + 1) * P], XD[0:DR, :], start=True, stop=True)
                i.then_inc(dt_ready.sem, 1)

                def spread(n, part, ready, used, bank):
                    if n >= 2:
                        pe.wait_ge(used.sem, used.at(b, n - 1))
                    row = identr[0:DR + 2 * DS, part + n:part + n + 1].to_broadcast([DR + 2 * DS, P])
                    pe.matmul(ps[:, bank + n % 2, :], row, XDr[:, 0, :], start=True, stop=False)
                    pe.matmul(ps[:, bank + n % 2, :], row, XDr[:, 1, :], start=False, stop=True).then_inc(ready.sem, 1)

                def spread_b(n):
                    spread(n, DR, b_ready, b_used, 4)

                def spread_c(n):
                    spread(n, DR + DS, c_ready, c_sb, 6)

                pe.wait_ge(xdr_ready.sem, xdr_ready.at(b, 1))
                spread_b(0)
                spread_b(1)
                spread_c(0)
                spread_b(2)
                for n in range(DS):
                    if n + 3 < DS:
                        spread_b(n + 3)
                    if n + 1 < DS:
                        spread_c(n + 1)
                    if n not in ENDS:
                        pe.wait_ge(hc_ready.sem, hc_ready.at(b, n + 1))
                    for e in range(KT):
                        if n in ENDS and e == 0:
                            pe.wait_ge(hc_half.sem, hc_half.at(b, ENDS.index(n) + 1))
                        if n in ENDS and e == HALF:
                            pe.wait_ge(hc_ready.sem, hc_ready.at(b, n + 1))
                        i = pe.matmul(ps[:, e, :], ident[:, :], hs[n % 3][:, e], start=(n == 0), stop=(n == DS - 1))
                    i.then_inc(hc_used.sem, 1)
                for e in range(KT):
                    pe.wait_ge(yz_ready.sem, yz_ready.at(b, e + 1))
                    for l in range(LT):
                        i = pe.transpose(ps[:, 4 + l, e * P:(e + 1) * P], yz[:, e, l * P:(l + 1) * P], ident[:, :])
                i.then_inc(yt_ready.sem, 1)

                for t in range(LT):
                    pe.wait_ge(tern_ready.sem, tern_ready.at(b, t + 1))
                    for k in range(KT):
                        i = pe.transpose(ps[:, t, :].bitcast(BF16)[:, k * P:(k + 1) * P], tern[:, t, k * P:(k + 1) * P],
                                         identb[:, :])
                    i.then_inc(ternT_ready.sem, 1)
                for t in range(LT):
                    pe.wait_ge(ternT_sb.sem, ternT_sb.at(b, t + 1))
                    for k in range(KT):
                        for part in range(3):
                            i = pe.matmul(ps[:, 4 + t, :], ternT[:, k, t * P:(t + 1) * P], W3[:, part, k, :],
                                          start=(k == 0 and part == 0), stop=(k == KT - 1 and part == 2))
                    i.then_inc(ffn_ready.sem, 1)

                pe.wait_ge(centred_ready, len(centred))
                pe.wait_ge(loaded, 16 * len(loads))
                for e in range(KT):
                    for k in range(KC):
                        pe.matmul(ps[:, e, 0:MAIN], Wk[:, k, e * P:(e + 1) * P], ctx[:, k, 0:MAIN], start=(k == 0),
                                  stop=(k == KC - 1))
                    for k in range(KC):
                        i = pe.matmul(ps[:, e, MAIN:L], Wkd[:, k, e * P:(e + 1) * P], ctx[:, k, MAIN:L],
                                      start=(k == 0), stop=(k == KC - 1))
                    i.then_inc(proj_ready.sem, 1)
                for t in range(LT):
                    pe.wait_ge(xn_ready.sem, xn_ready.at(b, t + 1))
                    for k in range(KT):
                        i = pe.transpose(ps[:, 4 + t, k * P:(k + 1) * P], xn[:, t, k * P:(k + 1) * P], ident[:, :])
                    i.then_inc(xT_ready.sem, 1)
                pe.wait_ge(xT_sb.sem, xT_sb.at(b, LT))
                for e in range(KT):
                    for k in range(KT):
                        i = pe.matmul(ps[:, 4 + e, :], Wq[:, k, e * P:(e + 1) * P], xnT[:, k], start=(k == 0),
                                      stop=(k == KT - 1))
                    i.then_inc(proj_ready.sem, 1)
                pe.wait_ge(qc_ready.sem, qc_ready.at(b, 5))
                for n, i8 in enumerate(K_THEN_Q):
                    pe.wait_ge(sq_ready.sem, sq_ready.at(b, n + 1))
                    i = pe.matmul(ps[0:32, 4, :], headvar[:, i8, :], sq[:, i8], start=(n == 0), stop=(n == 7))
                i.then_inc(var_ready.sem, 1)
                pe.wait_ge(qc_ready.sem, qc_ready.at(b, 8))
                for j in range(LT):
                    n = P if j < LT - 1 else MAIN - 3 * P
                    for k in range(KC):
                        pe.matmul(ps[0:n, j, :], ctx[:, k, j * P:j * P + n], Wv[:, k, :], start=(k == 0), stop=(k == KC - 1))
                for k in range(KC):
                    i = pe.matmul(ps[96:128, 5, :], ctx[:, k, L - 32:L], Wvd[:, k, :], start=(k == 0), stop=(k == KC - 1))
                i.then_inc(v_ready.sem, 1)
                pe.wait_ge(v_ready.sem, v_ready.at(b, 1))
                pe.sem_inc(ctx_free.sem, 1)
                pe.wait_ge(rrow_ready.sem, rrow_ready.at(b, 1))
                for i8 in range(8):
                    if i8 >= 2:
                        pe.wait_ge(rb_used.sem, rb_used.at(b, i8 - 1))
                    pe.matmul(ps[:, 6 + i8 % 2, :], headrow[:, i8, :], rrow_parts[:, 0, :], start=True, stop=False)
                    pe.matmul(ps[:, 6 + i8 % 2, :], headrow[:, i8, :], rrow_parts[:, 1, :], start=False, stop=True)\
                        .then_inc(rb_ready.sem, 1)
                pe.wait_ge(v_sb.sem, v_sb.at(b, 1))

                def scores(it):
                    qp, h = divmod(it, H)
                    rows, tile = slice(HD * (h % HPT), HD * (h % HPT + 1)), h // HPT
                    pe.wait_ge(qk_final.sem, qk_final.at(b, KT + tile + 1))
                    if it >= 2:
                        pe.wait_ge(p_raw.sem, p_raw.at(b, it - 1))
                    for q in range(2):
                        t = 2 * qp + q
                        i = pe.matmul(ps[:, 2 * (it % 2) + q, :], qk[rows, tile, t * P:(t + 1) * P], qk[rows, KT + tile, :],
                                      start=True, stop=True)
                    i.then_inc(s_ready.sem, 1)

                def turn(it):
                    pe.wait_ge(p_final.sem, p_final.at(b, it + 1))
                    pe.wait_ge(p_final1.sem, p_final1.at(b, it + 1))
                    if it >= 1:
                        pe.wait_ge(pt_d.sem, pt_d.at(b, it))
                        pe.wait_ge(pt_a.sem, pt_a.at(b, it))
                    for q in range(2):
                        for j in range(LT):
                            i = pe.transpose(ps[:, 4 + q, j * P:(j + 1) * P], Pr[:, it % 2, q, j * P:(j + 1) * P], ident[:, :])
                    i.then_inc(t_ready.sem, 1)

                def weigh(it):
                    qp, h = divmod(it, H)
                    pe.wait_ge(pt_d.sem, pt_d.at(b, it + 1))
                    pe.wait_ge(pt_a.sem, pt_a.at(b, it + 1))
                    if it == H:
                        pe.wait_ge(cT_sb.sem, cT_sb.at(b, 2))
                    rows, tile = slice(HD * (h % HPT), HD * (h % HPT + 1)), h // HPT
                    for j in range(LT):
                        i = pe.matmul(ps[rows, 6 + tile // 2, (tile % 2) * 2 * P:(tile % 2 + 1) * 2 * P],
                                      Vn[:, j, h * HD:(h + 1) * HD], PT[:, it % 2, :, j * P:(j + 1) * P],
                                      start=(j == 0), stop=(j == LT - 1))
                    i.then_inc(pv_done.sem, 1)

                scores(0)
                scores(1)
                for it in range(NIT):
                    if it + 2 < NIT:
                        scores(it + 2)
                    turn(it)
                    if it >= 1:
                        weigh(it - 1)
                weigh(NIT - 1)
                for t in range(LT):
                    pe.wait_ge(cT_sb.sem, cT_sb.at(b, 2 * (t // 2 + 1)))
                    for k in range(KT):
                        pe.matmul(ps[:, 4 + t, :], ctxnT[:, k, t * P:(t + 1) * P], Wo[:, k, :], start=(k == 0), stop=False)
                    pe.matmul(ps[:, 4 + t, :], ones1[:, :], bo[:, :], start=False, stop=True).then_inc(o_ready.sem, 1)

            pe.wait_ge(batch_done.sem, B + 1)

            def turn_h(b, u):
                for t in range(LT):
                    pe.wait_ge(hn_ready.sem, hn_ready.at(b, t + 1))
                    if b * LT + t >= 7:
                        pe.wait_ge(hT_sb.sem, hT_sb.at(b, t - 6))
                    for k in range(KT):
                        i = pe.transpose(ps[:, (b * LT + t) % 7, k * P:(k + 1) * P], hn[u][:, t, k * P:(k + 1) * P], ident[:, :])
                    i.then_inc(hT_ready.sem, 1)

            def route(b):
                pe.wait_ge(hT_sb.sem, hT_sb.at(b + 1, 0))
                for t in range(b * LT, (b + 1) * LT):
                    for k in range(KT):
                        i = pe.matmul(ps[:, 7, t * NE:(t + 1) * NE], HT[:, k, t * P:(t + 1) * P], Wg[:, k, :],
                                      start=(k == 0), stop=(k == KT - 1))
                return i

            for b in range(B):
                turn_h(b, b % 2)
                if b >= 1:
                    route(b - 1)
            route(B - 1).then_inc(logits_ready, 1)

            def shared_up(c, ms=(0, 1, 2)):
                for m in ms:
                    if isinstance(c, int) and c == 1:
                        pe.wait_ge(aS_ready.sem, aS_ready.at(0, m + 1))
                    for half in range(2):
                        for k in range(KT):
                            i = pe.matmul(ps[:, 2 * m + half, :], Wsh[:, k, half * FS + m * P:half * FS + (m + 1) * P],
                                          HT[:, k, bass.ds(c * L, L)], start=(k == 0), stop=(k == KT - 1))
                    i.then_inc(shg_ready.sem, 1)

            def shared_down(c):
                for t in range(LT):
                    if not isinstance(c, int) or c > 0 or t >= 2:
                        pe.wait_ge(shx_done.sem, shx_done.at(c, t - 1))
                    for m in range(3):
                        if t == 0:
                            pe.wait_ge(aS_ready.sem, aS_ready.at(c, m + 1))
                        i = pe.matmul(ps[:, 6 + t % 2, :], aS[:, m, t * P:(t + 1) * P], Wsd[:, m, :], start=(m == 0),
                                      stop=(m == 2))
                    i.then_inc(shy_ready.sem, 1)

            pe.wait_ge(sh_loaded, 32)
            shared_up(0, (0, 1))
            pe.wait_ge(mask_ready, 1)
            pe.matmul(ps[:, 6, :], tri[:, :], Mb[:, :], start=True, stop=True)
            pe.matmul(ps[:, 7, :], onesb[:, :], Mb[:, :], start=True, stop=True).then_inc(prefix_ready, 1)
            shared_up(0, (2,))
            shared_up(1)
            pe.wait_ge(slots_ready, 1)
            shared_down(0)
            shared_down(1)
            with pe.Fori(2, B) as c:
                shared_up(c)
                shared_down(c)
            pe.wait_ge(shx_done.sem, shx_done.at(B, 0))

            def turn_tokens(s, r, u):
                if isinstance(s, int) and s >= NBLK:
                    return
                pe.wait_ge(gathered[u], 32 * (r + 1))
                ge(pe, gt_lo, s)
                for k in range(KT):
                    for q in range(2):
                        i = pe.transpose(ps[:, k // 2, (k % 2) * BLK + q * P:(k % 2) * BLK + (q + 1) * P],
                                         G[:, u, q, k * P:(k + 1) * P], ident[:, :])
                i.then_inc(gt_ready, 1)

            def product(out, a, w, first, last):
                for i, (pa, pw) in enumerate(((0, 0), (0, 1), (1, 0))):
                    ins = pe.matmul(out, a(pa), w(pw), start=(first and i == 0), stop=(last and i == 2))
                return ins

            def up(s, r, u):
                pe.wait_ge(gt_lo, s + 1)
                pe.wait_ge(wgu_lo, s + 1)
                for q in range(2):
                    ge(pe, act_done, 2 * (s - 1) + q + 1)
                    for k in range(KT):
                        i = product(ps[:, 2 + q, 0:2 * FE], lambda h: GTp[:, 0, h, k, q * P:(q + 1) * P],
                                    lambda h: wgup[:, u, h, k], k == 0, k == KT - 1)
                    i.then_inc(gu_ready, 1)

            def turn_act(s, r, u):
                if isinstance(s, int) and s < 0:
                    return
                pe.wait_ge(act_done, 2 * (s + 1))
                ge(pe, at_lo, s)
                for f in range(2):
                    for q in range(2):
                        i = pe.transpose(ps[0:FH, 4, f * BLK + q * P:f * BLK + (q + 1) * P], act_m[:, q, f * FH:(f + 1) * FH],
                                         ident[:, :])
                i.then_inc(at_ready, 1)

            def down(s, r, u):
                if isinstance(s, int) and s < 0:
                    return
                pe.wait_ge(at_lo, s + 1)
                pe.wait_ge(wdn_lo, s + 1)
                ge(pe, y_a, s)
                ge(pe, y_d, s)
                for q in range(2):
                    for f in range(2):
                        i = product(ps[:, 5 + q, :], lambda h: aTp[:, 0, h, f, q * P:(q + 1) * P],
                                    lambda h: wdnp[:, u, h, f], f == 0, f == 1)
                    i.then_inc(y_ready, 1)

            def block_pe(s, r, u):
                before = (s - 1, r - 1 if u == 0 else r, 1 - u)
                turn_act(*before)
                up(s, r, u)
                turn_tokens(s + 1, r if u == 0 else r + 1, 1 - u)
                down(*before)

            turn_tokens(0, 0, 0)
            steps(pe, block_pe, 0, NBLK - 1)
            last = (NBLK - 1, (NBLK - 1) // 2, (NBLK - 1) % 2)
            turn_act(*last)
            down(*last)

        @block.vector
        def _(dve):
            order = Order(dve, dve_order, DVE_STEPS)
            o = order
            dve.memset(headmean[:, :], 0.0)
            o.mark(dve.memset(headvar[:, :, :], 0.0))
            o.wait()
            dve.wait_ge(setup_iota, 2)
            dve.tensor_copy(iota_f[:, :], iota_i[:, :])
            dve.tensor_copy(blk_f[:, :], blk_i[:, :])
            dve.tensor_copy(tri[:, :], tri_f[:, :])
            flat_var = headvar[:, :, :].rearrange("p i c -> p (i c)")
            for j in range(HPT):
                rows = slice(HD * j, HD * (j + 1))
                dve.memset(headmean[rows, rows], 1.0 / HD)
                i = dve.memset(flat_var[rows, j:j + 36 * 7 + 1:36], 1.0 / HD)
            i.then_inc(setup_dve, 1)
            dve.wait_ge(vecs_loaded, 16)
            dve.wait_ge(ffn_loaded, 32)
            w, r, lt, acc = wtmp
            a = o.mark(dve.tensor_scalar(lt, w, -TH_W, None, ALU.is_lt))
            o.wait(a)
            o.mark(dve.scalar_tensor_tensor(out=acc, in0=w, scalar=TH_W, in1=lt, op0=ALU.is_gt, op1=ALU.subtract))
            o.wait()
            o.mark(dve.scalar_tensor_tensor(out=acc, in0=acc, scalar=SC_W, in1=r, op0=ALU.mult, op1=ALU.add))
            o.wait()
            o.mark(dve.tensor_scalar(acc, acc, -SC_X, None, ALU.mult))
            for part in range(3):
                o.wait()
                o.mark(dve.tensor_copy(W3[:, part], acc))
                if part < 2:
                    o.wait()
                    o.mark(dve.tensor_tensor(acc, acc, W3[:, part], ALU.subtract))
            dve.wait_ge(wqk_loaded, 48)
            for W, kt, at in centred:
                o.mark(dve.tensor_reduce(wsum[:, at:at + kt * H], by_head(W), AX.X, ALU.add))
                o.wait()
                dve.tensor_scalar(wsum[:, at:at + kt * H], wsum[:, at:at + kt * H], 1.0 / HD, None, ALU.mult)\
                    .then_inc(means_ready, 1)
            dve.wait_ge(setup_pe, 1)
            dve.tensor_tensor(qkbias[:, :], vec("bq", 0, 3 * KT), ps[:, 7, 0:3 * KT], ALU.subtract)
            dve.tensor_tensor(bvsum[:, :], vec("bv", 0, KT), vec("bvd", 0, KT), ALU.add)
            dve.tensor_scalar(aff[:, 0:2], vec("qw", 0, 2), QK_SCALE, None, ALU.mult)
            dve.tensor_copy(aff[:, 2:6], vec("kw", 0, 4))
            dve.wait_ge(setup_act, 1)
            o.mark(dve.tensor_scalar(negA[:, :], negA[:, :], -1.0, None, ALU.mult))
            o.wait()
            dve.tensor_copy(std[:, 0:1], V_[:, 0:1]).then_inc(batch_done.sem, 1)

            def settle():
                dve.sem_inc(dve_passed, 1)

            def ln_stats(b, k):
                settle()
                for t in range(LT):
                    i = dve.bn_stats(st6[:, t, :], X[:, b * LT + t, :])
                o.mark(i)
                ln_means(b)

            def ln_means(b):
                o.wait()
                settle()
                for t in range(LT):
                    i = dve.bn_aggr(mv[:, t, :], st6[:, t, :])
                i.then_inc(ln_mv.sem, 1)

            def ln_coefs(b, k):
                dve.wait_ge(ln_std.sem, ln_std.at(b, k + 1))
                o.mark(dve.reciprocal(rstd[:, :], std[:, :]))
                o.wait()
                dve.scalar_tensor_tensor(out=nmr[:, :], in0=mv[:, :, 0], scalar=-1.0, in1=rstd[:, :], op0=ALU.mult,
                                         op1=ALU.mult).then_inc(ln_coef.sem, 1)

            with dve.Fori(0, B) as b:
                o.enter(b)
                dve.wait_ge(batch_done.sem, batch_done.at(b, 0))
                pad = o.mark(dve.memset(xpad[:, :, 0:3], 0.0))
                o.wait(pad)
                marks = []
                for tap, e in [(tap, e) for pair in (0, 2) for tap in (3, 2, 1, 0) for e in (pair, pair + 1)]:
                    wk = vec("conv_w", e * TAPS + tap)
                    if tap == 3:
                        dve.wait_ge(xpad_ready.sem, xpad_ready.at(b, e + 1))
                        i = dve.tensor_scalar(conv[:, e], xpad[:, e, tap:tap + L], wk, None, ALU.mult)
                    else:
                        o.wait(marks[-2])
                        i = dve.scalar_tensor_tensor(out=conv[:, e], in0=xpad[:, e, tap:tap + L], scalar=wk,
                                                     in1=conv[:, e], op0=ALU.mult, op1=ALU.add)
                    if tap:
                        marks.append(o.mark(i))
                    else:
                        i.then_inc(conv_ready.sem, 1)
                        marks.append(marks[-1])
                dve.wait_ge(loaded, 16 * len(loads))
                ln_stats(b, 0)
                dve.wait_ge(xd_ready.sem, xd_ready.at(b, 1))
                dve.tensor_copy(XD[:, :], ps[0:DR + 2 * DS, 4, :]).then_inc(xd_sb.sem, 1)
                xd_hi = o.mark(dve.tensor_copy(XDr[:, 0, :], ps[0:DR + 2 * DS, 4, :]))
                o.wait(xd_hi)
                dve.tensor_tensor(XDr[:, 1, :], ps[0:DR + 2 * DS, 4, :], XDr[:, 0, :], ALU.subtract)\
                    .then_inc(xdr_ready.sem, 1)
                dve.wait_ge(conv_ready.sem, conv_ready.at(b, KT))
                for s in range(2):
                    i = dve.memset(dA[s][:, :, 0:1], 0.0)
                zero = o.mark(i)
                for e in range(KT):
                    dve.wait_ge(sp_abs_ready.sem, sp_abs_ready.at(b, e + 1))
                    i = dve.tensor_scalar(sp_relu[:, e], ps[:, e, :], vec("dt_b", e), 0.0, ALU.add, ALU.max)
                o.mark(i)
                o.wait()
                dve.wait_ge(sp_ready.sem, sp_ready.at(b, 1))
                dve.tensor_tensor(delta, sp_relu, sp_ln, ALU.add).then_inc(delta_ready.sem, 1)
                dve.wait_ge(delta_ready.sem, delta_ready.at(b, 1))
                o.mark(dve.tensor_tensor(du, delta, U, ALU.mult))
                o.wait()

                def flat(t):
                    return t.rearrange("p e l -> p (e l)")

                def inputs(n):
                    dve.wait_ge(b_ready.sem, b_ready.at(b, n + 1))
                    if n >= 2:
                        dve.wait_ge(scan_done.sem, scan_done.at(b, n - 1))
                    dve.tensor_tensor(dBu[n % 2], du, ps[:, 4 + n % 2, :].unsqueeze(1).to_broadcast([P, KT, L]),
                                      ALU.mult).then_inc(b_used.sem, 1)

                def scan(n):
                    dve.wait_ge(dA_ready.sem, dA_ready.at(b, n + 1))
                    dve.wait_ge(b_used.sem, b_used.at(b, n + 1))
                    if n >= 3:
                        dve.wait_ge(hc_used.sem, hc_used.at(b, n - 2))
                    dve.tensor_tensor_scan(flat(hs[n % 3]), flat(dA[n % 2]), flat(dBu[n % 2]), 0.0, ALU.mult,
                                           ALU.add).then_inc(scan_done.sem, 1)

                inputs(0)
                for n in range(DS):
                    if n + 1 < DS:
                        inputs(n + 1)
                    scan(n)
                    if n in ENDS:
                        dve.wait_ge(c_sb.sem, c_sb.at(b, n + 1))
                        dve.wait_ge(scan_done.sem, scan_done.at(b, n + 1))
                        dve.tensor_tensor(hs[n % 3][:, 0:HALF], hs[n % 3][:, 0:HALF],
                                          Cr[:, n % 2, :].unsqueeze(1).to_broadcast([P, HALF, L]), ALU.mult)\
                            .then_inc(hc_half.sem, 1)
                ln_coefs(b, 0)
                dve.wait_ge(hc_used.sem, hc_used.at(b, DS))
                dve.wait_ge(siluz_ready.sem, siluz_ready.at(b, LT))
                for e in range(KT):
                    m = o.mark(dve.scalar_tensor_tensor(out=yt[:, e], in0=U[:, e], scalar=vec("D", e), in1=ps[:, e, :],
                                                        op0=ALU.mult, op1=ALU.add))
                    if e:
                        o.wait(m - 1)
                        dve.tensor_tensor(yz[:, e - 1], yt[:, e - 1], siluz[:, e - 1], ALU.mult).then_inc(yz_ready.sem, 1)
                o.wait(m)
                dve.tensor_tensor(yz[:, KT - 1], yt[:, KT - 1], siluz[:, KT - 1], ALU.mult).then_inc(yz_ready.sem, 1)

                def add(bank, gate):
                    return o.mark(dve.scalar_tensor_tensor(
                        out=X[:, b * LT + bank - 4, :], in0=ps[:, bank, :], scalar=tg[:, gate:gate + 1],
                        in1=X[:, b * LT + bank - 4, :], op0=ALU.mult, op1=ALU.add))

                dve.wait_ge(yt_ready.sem, yt_ready.at(b, 1))
                for l in range(LT):
                    add(4 + l, 0)
                o.wait()
                ln_stats(b, 1)
                ln_coefs(b, 1)
                dve.wait_ge(ln_coef.sem, ln_coef.at(b, 2))
                norms, greater = {}, {}
                for step in range(LT + 2):
                    if step < LT:
                        norms[step] = o.mark(dve.tensor_scalar(xn[:, step], X[:, b * LT + step, :], mv[:, step, 0:1],
                                                               rstd[:, step:step + 1], ALU.subtract, ALU.mult))
                    if 0 <= step - 1 < LT:
                        o.wait(norms[step - 1])
                        greater[step - 1] = o.mark(dve.tensor_scalar(gt[:, step - 1], xn[:, step - 1], TH_X, None, ALU.is_gt))
                    if 0 <= step - 2 < LT:
                        o.wait(greater[step - 2])
                        dve.scalar_tensor_tensor(out=tern[:, step - 2], in0=xn[:, step - 2], scalar=-TH_X,
                                                 in1=gt[:, step - 2], op0=ALU.is_lt, op1=ALU.subtract)\
                            .then_inc(tern_ready.sem, 1)
                for t in range(LT):
                    dve.wait_ge(ffn_ready.sem, ffn_ready.at(b, t + 1))
                    add(4 + t, 1)
                    o.wait()
                    settle()
                    i = dve.bn_stats(st6[:, t, :], X[:, b * LT + t, :])
                o.mark(i)
                ln_means(b)
                ln_coefs(b, 2)
                for t in range(LT):
                    dve.wait_ge(xT_ready.sem, xT_ready.at(b, t + 1))
                    dve.tensor_copy(xnT[:, :, t * P:(t + 1) * P], ps[:, 4 + t, :].rearrange("p (k l) -> p k l", k=KT))\
                        .then_inc(xT_sb.sem, 1)
                for n, i8 in enumerate(K_THEN_Q):
                    dve.wait_ge(qc_ready.sem, qc_ready.at(b, n + 1))
                    dve.tensor_tensor(sq[:, i8], qk[:, i8], qk[:, i8], ALU.mult).then_inc(sq_ready.sem, 1)
                dve.wait_ge(std_ready.sem, std_ready.at(b, 1))
                o.mark(dve.reciprocal(rrow[:, :], sdr[:, :]))
                o.wait()
                o.mark(dve.tensor_copy(rrow_parts[:, 0, :], rrow[:, :]))
                o.wait()
                dve.tensor_tensor(rrow_parts[:, 1, :], rrow[:, :], rrow_parts[:, 0, :], ALU.subtract)\
                    .then_inc(rrow_ready.sem, 1)
                for i8 in range(8):
                    dve.wait_ge(rb_ready.sem, rb_ready.at(b, i8 + 1))
                    bank = 6 + i8 % 2
                    if i8 < KT:
                        dve.scalar_tensor_tensor(out=qk[:, i8], in0=qk[:, i8], scalar=aff[:, 0:1], in1=ps[:, bank, :],
                                                 op0=ALU.mult, op1=ALU.mult).then_inc(rb_used.sem, 1)
                    else:
                        dve.scalar_tensor_tensor(out=qk[:, i8, 0:MAIN], in0=qk[:, i8, 0:MAIN], scalar=aff[:, 2:3],
                                                 in1=ps[:, bank, 0:MAIN], op0=ALU.mult, op1=ALU.mult)
                        dve.scalar_tensor_tensor(out=qk[:, i8, MAIN:L], in0=qk[:, i8, MAIN:L], scalar=aff[:, 4:5],
                                                 in1=ps[:, bank, MAIN:L], op0=ALU.mult, op1=ALU.mult)\
                            .then_inc(rb_used.sem, 1)

                def maxima(it):
                    s = it % 2
                    dve.wait_ge(s_ready.sem, s_ready.at(b, it + 1))
                    if it >= 2:
                        dve.wait_ge(p_raw.sem, p_raw.at(b, it - 1))
                    dve.tensor_reduce(nm[:, s, 0:2], ps[:, 2 * s:2 * s + 2, 0:MAIN], AX.X, ALU.max, negate=True)
                    dve.tensor_reduce(nm[:, s, 2:4], ps[:, 2 * s:2 * s + 2, MAIN:L], AX.X, ALU.max, negate=True)\
                        .then_inc(nm_ready.sem, 1)

                def over_sums(it):
                    dve.wait_ge(p_raw.sem, p_raw.at(b, it + 1))
                    dve.reciprocal(escale[:, it % 2, :], esum[:, it % 2, :]).then_inc(scale_ready.sem, 1)

                def normalise(it):
                    s = it % 2
                    dve.wait_ge(scale_ready.sem, scale_ready.at(b, it + 1))
                    dve.tensor_scalar(Pr[:, s, 0, 0:MAIN], Pr[:, s, 0, 0:MAIN], escale[:, s, 0:1], None, ALU.mult)
                    dve.tensor_tensor(Pr[:, s, :, MAIN:L], Pr[:, s, :, MAIN:L],
                                      escale[:, s, 2:4].unsqueeze(2).to_broadcast([P, 2, DCA]), ALU.mult)\
                        .then_inc(p_final.sem, 1)

                def heads_out(qp):
                    dve.wait_ge(pv_done.sem, pv_done.at(b, (qp + 1) * H))
                    for half in range(2):
                        dve.tensor_tensor(ctxnT[:, 2 * half:2 * half + 2, qp * 2 * P:(qp + 1) * 2 * P],
                                          ps[:, 6 + half, :].rearrange("p (k l) -> p k l", k=2),
                                          bvsum[:, 2 * half:2 * half + 2].unsqueeze(2).to_broadcast([P, 2, 2 * P]),
                                          ALU.add).then_inc(cT_sb.sem, 1)

                maxima(0)
                maxima(1)
                over_sums(0)
                normalise(0)
                for it in range(NIT):
                    if it + 2 < NIT:
                        maxima(it + 2)
                    if it + 1 < NIT:
                        over_sums(it + 1)
                    dve.wait_ge(t_ready.sem, t_ready.at(b, it + 1))
                    if it >= 2:
                        dve.wait_ge(pv_done.sem, pv_done.at(b, it - 1))
                    dve.tensor_copy(PT[:, it % 2, 0], ps[:, 4, :]).then_inc(pt_d.sem, 1)
                    if it + 1 < NIT:
                        normalise(it + 1)
                    if it == H:
                        heads_out(0)
                heads_out(1)
                for t in range(LT):
                    dve.wait_ge(o_ready.sem, o_ready.at(b, t + 1))
                    add(4 + t, 2)
                o.wait()
                settle()
                for t in range(LT):
                    i = dve.bn_stats(st6[:, t, :], X[:, b * LT + t, :])
                o.mark(i)
                o.wait()
                settle()
                for t in range(LT):
                    i = dve.bn_aggr(mv[:, t, :], st6[:, t, :])
                o.mark(i)
                o.wait()
                dve.tensor_copy(mv4[:, bass.ds(b * LT, LT), :], mv[:, :, :]).then_inc(batch_done.sem, 1)
            o.leave()

            dve.wait_ge(batch_done.sem, B + 1)
            dve.memset(zero_rows, 0.0).then_inc(zero_ready, 1)
            dve.wait_ge(ln4_std, 1)
            dve.reciprocal(rstd4[:, :], std4[:, :]).then_inc(prep_order, 1)
            dve.wait_ge(prep_order, 1)
            dve.scalar_tensor_tensor(out=nmr4[:, :], in0=mv4[:, :, 0], scalar=-1.0, in1=rstd4[:, :], op0=ALU.mult,
                                     op1=ALU.mult).then_inc(ln4_coef, 1)
            for t in range(NT):
                dve.wait_ge(hT_ready.sem, hT_ready.at(0, t + 1))
                dve.tensor_copy(HT[:, :, t * P:(t + 1) * P], ps[:, t % 7, :].rearrange("p (k l) -> p k l", k=KT))\
                    .then_inc(hT_sb.sem, 1)

            def chain(ins):
                o.mark(ins)
                o.wait()

            def shared_products(c, ms=(0, 1, 2)):
                for m in ms:
                    dve.wait_ge(sil_ready.sem, sil_ready.at(c, m + 1))
                    dve.tensor_tensor(aS[:, m], sil[:, m], ps[:, 2 * m + 1, :], ALU.mult).then_inc(aS_ready.sem, 1)

            def shared_sums(c):
                for t in range(LT):
                    dve.wait_ge(shy_ready.sem, shy_ready.at(c, t + 1))
                    dve.scalar_tensor_tensor(out=X[:, c * LT + t, :], in0=ps[:, 6 + t % 2, :], scalar=tg[:, 3:4],
                                             in1=X[:, c * LT + t, :], op0=ALU.mult, op1=ALU.add).then_inc(shx_done.sem, 1)

            dve.wait_ge(sc_ready, 1)
            for t in range(NT):
                i = dve.max(top[:, t, :], SC[:, t, :])
            chain(i)
            for t in range(NT):
                i = dve.max_index(topi[:, t, :], top[:, t, :], SC[:, t, :])
            chain(i)
            o.mark(dve.tensor_reduce(den[:, :], top[:, :, 0:TOPK], AX.X, ALU.add))
            chain(dve.tensor_copy(topf[:, :, :], topi[:, :, :]))
            chain(dve.tensor_scalar(den[:, :], den[:, :], 1e-20, None, ALU.add))
            chain(dve.reciprocal(den[:, :], den[:, :]))
            chain(dve.tensor_scalar(den[:, :], den[:, :], tg[:, 3:4], None, ALU.mult))
            dve.tensor_tensor(pairs[:, :, :, 1].bitcast(F32), top[:, :, 0:TOPK],
                              den[:, :].unsqueeze(2).to_broadcast([P, NT, TOPK]), ALU.mult)
            dve.tensor_copy(pairs[:, :, :, 0], tok_i[:, :].unsqueeze(2).to_broadcast([P, NT, TOPK]))
            for j in range(TOPK):
                i = dve.tensor_tensor(pick[:, j], iota_f[:, :].unsqueeze(1).to_broadcast([P, NT, NE]),
                                      topf[:, :, j:j + 1].to_broadcast([P, NT, NE]), ALU.is_equal)
            chain(i)
            for j in range(TOPK // 2):
                i = dve.tensor_tensor(pair_sums[j], pick[:, 2 * j], pick[:, 2 * j + 1], ALU.add)
            chain(i)
            chain(dve.tensor_tensor(msum, pair_sums[0], pair_sums[1], ALU.add))
            chain(dve.tensor_tensor(msum, msum, pair_sums[2], ALU.add))
            dve.tensor_copy(Mb[:, :], msum.rearrange("p t e -> p (t e)")).then_inc(mask_ready, 1)
            dve.wait_ge(h_stored[1].sem, h_stored[1].at(B // 2, 0))
            shared_products(0, (0,))
            dve.wait_ge(prefix_ready, 1)
            chain(dve.tensor_copy(tot, ps[:, 7, :].rearrange("p (t e) -> p e t", e=NE)))
            chain(dve.tensor_tensor_scan(cum.rearrange("p e t -> p (e t)"), keep[:, :, :].rearrange("p e t -> p (e t)"),
                                         tot.rearrange("p e t -> p (e t)"), 0.0, ALU.mult, ALU.add))
            o.mark(dve.tensor_scalar(nb_i[:, :], cum[:, :, NT - 1], float(BLK - 1), None, ALU.add))
            chain(dve.tensor_tensor(tot, cum, tot, ALU.subtract))
            chain(dve.tensor_scalar(nb_i[:, :], nb_i[:, :], BLK.bit_length() - 1, None, ALU.logical_shift_right))
            chain(dve.tensor_copy(nb_f[:, :], nb_i[:, :]))
            chain(dve.tensor_tensor_scan(end_b[:, :], ones_e[:, :], nb_f[:, :], 0.0, ALU.mult, ALU.add))
            chain(dve.tensor_tensor(start_b[:, :], end_b[:, :], nb_f[:, :], ALU.subtract))
            chain(dve.tensor_scalar(start_b[:, :], start_b[:, :], float(BLK), None, ALU.mult))
            chain(dve.tensor_tensor(slot, ps[:, 6, :].rearrange("p (t e) -> p t e", e=NE), tot.rearrange("p e t -> p t e"),
                                    ALU.add))
            chain(dve.tensor_tensor(slot, slot, start_b[:, :].unsqueeze(1).to_broadcast([P, NT, NE]), ALU.add))
            for j in range(TOPK):
                i = dve.tensor_tensor(pick[:, j], pick[:, j], slot, ALU.mult)
            chain(i)
            for j in range(TOPK):
                i = dve.tensor_reduce(slots_f[:, j, :], pick[:, j], AX.X, ALU.add)
            chain(i)
            chain(dve.tensor_copy(slots, slots_f))
            o.mark(dve.tensor_scalar(slot_p, slots, P - 1, None, ALU.bitwise_and))
            chain(dve.tensor_scalar(slots, slots, P.bit_length() - 1, None, ALU.logical_shift_right))
            dve.scalar_tensor_tensor(out=slots, in0=slot_p, scalar=float(NSLOT // P), in1=slots, op0=ALU.mult, op1=ALU.add)\
                .then_inc(slots_ready, 1)
            shared_products(0, (1, 2))
            chain(dve.tensor_tensor(le[:, :, :], end_b[0:1, :].unsqueeze(1).to_broadcast([1, NBLK, NE]),
                                    blk_f[:, :].unsqueeze(2).to_broadcast([1, NBLK, NE]), ALU.is_le))
            chain(dve.tensor_reduce(expert_f[:, :], le[:, :, :], AX.X, ALU.add))
            dve.tensor_scalar(expert_i[:, :], expert_f[:, :], float(NE - 1), None, ALU.min).then_inc(expert_ready, 1)

            shared_sums(0)
            with dve.Fori(1, B) as c:
                shared_products(c)
                shared_sums(c)
            dve.wait_ge(meta_loaded, 16)

            def turned(s):
                if isinstance(s, int) and s >= NBLK:
                    return
                dve.wait_ge(gt_hi, s + 1)
                ge(dve, gu_ready, 2 * s)
                dve.tensor_tensor(GTp[:, 0, 1], ps[:, 0:2, :].rearrange("p a (k l) -> p (a k) l", k=2), GTp[:, 0, 0], ALU.subtract)\
                    .then_inc(gt_lo, 1)

            def split_up(s, u):
                if isinstance(s, int) and s >= NBLK:
                    return
                dve.wait_ge(wgu_hi, s + 1)
                ge(dve, gu_ready, 2 * (s - 1))
                dve.tensor_tensor(wgup[:, u, 1], wgu[:, u], wgup[:, u, 0], ALU.subtract).then_inc(wgu_lo, 1)

            def turned_act(s):
                dve.wait_ge(at_hi, s + 1)
                ge(dve, y_ready, 2 * s)
                dve.tensor_tensor(aTp[:, 0, 1], ps[0:FH, 4, :].rearrange("p (f l) -> p f l", f=2), aTp[:, 0, 0], ALU.subtract)\
                    .then_inc(at_lo, 1)

            def block_dve(s, r, u):
                if not isinstance(s, int) or s >= 1:
                    turned_act(s - 1)
                split_up(s + 1, 1 - u)
                for q in range(2):
                    dve.wait_ge(silu_done, 2 * s + q + 1)
                    ge(dve, at_ready, s)
                    dve.tensor_tensor(act_m[:, q, :], act_s[:, q, :], ps[:, 2 + q, FE:2 * FE], ALU.mult)\
                        .then_inc(act_done, 1)
                    if q == 0:
                        dve.wait_ge(wdn_hi, s + 1)
                        ge(dve, y_ready, 2 * (s - 1))
                        dve.tensor_tensor(wdnp[:, u, 1], wdn[0:FH, u], wdnp[:, u, 0], ALU.subtract).then_inc(wdn_lo, 1)
                turned(s + 1)
                scaled(s - 1, 1 - u)

            def scaled(s, u):
                if isinstance(s, int) and s < 0:
                    return
                dve.wait_ge(y_ready, 2 * s + 1)
                ge(dve, added, 32 * (s - 1))
                dve.tensor_scalar(Yb[:, u, 0], ps[:, 5, :], meta[:, bass.ds(2 * s, 1), 1].bitcast(F32), None, ALU.mult)\
                    .then_inc(y_d, 1)

            split_up(0, 0)
            turned(0)
            steps(dve, block_dve, 0, NBLK - 1)
            turned_act(NBLK - 1)
            scaled(NBLK - 1, (NBLK - 1) % 2)


_INS = ["x", "ctxT", "vecs", "w_in", "w_xp", "w_dt", "ffn_w", "ffn_r", "w_q", "w_k", "w_v", "w_kd", "w_vd", "w_o", "b_o", "w_g",
        "w_sh", "w_sd", "w_gu", "w_dn"]
_OUTS = [((B * L + BLK, DM), "float32")]


def _by_row(w, p=P):
    k = w.shape[0] // p
    return w.reshape(k, p, -1).transpose(1, 0, 2)


def lay_out(a):
    g = {}
    g["x"] = a["x"].reshape(B * L, DM)
    g["ctxT"] = a["ctx_1024"].transpose(0, 2, 1).reshape(B, KC, P, L).transpose(0, 2, 1, 3)
    g["w_in"] = _by_row(a["L0_xattn_in_proj_w"].T)
    g["w_xp"] = _by_row(a["L0_xattn_x_proj_w"].T)
    g["w_dt"] = a["L0_xattn_dt_proj_w"].T
    g["ffn_w"] = _by_row(a["L0_ffn_weight"].T)
    g["ffn_r"] = _by_row(a["L0_ffn_rram_variation"].T)
    g["w_q"] = _by_row(a["L1_xattn_Wq"])
    kv = np.concatenate([a["L1_xattn_Wk"], a["L1_xattn_Wv"]], 1).reshape(DC, H, 2, HD)
    bkv = np.concatenate([a["L1_xattn_bk"], a["L1_xattn_bv"]]).reshape(H, 2, HD)
    g["w_k"] = _by_row(kv[:, :, 0].reshape(DC, DM))
    g["w_v"] = _by_row(kv[:, :, 1].reshape(DC, DM))
    g["w_kd"] = _by_row(a["L1_xattn_Wkv_dca"][:, :DM])
    g["w_vd"] = _by_row(a["L1_xattn_Wkv_dca"][:, DM:])
    g["w_o"] = _by_row(a["L1_xattn_Wo"])
    g["b_o"] = a["L1_xattn_bo"].reshape(1, DM)
    g["w_g"] = _by_row(a["L1_ffn_gate_w"])
    g["w_sh"] = _by_row(np.concatenate([a["L1_ffn_sg"], a["L1_ffn_su"]], 1))
    g["w_sd"] = _by_row(a["L1_ffn_sd"])
    gu = np.concatenate([a["L1_ffn_wg"], a["L1_ffn_wu"]], 2)
    g["w_gu"] = gu.reshape(NE, KT, P, 2 * FE).transpose(0, 2, 1, 3)
    g["w_dn"] = a["L1_ffn_wd"].reshape(NE, 2, FH, DM).transpose(0, 2, 1, 3)
    vecs = np.empty((P, NVEC), np.float32)

    def put(name, v):
        vecs[:, VEC[name][0]:VEC[name][1]] = v

    put("conv_w", _by_row(a["L0_xattn_conv_w"]).reshape(P, -1))
    put("conv_b", a["L0_xattn_conv_b"].reshape(KT, P).T)
    put("dt_b", a["L0_xattn_dt_proj_b"].reshape(KT, P).T)
    put("A_log", _by_row(a["L0_xattn_A_log"]).reshape(P, -1))
    put("D", a["L0_xattn_D"].reshape(KT, P).T)
    put("bq", a["L1_xattn_bq"].reshape(KT, P).T)
    put("bk", bkv[:, 0].reshape(KT, P).T)
    put("bkd", a["L1_xattn_bkv_dca"][:DM].reshape(KT, P).T)
    put("bv", bkv[:, 1].reshape(KT, P).T)
    put("bvd", a["L1_xattn_bkv_dca"][DM:].reshape(KT, P).T)
    for name, src in (("qw", "qn_w"), ("qb", "qn_b"), ("kw", "kn_w"), ("kb", "kn_b"), ("kdw", "kn_dca_w"), ("kdb", "kn_dca_b")):
        put(name, np.tile(a["L1_xattn_" + src], HPT).reshape(P, 1))
    for i, (src, j) in enumerate((("g_xattn", 0), ("g_ffn", 0), ("g_xattn", 1), ("g_ffn", 1))):
        vecs[:, VEC["gates"][0] + i] = a[src][j]
    g["vecs"] = vecs
    return g


def kernel(**inputs):
    import concourse.bacc as _bacc
    from concourse.bass_utils import run_bass_kernel_spmd as _run

    nc = _bacc.Bacc("TRN2", target_bir_lowering=False, num_devices=1)
    laid = lay_out({k: np.asarray(v) for k, v in inputs.items()})
    arrays, args = {}, []
    for name in _INS:
        a = np.ascontiguousarray(laid[name])
        arrays[f"in_{name}"] = a
        args.append(nc.dram_tensor(f"in_{name}", a.shape, mybir.dt.from_np(a.dtype), kind="ExternalInput").ap())
    for i, (shape, dtype) in enumerate(_OUTS):
        args.append(nc.dram_tensor(f"out_{i}", shape, mybir.dt.from_np(np.dtype(dtype)), kind="ExternalOutput").ap())
    program(nc, *args)
    r = _run(nc, [arrays], core_ids=[0])
    return r.results[0]["out_0"][:B * L].reshape(B, L, DM)
```
